# Optimizing a Trainium2 kernel written in Bass

```python
import numpy as np
import jax
import jax.numpy as jnp

def _softmax(x, axis=-1):
    return jax.nn.softmax(x, axis=axis)

def _gelu(x):
    return jax.nn.gelu(x, approximate=True)

def _silu(x):
    return jax.nn.silu(x)

def _sigmoid(x):
    return jax.nn.sigmoid(x)

def _layernorm(x, axis=-1, eps=1e-05):
    m = jnp.mean(x, axis=axis, keepdims=True)
    v = jnp.var(x, axis=axis, keepdims=True)
    return (x - m) / jnp.sqrt(v + eps)

def _scatter_add(tgt, idx, src, axis=0):
    return tgt.at[idx].add(src)

def _segment_sum(src, seg, n):
    return jax.ops.segment_sum(src, seg, n)
kernel_name = 'mk_hybrid_d1_jaxref_r8_733ad4'

def setup_inputs(seed: int=0):
    np.random.seed(seed)
    _w = jnp.asarray

    def _L0_attn_a_setup():
        import jax, jax.numpy as jnp
        import numpy as np
        B, S, D = (2, 1024, 128)
        NH = 4
        DH = D // NH
        DHID = 2 * DH
        CHUNK = 256
        BASE_LR_INV = float(np.log(np.expm1(0.001)))
        NS_COEFFS = ((4.0848, -6.8946, 2.927), (3.9505, -6.3029, 2.6377), (3.7418, -5.5913, 2.3037), (2.8769, -3.1427, 1.2046), (2.8366, -3.0525, 1.2012))

        def rms_norm(x, w, eps=1e-06):
            return x * jax.lax.rsqrt(jnp.mean(x * x, axis=-1, keepdims=True) + eps) * w

        def l2_normalize(x):
            return x / (jnp.linalg.norm(x, axis=-1, keepdims=True) + 1e-05)

        def silu(x):
            return x * jax.nn.sigmoid(x)

        def newton_schulz5(G):
            trans = G.shape[1] > G.shape[2]
            X = jnp.swapaxes(G, 1, 2) if trans else G
            X = X / (jnp.linalg.norm(X, axis=(1, 2), keepdims=True) + 1e-07)
            for a, b, c in NS_COEFFS:
                A = X @ jnp.swapaxes(X, 1, 2)
                Bm = b * A + c * (A @ A)
                X = a * X + Bm @ X
            return jnp.swapaxes(X, 1, 2) if trans else X
        ks = jax.random.split(jax.random.key(seed), 8)
        f32 = jnp.float32
        return {'hidden_states': jax.random.normal(ks[0], (B, S, D), f32), 'qkv_w': jax.random.normal(ks[1], (3 * D, D), f32) / np.sqrt(D), 'q_norm_w': jnp.ones((D,), f32), 'k_norm_w': jnp.ones((D,), f32), 'lr_proj_w': jax.random.normal(ks[2], (3 * NH, D), f32) / np.sqrt(D), 'lr_proj_b': jnp.zeros((3 * NH,), f32), 'w0': jax.random.normal(ks[3], (NH, DHID, DH), f32) / np.sqrt(DH), 'w1': jax.random.normal(ks[4], (NH, DH, DHID), f32) / np.sqrt(DHID), 'w2': jax.random.normal(ks[5], (NH, DHID, DH), f32) / np.sqrt(DH)}
    _L0_attn_a_in = _L0_attn_a_setup()

    def _L0_attn_b_setup():
        import jax, jax.numpy as jnp
        import numpy as np
        N_HEADS = 16

        def _rope_cos_sin(hs, T, dtype):
            t = jnp.arange(1, T + 1, dtype=dtype)[:, None]
            i = jnp.arange(hs // 2, dtype=dtype)
            theta = (1.0 / 10000.0) ** (2.0 * i / hs)
            ang = t * theta
            return (jnp.cos(ang), jnp.sin(ang))

        def _apply_rope(u, cos, sin):
            ue = u[..., ::2]
            uo = u[..., 1::2]
            real = cos * ue - sin * uo
            out = jnp.stack([real, jnp.zeros_like(real)], axis=-1)
            return out.reshape(u.shape)
        key = jax.random.key(seed)
        ks = jax.random.split(key, 6)
        B, T, H = (2, 256, 128)
        scale = 0.02
        return {'x': jax.random.normal(ks[0], (B, T, H), dtype=jnp.float32), 'Wq': jax.random.normal(ks[1], (H, H), dtype=jnp.float32) * scale, 'bq': jnp.zeros((H,), dtype=jnp.float32), 'Wk': jax.random.normal(ks[2], (H, H), dtype=jnp.float32) * scale, 'bk': jnp.zeros((H,), dtype=jnp.float32), 'Wv': jax.random.normal(ks[3], (H, H), dtype=jnp.float32) * scale, 'bv': jnp.zeros((H,), dtype=jnp.float32), 'Wo': jax.random.normal(ks[4], (H, H), dtype=jnp.float32) * scale, 'bo': jnp.zeros((H,), dtype=jnp.float32)}
    _L0_attn_b_in = _L0_attn_b_setup()

    def _L0_ffn_setup():
        import jax, jax.numpy as jnp
        import numpy as np
        NUM_EXPERTS = 8
        TOP_K = 2
        CAPACITY_FACTOR = 1.25
        key = jax.random.key(seed)
        ks = jax.random.split(key, 5)
        B, S, D, H, E = (4, 256, 128, 256, NUM_EXPERTS)
        scale = 0.02
        return {'x': jax.random.normal(ks[0], (B, S, D), dtype=jnp.float32), 'gate_w': jax.random.normal(ks[1], (E, D), dtype=jnp.float32) * scale, 'gate_proj_w': jax.random.normal(ks[2], (E, H, D), dtype=jnp.float32) * scale, 'up_proj_w': jax.random.normal(ks[3], (E, H, D), dtype=jnp.float32) * scale, 'down_proj_w': jax.random.normal(ks[4], (E, D, H), dtype=jnp.float32) * scale}
    _L0_ffn_in = _L0_ffn_setup()
    _d = {'L0_attn_a_hidden_states': _L0_attn_a_in['hidden_states'], 'L0_attn_a_qkv_w': _L0_attn_a_in['qkv_w'], 'L0_attn_a_q_norm_w': _L0_attn_a_in['q_norm_w'], 'L0_attn_a_k_norm_w': _L0_attn_a_in['k_norm_w'], 'L0_attn_a_lr_proj_w': _L0_attn_a_in['lr_proj_w'], 'L0_attn_a_lr_proj_b': _L0_attn_a_in['lr_proj_b'], 'L0_attn_a_w0': _L0_attn_a_in['w0'], 'L0_attn_a_w1': _L0_attn_a_in['w1'], 'L0_attn_a_w2': _L0_attn_a_in['w2'], 'L0_attn_b_Wq': _L0_attn_b_in['Wq'], 'L0_attn_b_bq': _L0_attn_b_in['bq'], 'L0_attn_b_Wk': _L0_attn_b_in['Wk'], 'L0_attn_b_bk': _L0_attn_b_in['bk'], 'L0_attn_b_Wv': _L0_attn_b_in['Wv'], 'L0_attn_b_bv': _L0_attn_b_in['bv'], 'L0_attn_b_Wo': _L0_attn_b_in['Wo'], 'L0_attn_b_bo': _L0_attn_b_in['bo'], 'L0_ffn_gate_w': _L0_ffn_in['gate_w'], 'L0_ffn_gate_proj_w': _L0_ffn_in['gate_proj_w'], 'L0_ffn_up_proj_w': _L0_ffn_in['up_proj_w'], 'L0_ffn_down_proj_w': _L0_ffn_in['down_proj_w']}
    _x0 = _d['L0_attn_a_hidden_states']
    _d['L0_attn_a_hidden_states'] = jax.random.normal(jax.random.fold_in(jax.random.key(seed), 1), (4, 1024, 128), dtype=_x0.dtype)
    del _x0
    return _d

def reference(L0_attn_a_hidden_states, L0_attn_a_qkv_w, L0_attn_a_q_norm_w, L0_attn_a_k_norm_w, L0_attn_a_lr_proj_w, L0_attn_a_lr_proj_b, L0_attn_a_w0, L0_attn_a_w1, L0_attn_a_w2, L0_attn_b_Wq, L0_attn_b_bq, L0_attn_b_Wk, L0_attn_b_bk, L0_attn_b_Wv, L0_attn_b_bv, L0_attn_b_Wo, L0_attn_b_bo, L0_ffn_gate_w, L0_ffn_gate_proj_w, L0_ffn_up_proj_w, L0_ffn_down_proj_w):

    def _L0_attn_a_ref(hidden_states, qkv_w, q_norm_w, k_norm_w, lr_proj_w, lr_proj_b, w0, w1, w2):
        import jax, jax.numpy as jnp
        import numpy as np
        B, S, D = (2, 1024, 128)
        NH = 4
        DH = D // NH
        DHID = 2 * DH
        CHUNK = 256
        BASE_LR_INV = float(np.log(np.expm1(0.001)))
        NS_COEFFS = ((4.0848, -6.8946, 2.927), (3.9505, -6.3029, 2.6377), (3.7418, -5.5913, 2.3037), (2.8769, -3.1427, 1.2046), (2.8366, -3.0525, 1.2012))

        def rms_norm(x, w, eps=1e-06):
            return x * jax.lax.rsqrt(jnp.mean(x * x, axis=-1, keepdims=True) + eps) * w

        def l2_normalize(x):
            return x / (jnp.linalg.norm(x, axis=-1, keepdims=True) + 1e-05)

        def silu(x):
            return x * jax.nn.sigmoid(x)

        def newton_schulz5(G):
            trans = G.shape[1] > G.shape[2]
            X = jnp.swapaxes(G, 1, 2) if trans else G
            X = X / (jnp.linalg.norm(X, axis=(1, 2), keepdims=True) + 1e-07)
            for a, b, c in NS_COEFFS:
                A = X @ jnp.swapaxes(X, 1, 2)
                Bm = b * A + c * (A @ A)
                X = a * X + Bm @ X
            return jnp.swapaxes(X, 1, 2) if trans else X
        b, s, d = hidden_states.shape
        qkv = hidden_states @ qkv_w.T
        q, k, v = jnp.split(qkv, 3, axis=-1)
        q = rms_norm(q, q_norm_w)
        k = rms_norm(k, k_norm_w)

        def to_heads(x):
            return x.reshape(b, s, NH, DH).transpose(0, 2, 1, 3).reshape(b * NH, s, DH)
        q = l2_normalize(to_heads(q))
        k = l2_normalize(to_heads(k))
        v = to_heads(v)
        lr = jax.nn.softplus(hidden_states @ lr_proj_w.T + lr_proj_b + BASE_LR_INV)
        lr = lr.reshape(b, s, NH, 3).transpose(0, 2, 1, 3).reshape(b * NH, s, 3)
        W0 = jnp.tile(w0, (b, 1, 1))
        W1 = jnp.tile(w1, (b, 1, 1))
        W2 = jnp.tile(w2, (b, 1, 1))
        n0 = jnp.linalg.norm(W0, axis=2, keepdims=True)
        n1 = jnp.linalg.norm(W1, axis=2, keepdims=True)
        n2 = jnp.linalg.norm(W2, axis=2, keepdims=True)
        nc = s // CHUNK

        def chunked(x):
            return x.reshape(b * NH, nc, CHUNK, -1).transpose(1, 0, 2, 3)
        qc, kc, vc, lrc = (chunked(q), chunked(k), chunked(v), chunked(lr))

        def renorm(w, n):
            return w / (jnp.linalg.norm(w, axis=2, keepdims=True) + 1e-05) * n

        def step(carry, xs):
            W0, W1, W2 = carry
            qi, ki, vi, li = xs
            l0, l1, l2 = (li[..., 0], li[..., 1], li[..., 2])
            gq = silu(jnp.einsum('bhd,bcd->bhc', W0, qi))
            hq = jnp.einsum('bhd,bcd->bhc', W2, qi)
            o = jnp.einsum('boh,bhc->bco', W1, gq * hq)
            gba = jnp.einsum('bhd,bcd->bhc', W0, ki)
            hbm = jnp.einsum('bhd,bcd->bhc', W2, ki)
            sg = silu(gba)
            hidden = sg * hbm
            dhid = jnp.einsum('boh,bco->bhc', W1, vi)
            dhbm = dhid * sg
            dgate = dhid * hbm
            sig = jax.nn.sigmoid(gba)
            dgba = dgate * sig * (1 + gba * (1 - sig))
            dw1 = jnp.einsum('bco,bhc,bc->boh', vi, hidden, l1)
            dw0 = jnp.einsum('bhc,bcd,bc->bhd', dgba, ki, l0)
            dw2 = jnp.einsum('bhc,bcd,bc->bhd', dhbm, ki, l2)
            dw0, dw1, dw2 = (newton_schulz5(dw0), newton_schulz5(dw1), newton_schulz5(dw2))
            W0 = renorm(W0 + dw0, n0)
            W1 = renorm(W1 + dw1, n1)
            W2 = renorm(W2 + dw2, n2)
            return ((W0, W1, W2), o)
        _, os_ = jax.lax.scan(step, (W0, W1, W2), (qc, kc, vc, lrc))
        out = os_.transpose(1, 0, 2, 3).reshape(b * NH, s, DH)
        return out.reshape(b, NH, s, DH).transpose(0, 2, 1, 3).reshape(b, s, d)

    def _L0_attn_b_ref(x, Wq, bq, Wk, bk, Wv, bv, Wo, bo):
        import jax, jax.numpy as jnp
        import numpy as np
        N_HEADS = 16

        def _rope_cos_sin(hs, T, dtype):
            t = jnp.arange(1, T + 1, dtype=dtype)[:, None]
            i = jnp.arange(hs // 2, dtype=dtype)
            theta = (1.0 / 10000.0) ** (2.0 * i / hs)
            ang = t * theta
            return (jnp.cos(ang), jnp.sin(ang))

        def _apply_rope(u, cos, sin):
            ue = u[..., ::2]
            uo = u[..., 1::2]
            real = cos * ue - sin * uo
            out = jnp.stack([real, jnp.zeros_like(real)], axis=-1)
            return out.reshape(u.shape)
        B, T, H = x.shape
        nh = N_HEADS
        hs = H // nh

        def proj(W, b):
            y = jnp.einsum('bth,oh->bto', x, W) + b
            return y.reshape(B, T, nh, hs).transpose(0, 2, 1, 3)
        Q = proj(Wq, bq)
        K = proj(Wk, bk)
        V = proj(Wv, bv)
        cos, sin = _rope_cos_sin(hs, T, x.dtype)
        Q = _apply_rope(Q, cos, sin)
        K = _apply_rope(K, cos, sin)
        scores = jnp.einsum('bhqd,bhkd->bhqk', Q, K) * (1.0 / jnp.sqrt(jnp.asarray(hs, x.dtype)))
        causal = jnp.tril(jnp.ones((T, T), dtype=bool))
        scores = jnp.where(causal, scores, jnp.asarray(-10000000000.0, x.dtype))
        att = jax.nn.softmax(scores, axis=-1)
        y = jnp.einsum('bhqk,bhkd->bhqd', att, V)
        y = y.transpose(0, 2, 1, 3).reshape(B, T, H)
        return jnp.einsum('bth,oh->bto', y, Wo) + bo

    def _L0_ffn_ref(x, gate_w, gate_proj_w, up_proj_w, down_proj_w):
        import jax, jax.numpy as jnp
        import numpy as np
        NUM_EXPERTS = 8
        TOP_K = 2
        CAPACITY_FACTOR = 1.25
        B, S, D = x.shape
        E, K = (NUM_EXPERTS, TOP_K)
        T = B * S
        xf = x.reshape(T, D)
        logits = xf @ gate_w.T
        probs = jax.nn.softmax(logits, axis=-1)
        top_p, top_i = jax.lax.top_k(probs, K)
        w = top_p / (jnp.sum(top_p, axis=-1, keepdims=True) + 1e-09)
        capacity = int(CAPACITY_FACTOR * T / E)
        oh = jax.nn.one_hot(top_i, E, dtype=jnp.int32)
        rank = jnp.cumsum(oh, axis=0) - 1
        my_rank = jnp.sum(rank * oh, axis=-1)
        keep = (my_rank < capacity).astype(w.dtype)
        comb = jnp.einsum('tk,tke->te', w * keep, oh.astype(w.dtype))
        out = jnp.zeros_like(xf)
        for e in range(E):
            g = jax.nn.silu(xf @ gate_proj_w[e].T)
            u = xf @ up_proj_w[e].T
            y = g * u @ down_proj_w[e].T
            out = out + comb[:, e:e + 1] * y
        return out.reshape(B, S, D)
    x = L0_attn_a_hidden_states
    x = x + _L0_attn_a_ref(_layernorm(x, axis=-1), L0_attn_a_qkv_w, L0_attn_a_q_norm_w, L0_attn_a_k_norm_w, L0_attn_a_lr_proj_w, L0_attn_a_lr_proj_b, L0_attn_a_w0, L0_attn_a_w1, L0_attn_a_w2)
    x = x + _L0_ffn_ref(_layernorm(x, axis=-1), L0_ffn_gate_w, L0_ffn_gate_proj_w, L0_ffn_up_proj_w, L0_ffn_down_proj_w)
    x = x + _L0_attn_b_ref(_layernorm(x, axis=-1), L0_attn_b_Wq, L0_attn_b_bq, L0_attn_b_Wk, L0_attn_b_bk, L0_attn_b_Wv, L0_attn_b_bv, L0_attn_b_Wo, L0_attn_b_bo)
    x = x + _L0_ffn_ref(_layernorm(x, axis=-1), L0_ffn_gate_w, L0_ffn_gate_proj_w, L0_ffn_up_proj_w, L0_ffn_down_proj_w)
    return x

_drawn_inputs = setup_inputs


def setup_inputs(seed=0):
    import zlib

    import numpy as np

    out = dict(_drawn_inputs(seed))
    spreads = {'L0_attn_a_q_norm_w': (1.0, 0.6),
     'L0_attn_a_k_norm_w': (1.0, 0.6),
     'L0_attn_a_lr_proj_b': (0.0, 0.8),
     'L0_attn_b_bq': (0.0, 0.8),
     'L0_attn_b_bk': (0.0, 0.8),
     'L0_attn_b_bv': (0.0, 0.319),
     'L0_attn_b_bo': (0.0, 0.1)}
    factors = {'L0_attn_a_qkv_w': 3.211,
     'L0_attn_a_lr_proj_w': 4.31,
     'L0_attn_a_w0': 3.553,
     'L0_attn_a_w1': 3.625,
     'L0_attn_a_w2': 3.532,
     'L0_attn_b_Wq': 8.0,
     'L0_attn_b_Wk': 8.0,
     'L0_attn_b_Wv': 8.0,
     'L0_ffn_gate_w': 5.689,
     'L0_ffn_gate_proj_w': 4.97,
     'L0_ffn_up_proj_w': 4.962,
     'L0_ffn_down_proj_w': 4.965}
    for name, (base, spread) in spreads.items():
        noise = np.random.default_rng([zlib.crc32(name.encode()), seed]).standard_normal(out[name].shape)
        drawn = base * np.exp(spread * noise) if base else spread * noise
        out[name] = jnp.asarray(drawn.astype(out[name].dtype))
    for name, factor in factors.items():
        out[name] = (out[name] * factor).astype(out[name].dtype)
    return out
```

```python
import concourse.bass as bass
from concourse import mybir
import math
from contextlib import ExitStack

F32, BF16 = mybir.dt.float32, mybir.dt.bfloat16
ALU = mybir.AluOpType
ACT = mybir.ActivationFunctionType
AX = mybir.AxisListType

P = 128
BATCH, SEQ, D = 4, 1024, 128
TOKENS = BATCH * SEQ
LN_EPS = 1e-5
EXPERTS = 8
CAPACITY = int(1.25 * TOKENS / EXPERTS)
GROUP = 512

BUFFERS = 2
TILES = SEQ // P
HEADS, HS = 16, 8
ROT = HS // 2
QUAD = 4
SCORE_SCALE = float(HS) ** -0.5
FW_HEADS, FW_D, FW_HID = 4, 32, 64
CHUNK = 256
CHUNKS = SEQ // CHUNK
BASE_LR_INV = math.log(math.expm1(0.001))
NEWTON = ((4.0848, -6.8946, 2.927), (3.9505, -6.3029, 2.6377), (3.7418, -5.5913, 2.3037),
          (2.8769, -3.1427, 1.2046), (2.8366, -3.0525, 1.2012))
MASKED = -1e30


def fast_weight_inputs(nc, x_in, tok_out, t_out, w_in, lr_bias, norm_w, consts):
    ctx = ExitStack()
    with ctx:
        sb = lambda n, shape, dt=F32: ctx.enter_context(nc.sbuf_tensor(f"prep_{n}", shape, dt))
        ps = lambda n, shape: ctx.enter_context(nc.psum_tensor(f"prep_{n}", shape, F32))
        sem = lambda n: ctx.enter_context(nc.semaphore(f"prep_{n}"))
        W = 3 * D + 3 * FW_HEADS
        w = sb("w", [P, W])
        bias = sb("bias", [P, 3 * FW_HEADS])
        nw = sb("nw", [P, 2 * D])
        ident = sb("ident", [P, P])
        half = sb("half", [P, TILES * 2 * FW_HEADS])
        negh = sb("negh", [P, TILES * 2])
        xb = sb("xb", [P, TILES, D])
        stats = sb("stats", [P, TILES, 6])
        mv = sb("mv", [P, TILES, 2])
        vareps = sb("vareps", [P, TILES])
        rstd = sb("rstd", [P, TILES])
        xn = sb("xn", [P, TILES, D])
        xT = sb("xT", [P, SEQ])
        raw = sb("raw", [P, TILES, W])
        sq = sb("sq", [P, TILES, 2 * D])
        qk = sb("qk", [P, TILES, 2 * D])
        qkn = sb("qkn", [P, TILES, 2 * D])
        ms = sb("ms", [P, TILES * 2])
        mse = sb("mse", [P, TILES * 2])
        rms = sb("rms", [P, TILES * 2])
        hs2 = sb("hs2", [P, TILES * 2 * FW_HEADS])
        hn = sb("hn", [P, TILES * 2 * FW_HEADS])
        rhn = sb("rhn", [P, TILES * 2 * FW_HEADS])
        L = 3 * FW_HEADS
        z = sb("z", [P, TILES, L])
        za = sb("za", [P, TILES, L])
        u = sb("u", [P, TILES, L])
        y1 = sb("y1", [P, TILES, L])
        ln = sb("ln", [P, TILES, L])
        dd = sb("dd", [P, TILES, L])
        one = sb("one", [P, TILES, L])
        lr = sb("lr", [P, TILES, L])
        tok = sb("tok", [P, CHUNKS, 2, 3 * D])
        tT = sb("tT", [P, CHUNKS, 3, CHUNK])
        psT = [ps(f"psT{s}", [P, 2, 512]) for s in range(2)]
        psW = [ps(f"psW{s}", [P, 512]) for s in range(4)]

        weights_in, setup, waits_passed = sem("weights_in"), sem("setup"), sem("waits_passed")
        x_loaded, stored = sem("x_loaded"), sem("stored")
        stats_done, rstd_done, xn_done, xt_psum, xt_done = sem("stats_done"), sem("rstd_done"), sem("xn_done"), sem("xt_psum"), sem("xt_done")
        w_psum, raw_done = sem("w_psum"), sem("raw_done")
        squares, sums, powers = sem("squares"), sem("sums"), sem("powers")
        scaled, heads_done, z_done, u_done, y1_done, ln_done, lr_done, tok_done = (sem(n) for n in ("scaled", "heads_done", "z_done", "u_done", "y1_done", "ln_done", "lr_done", "tok_done"))
        t_psum, t_done = sem("t_psum"), sem("t_done")
        SETUP = 2
        block = ctx.enter_context(nc.Block())

        def wait(engine, semaphore, value):
            engine.wait_ge(semaphore, value)
            engine.sem_inc(waits_passed, 1)

        @block.sync
        def _(sp):
            for count in (stored, t_done):
                sp.sem_inc(count, 1)
            for dst, src in ((w[:], w_in), (bias[:], lr_bias.broadcast_to([P, L])), (nw[:], norm_w.broadcast_to([P, 2 * D])), (ident[:], consts["ident"])):
                sp.dma_start(dst, src).then_inc(weights_in, 16)
            with sp.Fori(0, BATCH) as b:
                sp.dma_start(xb[:], x_in[bass.ds(b, 1)].rearrange("a (j p) d -> p (a j) d", p=P)).then_inc(x_loaded, 16)
                wait(sp, tok_done, b + 1)
                sp.dma_start(tok_out.rearrange("c p (b j) n -> b p c (j n)", b=BATCH)[bass.ds(b, 1)].rearrange("a p c n -> (a p) c n"),
                             tok[:].rearrange("p c j n -> p c (j n)")).then_inc(stored, 16)
                wait(sp, t_done, 1 + (b + 1) * 3)
                sp.dma_start(t_out.rearrange("c p b k n -> b p c (k n)")[bass.ds(b, 1)].rearrange("a p c n -> (a p) c n"),
                             tT[:].rearrange("p c k n -> p c (k n)")).then_inc(stored, 16)
                wait(sp, stored, 1 + b * 32 + 32)

        @block.gpsimd
        def _(pool):
            pool.memset(negh[:], -0.5).then_inc(setup, 1)
            pool.memset(half[:], 0.5).then_inc(setup, 1)
            pool.wait_ge(setup, SETUP)
            with pool.Fori(0, BATCH) as b:
                wait(pool, stats_done, b + 1)
                nc.gpsimd.tensor_scalar(vareps[:], mv[:, :, 1], LN_EPS, None, ALU.add)
                pool.drain()
                nc.gpsimd.tensor_tensor(rstd[:], vareps[:], negh[:, 0:TILES], ALU.pow).then_inc(rstd_done, 1)
                wait(pool, sums, 2 * b + 1)
                nc.gpsimd.tensor_scalar(mse[:], ms[:], 1.0 / D, 1e-6, ALU.mult, ALU.add)
                pool.drain()
                nc.gpsimd.tensor_tensor(rms[:], mse[:], negh[:], ALU.pow).then_inc(powers, 1)
                wait(pool, sums, 2 * b + 2)
                nc.gpsimd.tensor_tensor(hn[:], hs2[:], half[:], ALU.pow).then_inc(powers, 1)
                pool.wait_ge(heads_done, b + 1)
                pool.wait_ge(lr_done, b + 1)
                wait(pool, stored, 1 + b * 32)
                for n, (source, i) in enumerate(((qkn[:, :, D:2 * D], 0), (qkn[:, :, D:2 * D], 2), (raw[:, :, 2 * D:3 * D], 1))):
                    rate = lr[:].rearrange("p j (h i) -> p j h i", i=3)[:, :, :, i].unsqueeze(3).broadcast_to([P, TILES, FW_HEADS, FW_D])
                    last = nc.gpsimd.tensor_tensor(tok[:].rearrange("p c j n -> p (c j) n")[:, :, n * D:(n + 1) * D].rearrange("p j (h d) -> p j h d", d=FW_D),
                                                   source.rearrange("p j (h d) -> p j h d", d=FW_D), rate, ALU.mult)
                last.then_inc(tok_done, 1)

        @block.scalar
        def _(act):
            act.wait_ge(weights_in, 4 * 16)
            with act.Fori(0, BATCH) as b:
                act.wait_ge(xt_psum, b + 1)
                nc.scalar.activation(xT[:], psT[0][:].rearrange("p a n -> p (a n)"), ACT.Copy).then_inc(xt_done, 1)
                for j in range(TILES):
                    act.wait_ge(w_psum, b * TILES + (j + 1))
                    nc.scalar.activation(raw[:, j], psW[j % 4][:, 0:W], ACT.Copy).then_inc(raw_done, 1)
                act.drain()
                nc.scalar.activation(sq[:], raw[:, :, 0:2 * D], ACT.Square).then_inc(squares, 1)
                act.wait_ge(z_done, b + 1)
                nc.scalar.activation(u[:], za[:], ACT.Exp, scale=-1.0).then_inc(u_done, 1)
                act.wait_ge(y1_done, b + 1)
                nc.scalar.activation(ln[:], y1[:], ACT.Ln).then_inc(ln_done, 1)
                act.wait_ge(scaled, b + 1)
                nc.scalar.activation(sq[:], qk[:], ACT.Square).then_inc(squares, 1)
                act.wait_ge(stored, 1 + b * 32)
                for k in range(3):
                    act.wait_ge(t_psum, b * 3 + (k + 1))
                    nc.scalar.activation(tT[:, :, k], psT[k % 2][:].rearrange("p a (c n) -> p (a c) n", n=CHUNK), ACT.Copy).then_inc(t_done, 1)

        @block.tensor
        def _(pe):
            pe.wait_ge(weights_in, 4 * 16)
            with pe.Fori(0, BATCH) as b:
                def transpose_all(out, source, done):
                    for j in range(TILES):
                        last = nc.tensor.transpose(out[:, j // 4, (j % 4) * P:(j % 4 + 1) * P], source(j), ident[:])
                    last.then_inc(done, 1)
                pe.wait_ge(xn_done, b + 1)
                pe.wait_ge(t_done, 1 + b * 3)
                transpose_all(psT[0], lambda j: xn[:, j], xt_psum)
                pe.wait_ge(xt_done, b + 1)
                for j in range(TILES):
                    if j >= 4:
                        pe.wait_ge(raw_done, b * TILES + (j - 3))
                    nc.tensor.matmul(psW[j % 4][:, 0:W], xT[:, j * P:(j + 1) * P], w[:], start=True, stop=True).then_inc(w_psum, 1)
                pe.wait_ge(heads_done, b + 1)
                transpose_all(psT[0], lambda j: qkn[:, j, 0:D], t_psum)
                transpose_all(psT[1], lambda j: qkn[:, j, D:2 * D], t_psum)
                pe.wait_ge(t_done, 1 + b * 3 + 1)
                transpose_all(psT[0], lambda j: raw[:, j, 2 * D:3 * D], t_psum)

        @block.vector
        def _(dve):
            dve.wait_ge(weights_in, 4 * 16)
            dve.wait_ge(setup, SETUP)
            nc.vector.tensor_scalar(bias[:], bias[:], BASE_LR_INV, None, ALU.add)
            with dve.Fori(0, BATCH) as b:
                dve.wait_ge(x_loaded, b * 16 + 16)
                for j in range(TILES):
                    nc.vector.bn_stats(stats[:, j], xb[:, j])
                dve.drain()
                for j in range(TILES):
                    last = nc.vector.bn_aggr(mv[:, j], stats[:, j])
                last.then_inc(stats_done, 1)
                dve.wait_ge(rstd_done, b + 1)
                for j in range(TILES):
                    last = nc.vector.tensor_scalar(xn[:, j], xb[:, j], mv[:, j, 0:1], rstd[:, j:j + 1], ALU.subtract, ALU.mult)
                last.then_inc(xn_done, 1)
                dve.wait_ge(raw_done, (b + 1) * TILES)
                nc.vector.tensor_tensor(z[:], raw[:, :, 3 * D:W], bias[:].unsqueeze(1).broadcast_to([P, TILES, L]), ALU.add)
                dve.drain()
                nc.vector.scalar_tensor_tensor(za[:], z[:], -1.0, z[:], ALU.mult, ALU.max).then_inc(z_done, 1)
                dve.wait_ge(squares, 2 * b + 1)
                nc.vector.reduce_sum(ms[:], sq[:].rearrange("p j (k d) -> p (j k) d", d=D), AX.X).then_inc(sums, 1)
                dve.wait_ge(u_done, b + 1)
                nc.vector.tensor_scalar(y1[:], u[:], 1.0, None, ALU.add).then_inc(y1_done, 1)
                dve.wait_ge(powers, 2 * b + 1)
                nc.vector.tensor_tensor(qk[:].rearrange("p j (k d) -> p j k d", d=D), raw[:, :, 0:2 * D].rearrange("p j (k d) -> p j k d", d=D),
                                        rms[:].rearrange("p (j k) -> p j k", k=2).unsqueeze(3).broadcast_to([P, TILES, 2, D]), ALU.mult)
                dve.drain()
                nc.vector.tensor_tensor(qk[:], qk[:], nw[:].unsqueeze(1).broadcast_to([P, TILES, 2 * D]), ALU.mult).then_inc(scaled, 1)
                nc.vector.tensor_scalar(dd[:], y1[:], -1.0, None, ALU.add)
                dve.drain()
                nc.vector.tensor_scalar(one[:], dd[:], 0.0, None, ALU.is_equal)
                wait(dve, ln_done, b + 1)
                dve.drain()
                nc.vector.tensor_tensor(dd[:], dd[:], one[:], ALU.add)
                nc.vector.tensor_tensor(ln[:], ln[:], one[:], ALU.add)
                dve.drain()
                nc.vector.reciprocal(dd[:], dd[:])
                nc.vector.tensor_tensor(ln[:], ln[:], u[:], ALU.mult)
                dve.drain()
                nc.vector.tensor_tensor(ln[:], ln[:], dd[:], ALU.mult)
                dve.drain()
                nc.vector.scalar_tensor_tensor(lr[:], z[:], 0.0, ln[:], ALU.max, ALU.add).then_inc(lr_done, 1)
                dve.wait_ge(squares, 2 * b + 2)
                nc.vector.reduce_sum(hs2[:], sq[:].rearrange("p j (k d) -> p (j k) d", d=FW_D), AX.X).then_inc(sums, 1)
                dve.wait_ge(powers, 2 * b + 2)
                nc.vector.tensor_scalar(hn[:], hn[:], 1e-5, None, ALU.add)
                dve.drain()
                nc.vector.reciprocal(rhn[:], hn[:])
                dve.drain()
                nc.vector.tensor_tensor(qkn[:].rearrange("p j (k d) -> p (j k) d", d=FW_D), qk[:].rearrange("p j (k d) -> p (j k) d", d=FW_D),
                                        rhn[:].unsqueeze(2).broadcast_to([P, TILES * 2 * FW_HEADS, FW_D]), ALU.mult).then_inc(heads_done, 1)


def fast_weight_stage(nc, x_in, x_out, tok_in, t_in, w_start, consts):
    H, HID, DH = FW_HEADS, FW_HID, FW_D
    ctx = ExitStack()
    with ctx:
        sb = lambda n, shape, dt=F32: ctx.enter_context(nc.sbuf_tensor(f"fw_{n}", shape, dt))
        sem = lambda n: ctx.enter_context(nc.semaphore(f"fw_{n}"))
        ident = sb("ident", [P, P])
        block_ones = sb("block_ones", [P, 3, P])
        eye = sb("eye", [P, DH])
        eyes = sb("eyes", [P, len(NEWTON), DH])
        half = sb("half", [P, 36])
        state = sb("state", [P, 3, 256])
        norm0 = sb("norm0", [P, 20])
        tok = sb("tok", [P, 2 * BATCH, 3 * D])
        T = sb("T", [P, BATCH, 3, CHUNK])
        xc = sb("xc", [P, 2 * BATCH, D])
        xo = sb("xo", [P, 2 * BATCH, D])
        wb = sb("wb", [P, BATCH, 3, 256])
        w1b = sb("w1b", [P, BATCH, 2, 2 * DH])
        two = lambda n: [sb(f"{n}{s}", [P, 2, 256]) for s in range(2)]
        th, hb, sig, sg, v, dhbm, dgate, hidden, ds, dgba = (two(n) for n in ("th", "hb", "sig", "sg", "v", "dhbm", "dgate", "hidden", "ds", "dgba"))
        xr = sb("xr", [P, 3, BATCH, HID])
        yr = sb("yr", [P, 3, BATCH, 2, DH])
        X = sb("X", [P, 3, BATCH, HID])
        Y = sb("Y", [P, 3, BATCH, 2, DH])
        sq = sb("sq", [P, 768])
        rs = sb("rs", [P, 12])
        fro = sb("fro", [P, 3, 12])
        froot = sb("froot", [P, 3, 12])
        rn = sb("rn", [P, 3, 12])
        A = [sb(f"A{g}", [P, BATCH, DH]) for g in range(3)]
        T1 = [sb(f"T1{g}", [P, BATCH, DH]) for g in range(3)]
        M = [sb(f"M{g}", [P, BATCH, DH]) for g in range(3)]
        ssq = sb("ssq", [P, 20])
        wn = sb("wn", [P, 20])
        wf = sb("wf", [P, 20])
        qth = sb("qth", [P, 512])
        qgated = sb("qgated", [P, 512])
        prod = sb("prod", [P, 2, CHUNK])
        banks = ctx.enter_context(nc.psum_tensor("fw_banks", [P, 8, 512], F32))

        weights_in, setup, waits_passed = sem("weights_in"), sem("setup"), sem("waits_passed")
        tok_in_s, t_in_s, x_in_s, x_stored = sem("tok_loaded"), sem("t_loaded"), sem("x_loaded"), sem("x_stored")
        norm_sq, norm_root, state_done, turned = sem("norm_sq"), sem("norm_root"), sem("state_done"), sem("turned")
        wb_act, wb_dve, wb_pool = sem("wb_act"), sem("wb_dve"), sem("wb_pool")
        kv_psum, tanh_done, sg_done, v_done, dgate_done, back_dve, back_pool = (sem(n) for n in ("kv_psum", "tanh_done", "sg_done", "v_done", "dgate_done", "back_dve", "back_pool"))
        dw_psum, xr_done, yr_done, rs_done, fro_psum, fro_done, start_done = (sem(n) for n in ("dw_psum", "xr_done", "yr_done", "rs_done", "fro_psum", "fro_done", "start_done"))
        a_psum, a_done, aa_psum, m_done, xy_psum, x_done, y_done = (sem(n) for n in ("a_psum", "a_done", "aa_psum", "m_done", "xy_psum", "x_done", "y_done"))
        q_psum, qth_done, prod_done, o_psum, o_done = (sem(n) for n in ("q_psum", "qth_done", "prod_done", "o_psum", "o_done"))
        IT = len(NEWTON)
        SETUP = 3
        block = ctx.enter_context(nc.Block())

        def quadrant(h):
            return slice(DH * h, DH * h + DH)

        def side(h):
            return slice(HID * (h % 2), HID * (h % 2) + HID)

        def wait(engine, semaphore, value):
            engine.wait_ge(semaphore, value)
            engine.sem_inc(waits_passed, 1)

        @block.sync
        def _(sp):
            for count in (x_stored, o_done, x_done, y_done):
                sp.sem_inc(count, 1)
            for dst, src in ((ident[:], consts["ident"]), (block_ones[:], consts["block_ones"]), (eye[:], consts["eye"]), (state[:], w_start)):
                sp.dma_start(dst, src).then_inc(weights_in, 16)

            def load_tok(c):
                sp.dma_start(tok[:], tok_in[bass.ds(c, 1)].rearrange("a p b n -> (a p) b n")).then_inc(tok_in_s, 16)

            def load_t(c):
                sp.dma_start(T[:], t_in[bass.ds(c, 1)].rearrange("a p b k n -> (a p) b k n")).then_inc(t_in_s, 16)

            def load_x(c):
                for b in range(BATCH):
                    sp.dma_start(xc[:, 2 * b:2 * b + 2], x_in[b].rearrange("(c j p) d -> c p j d", c=CHUNKS, p=P)[bass.ds(c, 1)].rearrange("a p j d -> (a p) j d")).then_inc(x_in_s, 16)

            def store_x(c):
                wait(sp, o_done, 1 + (c + 1) * BATCH)
                for b in range(BATCH):
                    sp.dma_start(x_out[b].rearrange("(c j p) d -> c p j d", c=CHUNKS, p=P)[bass.ds(c, 1)].rearrange("a p j d -> (a p) j d"), xo[:, 2 * b:2 * b + 2]).then_inc(x_stored, 16)
                wait(sp, x_stored, 1 + (c + 1) * BATCH * 16)

            load_tok(0)
            load_t(0)
            load_x(0)
            with sp.Fori(0, CHUNKS - 1) as c:
                wait(sp, dw_psum, c + 1)
                load_tok(c + 1)
                store_x(c)
                load_t(c + 1)
                load_x(c + 1)
            store_x(CHUNKS - 1)

        def root_of_squares(c):
            nc.gpsimd.tensor_tensor(wn[:], ssq[:], half[:, 0:20], ALU.pow).then_inc(norm_root, 1)

        @block.gpsimd
        def _(pool):
            pool.memset(half[:], 0.5).then_inc(setup, 1)
            pool.memset(wb[:], 0.0).then_inc(setup, 1)
            pool.memset(w1b[:], 0.0).then_inc(setup, 1)
            pool.wait_ge(setup, SETUP)
            pool.wait_ge(weights_in, 4 * 16)
            pool.wait_ge(norm_sq, 1)
            root_of_squares(0)

            def place(c):
                for h in range(H):
                    last = nc.gpsimd.tensor_copy(wb[quadrant(h), :, 2, HID * h:HID * h + HID], state[quadrant(h), 2, :].rearrange("p (b n) -> p b n", b=BATCH))
                last.then_inc(wb_pool, 1)

            with pool.Fori(0, CHUNKS - 1) as c:
                wait(pool, state_done, c + 1)
                place(c)
                for b in range(BATCH):
                    s = b % 2
                    wait(pool, sg_done, c * BATCH + b + 1)
                    nc.gpsimd.tensor_tensor(hidden[s][:], sg[s][:], hb[s][:], ALU.mult)
                    wait(pool, v_done, c * BATCH + b + 1)
                    nc.gpsimd.tensor_tensor(ds[s][:], v[s][:], sig[s][:], ALU.mult)
                    wait(pool, dgate_done, c * BATCH + b + 1)
                    pool.drain()
                    nc.gpsimd.tensor_tensor(dgba[s][:], ds[s][:], dgate[s][:], ALU.mult).then_inc(back_pool, 1)
                pool.wait_ge(fro_psum, c + 1)
                wait(pool, fro_done, c + 1)
                nc.gpsimd.tensor_tensor(froot[:], fro[:], half[:].rearrange("p (a n) -> p a n", a=3), ALU.pow).then_inc(start_done, 1)
                wait(pool, norm_sq, c + 2)
                root_of_squares(c + 1)
            pool.wait_ge(state_done, CHUNKS)
            place(CHUNKS - 1)

        @block.scalar
        def _(act):
            act.wait_ge(setup, SETUP)
            act.wait_ge(weights_in, 4 * 16)

            def distribute(c):
                act.wait_ge(turned, c + 1)
                for h in range(H):
                    nc.scalar.activation(wb[quadrant(h), :, 0, HID * h:HID * h + HID], banks[quadrant(h), 0, 0:256].rearrange("p (b n) -> p b n", b=BATCH), ACT.Copy)
                for m in range(2):
                    last = nc.scalar.activation(w1b[side(m), :, 0, DH * m:DH * m + DH], banks[side(m), 2, 0:P].rearrange("p (b n) -> p b n", b=BATCH), ACT.Copy)
                last.then_inc(wb_act, 1)

            def query_tanh(c, b):
                act.wait_ge(q_psum, c * BATCH + b + 1)
                nc.scalar.activation(qth[:], banks[:, 6], ACT.Tanh, scale=0.5).then_inc(qth_done, 1)

            with act.Fori(0, CHUNKS - 1) as c:
                distribute(c)
                for b in range(BATCH):
                    s = b % 2
                    act.wait_ge(kv_psum, c * BATCH + b + 1)
                    if b >= 2:
                        act.wait_ge(back_pool, c * BATCH + b - 1)
                        act.wait_ge(back_dve, c * BATCH + b - 1)
                    nc.scalar.activation(th[s][:], banks[:, 0:2, 0:256], ACT.Tanh, scale=0.5)
                    nc.scalar.activation(hb[s][:], banks[:, 0:2, 256:512], ACT.Copy).then_inc(tanh_done, 1)
                act.wait_ge(dw_psum, c + 1)
                for g in range(3):
                    src = banks[:, 5, 256 * g:256 * g + 256] if g < 2 else banks[:, 7, 0:256]
                    last = nc.scalar.activation(yr[:, g], src.rearrange("p (b k n) -> p b k n", b=BATCH, k=2), ACT.Copy)
                last.then_inc(yr_done, 1)
                for it in range(IT):
                    step = (c * IT + it) * 3
                    for g in range(3):
                        act.wait_ge(a_psum, step + g + 1)
                        nc.scalar.activation(A[g][:], banks[:, g, 0:P].rearrange("p (b n) -> p b n", b=BATCH), ACT.Copy).then_inc(a_done, 1)
                    if it < BATCH:
                        query_tanh(c, it)
                    for g in range(3):
                        act.wait_ge(xy_psum, step + g + 1)
                        nc.scalar.activation(X[:, g], banks[:, 3, 0:256].rearrange("p (b n) -> p b n", b=BATCH), ACT.Copy).then_inc(x_done, 1)
            distribute(CHUNKS - 1)
            for b in range(BATCH):
                query_tanh(CHUNKS - 1, b)

        @block.tensor
        def _(pe):
            pe.wait_ge(setup, SETUP)
            pe.wait_ge(weights_in, 4 * 16)

            def turn_state(c):
                wait(pe, state_done, c + 1)
                for g in range(2):
                    for b in range(BATCH):
                        for h in range(H):
                            k = (b * 2 + h // 2) * DH
                            nc.tensor.matmul(banks[quadrant(h), g, HID * b:HID * b + HID], state[side(h), g, k:k + DH], ident[side(h), side(h)], start=True, stop=True)
                for b in range(BATCH):
                    for h in range(H):
                        last = nc.tensor.matmul(banks[side(h), 2 + h // 2, DH * b:DH * b + DH], state[quadrant(h), 2, HID * b:HID * b + HID], ident[quadrant(h), quadrant(h)], start=True, stop=True)
                last.then_inc(turned, 1)

            def backward(c, b):
                if b == 0:
                    for w in (wb_act, wb_dve, wb_pool):
                        pe.wait_ge(w, c + 1)
                    wait(pe, t_in_s, (c + 1) * 16)
                else:
                    wait(pe, dgate_done, c * BATCH + b)
                for j in range(2):
                    nc.tensor.matmul(banks[:, j, :], T[:, b, 1, j * P:(j + 1) * P], wb[:, b, 0:2, :], start=True, stop=True)
                    last = nc.tensor.matmul(banks[:, 2, 256 * j:256 * j + 256], T[:, b, 2, j * P:(j + 1) * P], wb[:, b, 2, :], start=True, stop=True)
                last.then_inc(kv_psum, 1)

            def gradients(c, b):
                pe.wait_ge(back_dve, c * BATCH + b + 1)
                wait(pe, back_pool, c * BATCH + b + 1)
                if b == 0:
                    wait(pe, tok_in_s, (c + 1) * 16)
                s = b % 2
                for g, left in enumerate((dgba[s], dhbm[s], hidden[s])):
                    for h in range(H):
                        xb_ = banks[quadrant(h), 3, 256 * g + HID * b:256 * g + HID * (b + 1)] if g < 2 else banks[quadrant(h), 4, HID * b:HID * (b + 1)]
                        k = (b * 2 + h // 2) * DH
                        yb_ = banks[side(h), 5, 256 * g + k:256 * g + k + DH] if g < 2 else banks[side(h), 7, k:k + DH]
                        rows = lambda j: tok[:, 2 * b + j, D * g + DH * h:D * g + DH * h + DH]
                        cols = lambda j: left[:, j, HID * h:HID * h + HID]
                        for j in range(2):
                            nc.tensor.matmul(xb_, rows(j), cols(j), start=(j == 0), stop=(j == 1))
                        for j in range(2):
                            last = nc.tensor.matmul(yb_, cols(j), rows(j), start=(j == 0), stop=(j == 1))
                if b == BATCH - 1:
                    last.then_inc(dw_psum, 1)

            def query(c, b):
                if b == 0:
                    for w in (wb_act, wb_dve, wb_pool):
                        pe.wait_ge(w, c + 1)
                    pe.wait_ge(t_in_s, (c + 1) * 16)
                wait(pe, o_done, 1 + c * BATCH + b)
                for g in range(2):
                    for k in range(2):
                        last = nc.tensor.matmul(banks[:, 6 + g, CHUNK * k:CHUNK * (k + 1)], wb[:, b, g, P * k:P * k + P], T[:, b, 0, :], start=True, stop=True)
                last.then_inc(q_psum, 1)

            def output(c, b):
                wait(pe, prod_done, c * BATCH + b + 1)
                for j in range(2):
                    for k in range(2):
                        last = nc.tensor.matmul(banks[:, 7, D * j + 2 * DH * k:D * j + 2 * DH * (k + 1)], prod[:, k, j * P:(j + 1) * P], w1b[:, b, k, :], start=True, stop=True)
                last.then_inc(o_psum, 1)

            with pe.Fori(0, CHUNKS - 1) as c:
                turn_state(c)
                for b in range(BATCH):
                    backward(c, b)
                    if b == 0:
                        wait(pe, o_done, 1 + c * BATCH)
                    if b >= 1:
                        gradients(c, b - 1)
                gradients(c, BATCH - 1)
                wait(pe, rs_done, c + 1)
                for n in range(3):
                    last = nc.tensor.matmul(banks[:, 6, 16 * n:16 * n + 12], block_ones[:, n], rs[:], start=True, stop=True)
                last.then_inc(fro_psum, 1)
                wait(pe, yr_done, c + 1)
                for it in range(IT):
                    step = (c * IT + it) * 3
                    for g in range(3):
                        if it == 0:
                            wait(pe, m_done, c * (IT * 3 + 1) + 1)
                        else:
                            wait(pe, y_done, 1 + step - 3 + g + 1)
                        for b in range(BATCH):
                            for h in range(H):
                                y = Y[side(h), g, b, h // 2, :]
                                last = nc.tensor.matmul(banks[quadrant(h), g, DH * b:DH * b + DH], y, y, start=True, stop=True)
                        last.then_inc(a_psum, 1)
                    if it < BATCH:
                        query(c, it)
                    for g in range(3):
                        wait(pe, a_done, step + g + 1)
                        for b in range(BATCH):
                            for h in range(H):
                                a = A[g][quadrant(h), b, :]
                                last = nc.tensor.matmul(banks[quadrant(h), g, P + DH * b:P + DH * b + DH], a, a, start=True, stop=True)
                        last.then_inc(aa_psum, 1)
                    for g in range(3):
                        wait(pe, m_done, c * (IT * 3 + 1) + 1 + it * 3 + g + 1)
                        pe.wait_ge(x_done, 1 + step + g)
                        wait(pe, y_done, 1 + step + g)
                        for b in range(BATCH):
                            for h in range(H):
                                m, x = M[g][quadrant(h), b, :], X[quadrant(h), g, b, :]
                                nc.tensor.matmul(banks[quadrant(h), 3, HID * b:HID * b + HID], m, x, start=True, stop=True)
                                last = nc.tensor.matmul(banks[side(h), 4 + h // 2, DH * b:DH * b + DH], x, m, start=True, stop=True)
                        last.then_inc(xy_psum, 1)
                    if it < BATCH:
                        output(c, it)
            turn_state(CHUNKS - 1)
            for b in range(BATCH):
                query(CHUNKS - 1, b)
                output(CHUNKS - 1, b)

        @block.vector
        def _(dve):
            dve.wait_ge(setup, SETUP)
            dve.wait_ge(weights_in, 4 * 16)

            def sum_state_squares():
                nc.vector.tensor_tensor(sq[:], state[:].rearrange("p g n -> p (g n)"), state[:].rearrange("p g n -> p (g n)"), ALU.mult)
                dve.drain()
                nc.vector.reduce_sum(ssq[:, 0:16], sq[:, 0:512].rearrange("p (a n) -> p a n", n=DH), AX.X)
                nc.vector.reduce_sum(ssq[:, 16:20], sq[:, 512:768].rearrange("p (a n) -> p a n", n=HID), AX.X).then_inc(norm_sq, 1)

            def distribute(c):
                dve.wait_ge(turned, c + 1)
                for h in range(H):
                    nc.vector.tensor_copy(wb[quadrant(h), :, 1, HID * h:HID * h + HID], banks[quadrant(h), 1, 0:256].rearrange("p (b n) -> p b n", b=BATCH))
                for m in range(2):
                    last = nc.vector.tensor_copy(w1b[side(m), :, 1, DH * m:DH * m + DH], banks[side(m), 3, 0:P].rearrange("p (b n) -> p b n", b=BATCH))
                last.then_inc(wb_dve, 1)

            def query_product(c, b):
                dve.wait_ge(qth_done, c * BATCH + b + 1)
                nc.vector.scalar_tensor_tensor(qgated[:], qth[:], 1.0, banks[:, 6], ALU.add, ALU.mult)
                dve.drain()
                nc.vector.tensor_tensor(prod[:].rearrange("p k n -> p (k n)"), qgated[:], banks[:, 7], ALU.mult).then_inc(prod_done, 1)

            def add_output(c, b):
                if b == 0:
                    dve.wait_ge(x_in_s, (c + 1) * BATCH * 16)
                    dve.wait_ge(x_stored, 1 + c * BATCH * 16)
                dve.wait_ge(o_psum, c * BATCH + b + 1)
                nc.vector.scalar_tensor_tensor(xo[:, 2 * b:2 * b + 2], banks[:, 7, 0:2 * D].rearrange("p (j d) -> p j d", d=D), 0.5, xc[:, 2 * b:2 * b + 2],
                                               ALU.mult, ALU.add).then_inc(o_done, 1)

            for n, (a, _, _) in enumerate(NEWTON):
                nc.vector.tensor_scalar(eyes[:, n], eye[:], a, None, ALU.mult)
            sum_state_squares()
            dve.wait_ge(norm_root, 1)
            nc.vector.tensor_copy(norm0[:], wn[:]).then_inc(state_done, 1)

            with dve.Fori(0, CHUNKS - 1) as c:
                distribute(c)
                for b in range(BATCH):
                    s = b % 2
                    dve.wait_ge(tanh_done, c * BATCH + b + 1)
                    gba, dhid = banks[:, 0:2, 0:256], banks[:, 2].rearrange("p (j n) -> p j n", j=2)
                    nc.vector.tensor_scalar(sig[s][:], th[s][:], 0.5, 0.5, ALU.mult, ALU.add)
                    dve.drain()
                    nc.vector.tensor_tensor(sg[s][:], gba, sig[s][:], ALU.mult).then_inc(sg_done, 1)
                    dve.drain()
                    nc.vector.scalar_tensor_tensor(v[s][:], gba, 1.0, sg[s][:], ALU.add, ALU.subtract).then_inc(v_done, 1)
                    nc.vector.tensor_tensor(dhbm[s][:], dhid, sg[s][:], ALU.mult).then_inc(back_dve, 1)
                    nc.vector.tensor_tensor(dgate[s][:], dhid, hb[s][:], ALU.mult).then_inc(dgate_done, 1)
                dve.wait_ge(dw_psum, c + 1)
                for g in range(3):
                    src = banks[:, 3, 256 * g:256 * g + 256] if g < 2 else banks[:, 4, 0:256]
                    nc.vector.tensor_copy(xr[:, g], src.rearrange("p (b n) -> p b n", b=BATCH))
                dve.drain()
                nc.vector.tensor_tensor(sq[:], xr[:].rearrange("p g b n -> p (g b n)"), xr[:].rearrange("p g b n -> p (g b n)"), ALU.mult)
                dve.drain()
                nc.vector.reduce_sum(rs[:], sq[:].rearrange("p (a n) -> p a n", n=HID), AX.X).then_inc(rs_done, 1)
                dve.wait_ge(fro_psum, c + 1)
                nc.vector.tensor_copy(fro[:], banks[:, 6, 0:48].rearrange("p (a n) -> p a n", n=16)[:, :, 0:12]).then_inc(fro_done, 1)
                dve.wait_ge(start_done, c + 1)
                nc.vector.tensor_scalar(froot[:], froot[:], 1e-7, None, ALU.add)
                dve.drain()
                nc.vector.reciprocal(rn[:], froot[:])
                wait(dve, yr_done, c + 1)
                dve.drain()
                nc.vector.tensor_tensor(X[:].rearrange("p g b n -> p (g b) n"), xr[:].rearrange("p g b n -> p (g b) n"), rn[:, 0].unsqueeze(2).broadcast_to([P, 12, HID]), ALU.mult)
                nc.vector.tensor_tensor(Y[:].rearrange("p g b k n -> p (g b) k n"), yr[:].rearrange("p g b k n -> p (g b) k n"),
                                        rn[:, 1:3].rearrange("p k a -> p a k").unsqueeze(3).broadcast_to([P, 12, 2, DH]), ALU.mult).then_inc(m_done, 1)
                for it, (_, b_, c_) in enumerate(NEWTON):
                    step = (c * IT + it) * 3
                    for g in range(3):
                        dve.wait_ge(a_done, step + g + 1)
                        nc.vector.scalar_tensor_tensor(T1[g][:], A[g][:], b_, eyes[:, it].unsqueeze(1).broadcast_to([P, BATCH, DH]), ALU.mult, ALU.add)
                    dve.drain()
                    for g in range(3):
                        dve.wait_ge(aa_psum, step + g + 1)
                        nc.vector.scalar_tensor_tensor(M[g][:], banks[:, g, P:2 * P].rearrange("p (b n) -> p b n", b=BATCH), c_, T1[g][:], ALU.mult, ALU.add).then_inc(m_done, 1)
                    if it < BATCH:
                        query_product(c, it)
                    for g in range(3):
                        dve.wait_ge(xy_psum, step + g + 1)
                        nc.vector.tensor_copy(Y[:, g].rearrange("p b k n -> p k b n"), banks[:, 4:6, 0:P].rearrange("p k (b n) -> p k b n", b=BATCH)).then_inc(y_done, 1)
                    if it < BATCH:
                        add_output(c, it)
                wait(dve, x_done, 1 + (c + 1) * IT * 3)
                dve.drain()
                nc.vector.tensor_tensor(state[:, 0:2].rearrange("p g n -> p (g n)"), state[:, 0:2].rearrange("p g n -> p (g n)"), Y[:, 0:2].rearrange("p g b k n -> p (g b k n)"), ALU.add)
                nc.vector.tensor_tensor(state[:, 2], state[:, 2], X[:, 2].rearrange("p b n -> p (b n)"), ALU.add)
                dve.drain()
                sum_state_squares()
                dve.wait_ge(norm_root, c + 2)
                nc.vector.tensor_scalar(wn[:], wn[:], 1e-5, None, ALU.add)
                dve.drain()
                nc.vector.reciprocal(wf[:], wn[:])
                dve.drain()
                nc.vector.tensor_tensor(wf[:], wf[:], norm0[:], ALU.mult)
                dve.drain()
                nc.vector.tensor_tensor(state[:, 0:2].rearrange("p g (a n) -> p (g a) n", n=DH), state[:, 0:2].rearrange("p g (a n) -> p (g a) n", n=DH),
                                        wf[:, 0:16].unsqueeze(2).broadcast_to([P, 16, DH]), ALU.mult)
                nc.vector.tensor_tensor(state[:, 2].rearrange("p (a n) -> p a n", n=HID), state[:, 2].rearrange("p (a n) -> p a n", n=HID),
                                        wf[:, 16:20].unsqueeze(2).broadcast_to([P, 4, HID]), ALU.mult).then_inc(state_done, 1)
            distribute(CHUNKS - 1)
            for b in range(BATCH):
                query_product(CHUNKS - 1, b)
                add_output(CHUNKS - 1, b)


def expert_stage(nc, name, x_in, x_out, gate_w, gate_proj, up_proj, down_proj, consts):
    groups, tiles = TOKENS // GROUP, GROUP // P
    units = 2 * EXPERTS
    ctx = ExitStack()
    with ctx:
        sb = lambda n, shape, dt=F32: ctx.enter_context(nc.sbuf_tensor(f"{name}_{n}", shape, dt))
        ps = lambda n, shape: ctx.enter_context(nc.psum_tensor(f"{name}_{n}", shape, F32))
        sem = lambda n: ctx.enter_context(nc.semaphore(f"{name}_{n}"))

        wg = sb("wg", [P, EXPERTS, 2 * P])
        wu = sb("wu", [P, EXPERTS, 2 * P])
        wd = sb("wd", [P, EXPERTS, 2, P])
        wr = sb("wr", [P, EXPERTS])
        ident = sb("ident", [P, P])
        tri = sb("tri", [P, P])
        ones = sb("ones", [P, P])
        rev = sb("rev", [P, tiles, EXPERTS])
        negh = sb("negh", [P, tiles])
        acc = [sb(f"acc{s}", [P, tiles, P]) for s in range(2)]
        stats = sb("stats", [P, tiles, 6])
        mv = sb("mv", [P, tiles, 2])
        vareps = sb("vareps", [P, tiles])
        rstd = sb("rstd", [P, tiles])
        xn = sb("xn", [P, tiles, P])
        xT = [sb(f"xT{s}", [P, GROUP]) for s in range(2)]
        th = [sb(f"th{s}", [P, GROUP]) for s in range(2)]
        gated = [sb(f"gated{k}", [P, GROUP]) for k in range(2)]
        hid = [[sb(f"hid{s}{k}", [P, GROUP]) for k in range(2)] for s in range(2)]
        lmax = sb("lmax", [P, tiles])
        lsub = sb("lsub", [P, tiles, EXPERTS])
        prob = sb("prob", [P, tiles, EXPERTS])
        probs2 = sb("probs2", [P, tiles, EXPERTS])
        psum_ = sb("psum_", [P, tiles])
        pinv = sb("pinv", [P, tiles])
        eq = sb("eq", [P, tiles, EXPERTS])
        pick = sb("pick", [P, tiles])
        top = sb("top", [P, 2, tiles])
        chosen = sb("chosen", [P, tiles, 2, EXPERTS])
        wsum = sb("wsum", [P, tiles])
        winv = sb("winv", [P, tiles])
        rank = sb("rank", [P, tiles, 2, EXPERTS])
        carry = sb("carry", [P, 2, EXPERTS])
        comb2 = sb("comb2", [P, tiles, 2, EXPERTS])
        comb = [sb(f"comb{s}", [P, tiles, EXPERTS]) for s in range(2)]

        ps_g = [ps(f"ps_g{s}", [P, GROUP]) for s in range(2)]
        ps_u = [ps(f"ps_u{s}", [P, GROUP]) for s in range(2)]
        ps_y = [ps(f"ps_y{s}", [P, tiles, P]) for s in range(2)]
        ps_t = ps("ps_t", [P, GROUP])
        ps_r = ps("ps_r", [P, 512])
        logits = ps_r[:, 0:tiles * EXPERTS].rearrange("p (j e) -> p j e", e=EXPERTS)
        counts = ps_r[:, 128:128 + tiles * 2 * EXPERTS].rearrange("p (j k e) -> p j k e", k=2, e=EXPERTS)
        total = ps_r[:, 256:256 + 2 * EXPERTS].rearrange("p (k e) -> p k e", e=EXPERTS)

        weights_in, x_loaded, x_stored = sem("weights_in"), [sem("x_loaded0"), sem("x_loaded1")], sem("x_stored")
        stats_done, rstd_done, xn_done, xt_psum, xt_done = sem("stats_done"), sem("rstd_done"), sem("xn_done"), sem("xt_psum"), sem("xt_done")
        logits_done, lsub_done, exp_done, chosen_done, ranks_done = sem("logits_done"), sem("lsub_done"), sem("exp_done"), sem("chosen_done"), sem("ranks_done")
        gu_done, tanh_done, hid_done, y_done, y_free = sem("gu_done"), sem("tanh_done"), sem("hid_done"), sem("y_done"), sem("y_free")
        setup, waits_passed = sem("setup"), sem("waits_passed")

        SETUP = 3
        block = ctx.enter_context(nc.Block())

        def both(engine, body):
            with engine.Fori(0, groups // 2 - 1) as i:
                body(i * 2, 0, True)
                body(i * 2 + 1, 1, True)
            body(groups - 2, 0, True)
            body(groups - 1, 1, False)

        def wait(engine, semaphore, value):
            engine.wait_ge(semaphore, value)
            engine.sem_inc(waits_passed, 1)

        @block.sync
        def _(sp):
            for count in (x_stored,):
                sp.sem_inc(count, 1)
            for dst, src in ((wr, gate_w), (ident, consts["ident"]), (tri, consts["tri"]), (rev, consts["rev"]),
                             (wg, gate_proj), (wu, up_proj), (wd, down_proj)):
                sp.dma_start(dst[:], src).then_inc(weights_in, 16)

            def load(g, s):
                sp.dma_start(acc[s][:], x_in[bass.ds(g, 1)].rearrange("a (j p) d -> p (a j) d", p=P)).then_inc(x_loaded[s], 16)

            def group(g, s, more):
                if more:
                    wait(sp, x_stored, 1 + g * 16)
                    load(g + 1, 1 - s)
                wait(sp, y_free, (g + 1) * EXPERTS + BUFFERS)
                sp.dma_start(x_out[bass.ds(g, 1)].rearrange("a (j p) d -> p (a j) d", p=P), acc[s][:]).then_inc(x_stored, 16)
                wait(sp, x_stored, 1 + g * 16 + 16)

            load(0, 0)
            both(sp, group)

        @block.gpsimd
        def _(pool):
            pool.memset(negh[:], -0.5).then_inc(setup, 1)
            pool.memset(ones[:], 1.0).then_inc(setup, 1)
            pool.memset(carry[:], 0.0).then_inc(setup, 1)
            pool.wait_ge(setup, SETUP)

            def rsqrt(g):
                wait(pool, stats_done, g + 1)
                nc.gpsimd.tensor_scalar(vareps[:], mv[:, :, 1], LN_EPS, None, ALU.add)
                pool.drain()
                nc.gpsimd.tensor_tensor(rstd[:], vareps[:], negh[:], ALU.pow).then_inc(rstd_done, 1)

            def group(g, s, more):
                if more:
                    rsqrt(g + 1)

            rsqrt(0)
            both(pool, group)

        @block.scalar
        def _(act):
            def copy_xt(g, s):
                act.wait_ge(xt_psum, g + 1)
                nc.scalar.activation(xT[s][:], ps_t[:], ACT.Copy).then_inc(xt_done, 1)

            def exp_logits(g):
                act.wait_ge(lsub_done, g + 1)
                nc.scalar.activation(prob[:], lsub[:], ACT.Exp).then_inc(exp_done, 1)

            def group(g, s, more):
                for u in range(units):
                    act.wait_ge(gu_done, g * units + (u + 1))
                    nc.scalar.activation(th[u % 2][:], ps_g[u % 2][:], ACT.Tanh, scale=0.5).then_inc(tanh_done, 1)
                    if more and u == 7:
                        copy_xt(g + 1, 1 - s)
                    if more and u == 11:
                        exp_logits(g + 1)

            copy_xt(0, 0)
            exp_logits(0)
            both(act, group)

        @block.tensor
        def _(pe):
            def transposes(g):
                pe.wait_ge(xn_done, g + 1)
                for j in range(tiles):
                    last = nc.tensor.transpose(ps_t[:, j * P:(j + 1) * P], xn[:, j, :], ident[:])
                last.then_inc(xt_psum, 1)

            def router(g, s):
                pe.wait_ge(xt_done, g + 1)
                for j in range(tiles):
                    last = nc.tensor.matmul(logits[:, j, :], xT[s][:, j * P:(j + 1) * P], wr[:], start=True, stop=True)
                last.then_inc(logits_done, 1)

            def ranks(g):
                pe.wait_ge(chosen_done, g + 1)
                for j in range(tiles):
                    for i in range(j):
                        nc.tensor.matmul(counts[:, j], ones[:], chosen[:, i], start=(i == 0), stop=False)
                    nc.tensor.matmul(counts[:, j], tri[:], chosen[:, j], start=(j == 0), stop=True)
                for i in range(tiles):
                    last = nc.tensor.matmul(total, ones[:], chosen[:, i], start=(i == 0), stop=(i == tiles - 1))
                last.then_inc(ranks_done, 1)

            def gate_up(g, s, u):
                e, k = u // 2, u % 2
                pe.wait_ge(hid_done, g * units + (u + 1))
                nc.tensor.matmul(ps_g[k][:], wg[:, e, k * P:(k + 1) * P], xT[s][:], start=True, stop=True)
                nc.tensor.matmul(ps_u[k][:], wu[:, e, k * P:(k + 1) * P], xT[s][:], start=True, stop=True).then_inc(gu_done, 1)

            def down(g, e):
                pe.wait_ge(hid_done, g * units + 2 * (e + 1) + BUFFERS)
                pe.wait_ge(y_free, g * EXPERTS + (e + 1))
                for j in range(tiles):
                    for k in range(2):
                        last = nc.tensor.matmul(ps_y[e % 2][:, j], hid[e % 2][k][:, j * P:(j + 1) * P], wd[:, e, k],
                                                start=(k == 0), stop=(k == 1))
                last.then_inc(y_done, 1)

            def group(g, s, more):
                for e in range(EXPERTS):
                    gate_up(g, s, 2 * e)
                    gate_up(g, s, 2 * e + 1)
                    if e >= 1:
                        down(g, e - 1)
                    if more and e == 3:
                        transposes(g + 1)
                    if more and e == 4:
                        router(g + 1, 1 - s)
                down(g, EXPERTS - 1)
                if more:
                    ranks(g + 1)

            pe.wait_ge(weights_in, 7 * 16)
            pe.wait_ge(setup, SETUP)
            transposes(0)
            router(0, 0)
            ranks(0)
            both(pe, group)

        @block.vector
        def _(dve):
            def statistics(g, s):
                dve.wait_ge(x_loaded[s], (g - s) * 8 + 16)
                for j in range(tiles):
                    nc.vector.bn_stats(stats[:, j], acc[s][:, j])
                dve.drain()
                for j in range(tiles):
                    last = nc.vector.bn_aggr(mv[:, j], stats[:, j])
                last.then_inc(stats_done, 1)

            def normalize(g, s):
                dve.wait_ge(rstd_done, g + 1)
                for j in range(tiles):
                    last = nc.vector.tensor_scalar(xn[:, j], acc[s][:, j], mv[:, j, 0:1], rstd[:, j:j + 1], ALU.subtract, ALU.mult)
                last.then_inc(xn_done, 1)

            def row(t):
                return t.unsqueeze(2).broadcast_to([P, tiles, EXPERTS])

            def shift_logits(g):
                dve.wait_ge(logits_done, g + 1)
                nc.vector.reduce_max(lmax[:], logits, AX.X)
                dve.drain()
                nc.vector.tensor_tensor(lsub[:], logits, row(lmax[:]), ALU.subtract).then_inc(lsub_done, 1)

            def choose(k, p):
                nc.vector.reduce_max(top[:, k], p[:], AX.X)
                dve.drain()
                nc.vector.tensor_tensor(eq[:], p[:], row(top[:, k]), ALU.is_equal)
                dve.drain()
                nc.vector.tensor_tensor(eq[:], eq[:], rev[:], ALU.mult)
                dve.drain()
                nc.vector.reduce_max(pick[:], eq[:], AX.X)
                dve.drain()
                return nc.vector.tensor_tensor(chosen[:, :, k], eq[:], row(pick[:]), ALU.is_equal)

            def choose_experts(g):
                dve.wait_ge(exp_done, g + 1)
                nc.vector.reduce_sum(psum_[:], prob[:], AX.X)
                dve.drain()
                nc.vector.reciprocal(pinv[:], psum_[:])
                dve.drain()
                nc.vector.tensor_tensor(prob[:], prob[:], row(pinv[:]), ALU.mult)
                dve.drain()
                choose(0, prob)
                dve.drain()
                nc.vector.scalar_tensor_tensor(probs2[:], chosen[:, :, 0], -2.0, prob[:], ALU.mult, ALU.add)
                dve.drain()
                choose(1, probs2).then_inc(chosen_done, 1)
                nc.vector.tensor_tensor(wsum[:], top[:, 0], top[:, 1], ALU.add)
                dve.drain()
                nc.vector.tensor_scalar(wsum[:], wsum[:], 1e-9, None, ALU.add)
                dve.drain()
                nc.vector.reciprocal(winv[:], wsum[:])
                dve.drain()
                for k in range(2):
                    nc.vector.tensor_tensor(top[:, k], top[:, k], winv[:], ALU.mult)
                dve.drain()

            def capacities(g, s):
                dve.wait_ge(ranks_done, g + 1)
                nc.vector.tensor_tensor(rank[:], counts, carry[:].unsqueeze(1).broadcast_to([P, tiles, 2, EXPERTS]), ALU.add)
                dve.drain()
                nc.vector.tensor_tensor(carry[:], carry[:], total, ALU.add)
                nc.vector.tensor_scalar(rank[:], rank[:], float(CAPACITY), None, ALU.is_le)
                dve.drain()
                nc.vector.tensor_tensor(rank[:], rank[:], chosen[:], ALU.mult)
                dve.drain()
                for k in range(2):
                    nc.vector.tensor_tensor(comb2[:, :, k], rank[:, :, k], row(top[:, k]), ALU.mult)
                dve.drain()
                nc.vector.tensor_tensor(comb[s][:], comb2[:, :, 0], comb2[:, :, 1], ALU.add)
                dve.drain()
                nc.vector.tensor_scalar(comb[s][:], comb[s][:], 0.5, None, ALU.mult)
                dve.drain()

            def hidden(g, u):
                e, k = u // 2, u % 2
                dve.wait_ge(tanh_done, g * units + (u + 1))
                nc.vector.scalar_tensor_tensor(gated[k][:], th[k][:], 1.0, ps_g[k][:], ALU.add, ALU.mult)
                dve.drain()
                nc.vector.tensor_tensor(hid[e % 2][k][:], gated[k][:], ps_u[k][:], ALU.mult).then_inc(hid_done, 1)

            def combine(g, s, e):
                dve.wait_ge(y_done, g * EXPERTS + (e + 1))
                for j in range(tiles):
                    last = nc.vector.scalar_tensor_tensor(acc[s][:, j], ps_y[e % 2][:, j], comb[s][:, j, e:e + 1], acc[s][:, j],
                                                          ALU.mult, ALU.add)
                last.then_inc(y_free, 1)

            def group(g, s, more):
                capacities(g, s)
                for e in range(EXPERTS):
                    if e >= 2:
                        combine(g, s, e - 2)
                    hidden(g, 2 * e)
                    hidden(g, 2 * e + 1)
                    if more and e == 1:
                        statistics(g + 1, 1 - s)
                    if more and e == 2:
                        normalize(g + 1, 1 - s)
                    if more and e == 5:
                        shift_logits(g + 1)
                    if more and e == 6:
                        choose_experts(g + 1)
                combine(g, s, EXPERTS - 2)
                dve.drain()
                combine(g, s, EXPERTS - 1)

            nc.vector.engine_nop().then_inc(hid_done, BUFFERS)
            nc.vector.engine_nop().then_inc(y_free, BUFFERS)
            dve.wait_ge(weights_in, 7 * 16)
            dve.wait_ge(setup, SETUP)
            statistics(0, 0)
            normalize(0, 0)
            shift_logits(0)
            choose_experts(0)
            both(dve, group)


def causal_attention_stage(nc, x_in, x_out, w_qkv, b_qkv, w_o, b_o, consts):
    ctx = ExitStack()
    with ctx:
        sb = lambda n, shape, dt=F32: ctx.enter_context(nc.sbuf_tensor(f"att_{n}", shape, dt))
        ps = lambda n, shape: ctx.enter_context(nc.psum_tensor(f"att_{n}", shape, F32))
        sem = lambda n: ctx.enter_context(nc.semaphore(f"att_{n}"))

        wqkv = sb("wqkv", [P, 3 * D])
        wo = sb("wo", [P, D])
        bias = sb("bias", [P, 3 * D])
        bo = sb("bo", [P, D])
        ident = sb("ident", [P, P])
        identb = sb("identb", [P, P], BF16)
        mask_f = sb("mask_f", [P, 2, P])
        mask = sb("mask", [P, 2, P], BF16)
        cs = sb("cs", [P, TILES, 2, ROT])
        negh = sb("negh", [P, TILES])
        xb = sb("xb", [P, TILES, D])
        stats = sb("stats", [P, TILES, 6])
        mv = sb("mv", [P, TILES, 2])
        vareps = sb("vareps", [P, TILES])
        rstd = sb("rstd", [P, TILES])
        xn = sb("xn", [P, TILES, D])
        xT = sb("xT", [P, SEQ])
        qkv = sb("qkv", [P, TILES, 3 * D])
        JH = TILES * HEADS
        turned = [sb(f"turned{k}", [P, JH, ROT]) for k in range(2)]
        turned2 = [sb(f"turned2{k}", [P, JH, ROT]) for k in range(2)]
        parts = [sb(f"parts{k}", [P, JH, 3, ROT], BF16) for k in range(2)]
        stack = [sb(f"stack{k}", [P, JH, 32], BF16) for k in range(2)]
        v1 = sb("v1", [P, JH, 32])
        kT = [[sb(f"kT{s}{h}", [P, SEQ], BF16) for h in range(QUAD)] for s in range(2)]
        q1T = [sb(f"q1T{s}", [P, SEQ], BF16) for s in range(2)]
        q2T = [sb(f"q2T{s}", [P, SEQ], BF16) for s in range(2)]
        mx = sb("mx", [P, 2, TILES, QUAD])
        nm = sb("nm", [P, TILES, QUAD])
        nm2 = sb("nm2", [P, TILES, QUAD])
        prob = [sb(f"prob{s}", [P, 2, 512]) for s in range(4)]
        oT = sb("oT", [P, 2, 512])
        rden = sb("rden", [P, 4, QUAD])
        y = sb("y", [P, TILES, D])
        yT = sb("yT", [P, SEQ])

        ps1 = [ps(f"ps1{s}", [P, 512]) for s in range(2)]
        ps2 = [ps(f"ps2{s}", [P, 2, 512]) for s in range(2)]
        pso = ps("pso", [P, 512])
        psm = ps("psm", [P, 512])
        psm_b = psm[:].bitcast(BF16)
        qkv_banks = [ps1[0][:], ps1[1][:], ps2[1][:, 0], ps2[1][:, 1]]

        weights_in, setup, casts, waits_passed = sem("weights_in"), sem("setup"), sem("casts"), sem("waits_passed")
        x_loaded, x_stored = sem("x_loaded"), sem("x_stored")
        stats_done, rstd_done, xn_done, xt_psum, xt_done = sem("stats_done"), sem("rstd_done"), sem("xn_done"), sem("xt_psum"), sem("xt_done")
        qkv_psum, qkv_done = sem("qkv_psum"), sem("qkv_done")
        q_stacked, k_stacked, v_placed = sem("q_stacked"), sem("k_stacked"), sem("v_placed")
        misc_full, misc_free = sem("misc_full"), sem("misc_free")
        s1_done, max_done, quad_max, max_stacked = sem("s1_done"), sem("max_done"), sem("quad_max"), sem("max_stacked")
        s2_done, exp_done, pv_done, o_copied = sem("s2_done"), sem("exp_done"), sem("pv_done"), sem("o_copied")
        y_done, yt_psum, yt_done, out_psum, out_done = sem("y_done"), sem("yt_psum"), sem("yt_done"), sem("out_psum"), sem("out_done")

        QUADS = HEADS // QUAD
        MAX_STEPS = [(j, c) for j in range(TILES) for c in range(1 + (j >= 4))]
        EXP_STEPS = [(c, i) for c in range(2) for i in range(4 * c + 4)]
        STEPS = len(MAX_STEPS)
        assert len(EXP_STEPS) == STEPS
        MISC = 5
        misc_order = {("k", 0): 0, ("q1", 0): 1, ("q2", 0): 2}
        for t in range(QUADS):
            for use in ([("k", t + 1), ("q1", t + 1)] if t + 1 < QUADS else []) + [("o", t, 0)] + ([("q2", t + 1)] if t + 1 < QUADS else []) + [("o", t, 1)]:
                misc_order[use] = len(misc_order)
        assert len(misc_order) == QUADS * MISC

        def misc(b, *use):
            return b * (QUADS * MISC) + misc_order[use]

        SETUP = 4
        block = ctx.enter_context(nc.Block())

        def wait(engine, semaphore, value):
            engine.wait_ge(semaphore, value)
            engine.sem_inc(waits_passed, 1)

        @block.sync
        def _(sp):
            for count in (misc_free, o_copied):
                sp.sem_inc(count, 1)
            for dst, src in ((wqkv[:], w_qkv), (wo[:], w_o), (bias[:], b_qkv.broadcast_to([P, 3 * D])), (bo[:], b_o.broadcast_to([P, D])),
                             (ident[:], consts["ident"]), (mask_f[:], consts["mask"]), (cs[:], consts["cs"])):
                sp.dma_start(dst, src).then_inc(weights_in, 16)
            with sp.Fori(0, BATCH) as b:
                sp.dma_start(xb[:], x_in[bass.ds(b, 1)].rearrange("a (j p) d -> p (a j) d", p=P)).then_inc(x_loaded, 16)
                wait(sp, out_done, b + 1)
                sp.dma_start(x_out[bass.ds(b, 1)].rearrange("a (j p) d -> p (a j) d", p=P), xb[:]).then_inc(x_stored, 16)
                wait(sp, x_stored, b * 16 + 16)

        def rotate(engine, k):
            even = qkv[:, :, 128 * k:128 * k + 64].rearrange("p j (h r) -> p j h r", r=ROT)
            odd = qkv[:, :, 128 * k + 64:128 * k + 128].rearrange("p j (h r) -> p j h r", r=ROT)
            cos = cs[:, :, 0].unsqueeze(2).broadcast_to([P, TILES, HEADS, ROT])
            sin = cs[:, :, 1].unsqueeze(2).broadcast_to([P, TILES, HEADS, ROT])
            a, c = turned[k], turned2[k]
            shaped = lambda t: t[:].rearrange("p (j h) r -> p j h r", h=HEADS)
            engine.tensor_tensor(shaped(a), even, cos, ALU.mult)
            engine.tensor_tensor(shaped(c), odd, sin, ALU.mult)
            engine.drain()
            engine.tensor_tensor(a[:], a[:], c[:], ALU.subtract)
            engine.drain()
            for n in range(3):
                engine.tensor_copy(parts[k][:, :, n], a[:])
                engine.drain()
                if n < 2:
                    engine.tensor_tensor(a[:], a[:], parts[k][:, :, n], ALU.subtract)
                    engine.drain()

        @block.gpsimd
        def _(pool):
            pool.memset(negh[:], -0.5).then_inc(setup, 1)
            pool.memset(v1[:], 0.0).then_inc(setup, 1)
            pool.memset(stack[0][:], 0.0)
            for s in range(2):
                for h in range(QUAD):
                    pool.memset(kT[s][h][:], 0.0)
            pool.drain()
            pool.memset(stack[1][:], 0.0)
            pool.drain()
            pool.wait_ge(setup, 2)
            pool.memset(v1[:, :, HS:HS + 1], 1.0).then_inc(setup, 1)
            pool.memset(stack[1][:, :, 24:27], 1.0).then_inc(setup, 1)
            pool.wait_ge(setup, SETUP)
            with pool.Fori(0, BATCH) as b:
                wait(pool, stats_done, b + 1)
                nc.gpsimd.tensor_scalar(vareps[:], mv[:, :, 1], LN_EPS, None, ALU.add)
                pool.drain()
                nc.gpsimd.tensor_tensor(rstd[:], vareps[:], negh[:], ALU.pow).then_inc(rstd_done, 1)
                wait(pool, qkv_done, (b + 1) * TILES)
                rotate(nc.gpsimd, 1)
                nc.gpsimd.tensor_copy(stack[1][:, :, 0:12], parts[1][:].rearrange("p a n r -> p a (n r)"))
                nc.gpsimd.tensor_copy(stack[1][:, :, 12:20], parts[1][:, :, 0:2].rearrange("p a n r -> p a (n r)"))
                nc.gpsimd.tensor_copy(stack[1][:, :, 20:24], parts[1][:, :, 0])
                pool.drain()
                pool.engine_nop().then_inc(k_stacked, 1)
                for t in range(QUADS):
                    wait(pool, quad_max, b * QUADS + (t + 1))
                    place = lambda n: stack[0][:].rearrange("p (j h) r -> p j h r", h=HEADS)[:, :, QUAD * t:QUAD * (t + 1), 24 + n]
                    source = nm
                    for n in range(3):
                        nc.gpsimd.tensor_copy(place(n), source[:])
                        pool.drain()
                        if n < 2:
                            nc.gpsimd.tensor_tensor(nm2[:], source[:], place(n), ALU.subtract)
                            pool.drain()
                            source = nm2
                    pool.engine_nop().then_inc(max_stacked, 1)

        @block.scalar
        def _(act):
            act.wait_ge(weights_in, 7 * 16)
            nc.scalar.activation(identb[:], ident[:], ACT.Copy).then_inc(casts, 1)
            nc.scalar.activation(mask[:], mask_f[:], ACT.Copy).then_inc(casts, 1)
            act.wait_ge(setup, SETUP)

            def from_misc(b, dst, *use):
                act.wait_ge(misc_full, misc(b, *use) + 1)
                nc.scalar.activation(dst[:], psm_b, ACT.Copy).then_inc(misc_free, 1)

            def keys_from_misc(b, t):
                act.wait_ge(misc_full, misc(b, "k", t) + 1)
                for h in range(QUAD):
                    rows = slice(32 * h, 32 * h + 32)
                    last = nc.scalar.activation(kT[t % 2][h][rows, :], psm_b[rows, :], ACT.Copy)
                last.then_inc(misc_free, 1)

            with act.Fori(0, BATCH) as b:
                act.wait_ge(xt_psum, b + 1)
                nc.scalar.activation(xT[:], ps2[0][:].rearrange("p a n -> p (a n)"), ACT.Copy).then_inc(xt_done, 1)
                act.wait_ge(qkv_done, (b + 1) * TILES)
                nc.scalar.activation(v1[:].rearrange("p (j h) r -> p j h r", h=HEADS)[:, :, :, 0:HS],
                                     qkv[:, :, 2 * D:3 * D].rearrange("p j (h r) -> p j h r", r=HS), ACT.Copy).then_inc(v_placed, 1)
                keys_from_misc(b, 0)
                from_misc(b, q1T[0], "q1", 0)
                from_misc(b, q2T[0], "q2", 0)
                for t in range(QUADS):
                    if t + 1 < QUADS:
                        keys_from_misc(b, t + 1)
                        from_misc(b, q1T[(t + 1) % 2], "q1", t + 1)
                    for n, (c, i) in enumerate(EXP_STEPS):
                        size = 512 - max(0, i - 4 * c) * P
                        for pair in range(2):
                            v = (b * QUADS + t) * (2 * STEPS) + (2 * n + pair)
                            act.wait_ge(s2_done, v + 1)
                            nc.scalar.activation(prob[(2 * n + pair) % 4][:, :, 0:size], ps2[pair][:, :, 0:size], ACT.Exp,
                                                 scale=SCORE_SCALE).then_inc(exp_done, 1)
                        if n in (4, STEPS - 1):
                            act.wait_ge(pv_done, (b * QUADS + t) * STEPS + (4 if n == 4 else STEPS))
                            nc.scalar.activation(oT[:, int(n > 4)], pso[:], ACT.Copy).then_inc(o_copied, 1)
                    if t + 1 < QUADS:
                        from_misc(b, q2T[(t + 1) % 2], "q2", t + 1)
                act.wait_ge(yt_psum, b + 1)
                nc.scalar.activation(yT[:], ps2[0][:].rearrange("p a n -> p (a n)"), ACT.Copy).then_inc(yt_done, 1)

        @block.tensor
        def _(pe):
            def to_misc(b, k, *use):
                t = use[1]
                pe.wait_ge(misc_free, 1 + misc(b, *use))
                for j in range(TILES):
                    rows = stack[k][:].rearrange("p (j h) r -> p j (h r)", h=HEADS)[:, j, P * t:P * (t + 1)]
                    last = nc.tensor.transpose(psm_b[:, j * P:(j + 1) * P], rows, identb[:])
                last.then_inc(misc_full, 1)

            def max_step(b, t, n, heads=range(QUAD)):
                j, c = MAX_STEPS[n]
                size = min(512, P * (j + 1) - 512 * c)
                for h in heads:
                    u = (b * QUADS + t) * (STEPS * QUAD) + (n * QUAD + h)
                    out = ps1[(n * QUAD + h) % 2]
                    diagonal = P * (j + 1) == 512 * c + size
                    pe.wait_ge(max_done, u + 1)
                    last = nc.tensor.matmul(out[:, 0:size], q1T[t % 2][:, j * P:(j + 1) * P], kT[t % 2][h][:, 512 * c:512 * c + size],
                                            start=True, stop=not diagonal)
                    if diagonal:
                        last = nc.tensor.matmul(out[:, size - P:size], identb[:], mask[:, 0], start=False, stop=True)
                    last.then_inc(s1_done, 1)

            def exp_step(b, t, n, pair):
                c, i = EXP_STEPS[n]
                first = max(512 * c, P * i)
                size = 512 * (c + 1) - first
                if True:
                    v = (b * QUADS + t) * (2 * STEPS) + (2 * n + pair)
                    pe.wait_ge(exp_done, v + 1)
                    for h in range(2):
                        last = nc.tensor.matmul(ps2[pair][:, h, 0:size], kT[t % 2][2 * pair + h][:, i * P:(i + 1) * P], q2T[t % 2][:, first:first + size],
                                                start=True, stop=(i < 4 * c))
                        if i >= 4 * c:
                            last = nc.tensor.matmul(ps2[pair][:, h, 0:P], identb[:], mask[:, 1], start=False, stop=True)
                    last.then_inc(s2_done, 1)

            def value_step(b, t, n):
                c, i = EXP_STEPS[n]
                first = max(0, P * i - 512 * c)
                pe.wait_ge(exp_done, (b * QUADS + t) * (2 * STEPS) + 2 * (n + 1) + BUFFERS)
                if i == 0:
                    pe.wait_ge(o_copied, 1 + (b * QUADS + t) * 2 + c)
                for h in range(QUAD):
                    last = nc.tensor.matmul(pso[32 * h:32 * h + 32, first:512], v1[:, i * HEADS + QUAD * t + h, :],
                                            prob[(2 * n + h // 2) % 4][:, h % 2, 0:512 - first], start=(i == 0), stop=(i == 4 * c + 3))
                last.then_inc(pv_done, 1)

            def transpose_output(b, t, c):
                pe.wait_ge(misc_free, 1 + misc(b, "o", t, c))
                pe.wait_ge(o_copied, 1 + (b * QUADS + t) * 2 + (c + 1))
                for j in range(4):
                    last = nc.tensor.transpose(psm[:, j * P:(j + 1) * P], oT[:, c, j * P:(j + 1) * P], ident[:])
                last.then_inc(misc_full, 1)

            pe.wait_ge(weights_in, 7 * 16)
            pe.wait_ge(casts, 2)
            pe.wait_ge(setup, SETUP)
            with pe.Fori(0, BATCH) as b:
                pe.wait_ge(xn_done, b + 1)
                for j in range(TILES):
                    last = nc.tensor.transpose(ps2[0][:, j // 4, (j % 4) * P:(j % 4 + 1) * P], xn[:, j], ident[:])
                last.then_inc(xt_psum, 1)
                pe.wait_ge(xt_done, b + 1)
                for j in range(TILES):
                    if j >= 4:
                        pe.wait_ge(qkv_done, b * TILES + (j - 3))
                    nc.tensor.matmul(qkv_banks[j % 4][:, 0:3 * D], xT[:, j * P:(j + 1) * P], wqkv[:], start=True, stop=True).then_inc(qkv_psum, 1)
                pe.wait_ge(k_stacked, b + 1)
                to_misc(b, 1, "k", 0)
                pe.wait_ge(q_stacked, b + 1)
                to_misc(b, 0, "q1", 0)
                pe.wait_ge(misc_free, 1 + misc(b, "q1", 0) + 1)
                for n in range(STEPS):
                    max_step(b, 0, n)
                pe.wait_ge(max_stacked, b * QUADS + 1)
                to_misc(b, 0, "q2", 0)
                pe.wait_ge(v_placed, b + 1)
                for t in range(QUADS):
                    pe.wait_ge(misc_free, 1 + misc(b, "q2", t) + 1)
                    if t + 1 < QUADS:
                        to_misc(b, 1, "k", t + 1)
                        to_misc(b, 0, "q1", t + 1)
                    for n in range(STEPS):
                        more = t + 1 < QUADS
                        exp_step(b, t, n, 0)
                        if more:
                            if n == 0:
                                pe.wait_ge(misc_free, 1 + misc(b, "q1", t + 1) + 1)
                            max_step(b, t + 1, n, [0])
                        exp_step(b, t, n, 1)
                        if more:
                            max_step(b, t + 1, n, [1])
                        if n >= 1:
                            value_step(b, t, n - 1)
                        if n == 6:
                            transpose_output(b, t, 0)
                        if more:
                            max_step(b, t + 1, n, [2, 3])
                    value_step(b, t, STEPS - 1)
                    if t + 1 < QUADS:
                        pe.wait_ge(max_stacked, b * QUADS + (t + 2))
                        to_misc(b, 0, "q2", t + 1)
                    transpose_output(b, t, 1)
                pe.wait_ge(y_done, b + 1)
                for j in range(TILES):
                    last = nc.tensor.transpose(ps2[0][:, j // 4, (j % 4) * P:(j % 4 + 1) * P], y[:, j], ident[:])
                last.then_inc(yt_psum, 1)
                pe.wait_ge(yt_done, b + 1)
                for j in range(TILES):
                    last = nc.tensor.matmul(ps2[1][:, j // 4, (j % 4) * P:(j % 4 + 1) * P], yT[:, j * P:(j + 1) * P], wo[:], start=True, stop=True)
                last.then_inc(out_psum, 1)

        @block.vector
        def _(dve):
            def maxima(b, t, n):
                j, c = MAX_STEPS[n]
                size = min(512, P * (j + 1) - 512 * c)
                for h in range(QUAD):
                    dve.wait_ge(s1_done, (b * QUADS + t) * (STEPS * QUAD) + (n * QUAD + h + 1))
                    nc.vector.reduce_max(mx[:, c, j, h:h + 1], ps1[(n * QUAD + h) % 2][:, 0:size], AX.X).then_inc(max_done, 1)

            def negate_maxima(b, t):
                dve.drain()
                nc.vector.tensor_tensor(mx[:, 0, 4:8], mx[:, 0, 4:8], mx[:, 1, 4:8], ALU.max)
                if t >= 1:
                    wait(dve, max_stacked, b * QUADS + t)
                dve.drain()
                nc.vector.tensor_scalar(nm[:], mx[:, 0], -1.0, None, ALU.mult).then_inc(quad_max, 1)

            def divide(b, t, c):
                heads = psm[:].rearrange("p (j h r) -> p j h r", h=QUAD, r=32)
                dve.wait_ge(misc_full, misc(b, "o", t, c) + 1)
                nc.vector.reciprocal(rden[:], heads[:, :, :, HS])
                dve.drain()
                nc.vector.tensor_tensor(y[:, 4 * c:4 * c + 4, 32 * t:32 * t + 32].rearrange("p j (h r) -> p j h r", r=HS), heads[:, :, :, 0:HS],
                                        rden[:].unsqueeze(3).broadcast_to([P, 4, QUAD, HS]), ALU.mult).then_inc(misc_free, 1)

            dve.wait_ge(weights_in, 7 * 16)
            dve.wait_ge(setup, SETUP)
            nc.vector.engine_nop().then_inc(exp_done, BUFFERS)
            nc.vector.engine_nop().then_inc(max_done, BUFFERS)
            with dve.Fori(0, BATCH) as b:
                dve.wait_ge(x_loaded, b * 16 + 16)
                for j in range(TILES):
                    nc.vector.bn_stats(stats[:, j], xb[:, j])
                dve.drain()
                for j in range(TILES):
                    last = nc.vector.bn_aggr(mv[:, j], stats[:, j])
                last.then_inc(stats_done, 1)
                dve.wait_ge(rstd_done, b + 1)
                for j in range(TILES):
                    last = nc.vector.tensor_scalar(xn[:, j], xb[:, j], mv[:, j, 0:1], rstd[:, j:j + 1], ALU.subtract, ALU.mult)
                last.then_inc(xn_done, 1)
                dve.drain()
                nc.vector.tensor_tensor(xb[:], xb[:], bo[:].unsqueeze(1).broadcast_to([P, TILES, D]), ALU.add)
                for j in range(TILES):
                    dve.wait_ge(qkv_psum, b * TILES + (j + 1))
                    nc.vector.tensor_tensor(qkv[:, j], qkv_banks[j % 4][:, 0:3 * D], bias[:], ALU.add).then_inc(qkv_done, 1)
                dve.drain()
                nc.vector.memset(stack[0][:, :, 24:27], 0.0)
                rotate(nc.vector, 0)
                nc.vector.tensor_copy(stack[0][:, :, 0:12].rearrange("p a (n r) -> p a n r", r=ROT), parts[0][:, :, 0].unsqueeze(2).broadcast_to([P, JH, 3, ROT]))
                nc.vector.tensor_copy(stack[0][:, :, 12:20].rearrange("p a (n r) -> p a n r", r=ROT), parts[0][:, :, 1].unsqueeze(2).broadcast_to([P, JH, 2, ROT]))
                nc.vector.tensor_copy(stack[0][:, :, 20:24], parts[0][:, :, 2]).then_inc(q_stacked, 1)
                for n in range(STEPS):
                    maxima(b, 0, n)
                negate_maxima(b, 0)
                for t in range(QUADS):
                    for n in range(STEPS):
                        if t + 1 < QUADS:
                            maxima(b, t + 1, n)
                        if n == 6:
                            divide(b, t, 0)
                    if t + 1 < QUADS:
                        negate_maxima(b, t + 1)
                    divide(b, t, 1)
                dve.drain()
                nc.vector.engine_nop().then_inc(y_done, 1)
                dve.wait_ge(out_psum, b + 1)
                nc.vector.tensor_tensor(xb[:], xb[:], ps2[1][:].rearrange("p a (j d) -> p (a j) d", d=D), ALU.add).then_inc(out_done, 1)


def block(nc, x, out, fast_qkv, fast_norm, fast_lr_bias, fast_start, att_qkv, att_bias, att_out, att_out_bias,
          router, gate_proj, up_proj, down_proj, ident, block_ones, eye, tri, rev, mask, cs):
    consts = {"ident": ident, "block_ones": block_ones, "eye": eye, "tri": tri, "rev": rev, "mask": mask, "cs": cs}
    scratch = lambda n, shape: nc.dram_tensor(n, shape, F32, kind="Internal").ap()
    tok = scratch("tok", [CHUNKS, P, 2 * BATCH, 3 * D])
    turned = scratch("turned", [CHUNKS, P, BATCH, 3, CHUNK])
    x1, x2, x3 = (scratch(f"x{n}", [BATCH, SEQ, D]) for n in (1, 2, 3))
    groups = lambda t: t.rearrange("b (g n) d -> (b g) n d", n=GROUP)
    fast_weight_inputs(nc, x, tok, turned, fast_qkv, fast_lr_bias, fast_norm, consts)
    fast_weight_stage(nc, x, x1, tok, turned, fast_start, consts)
    expert_stage(nc, "moe1", groups(x1), groups(x2), router, gate_proj, up_proj, down_proj, consts)
    causal_attention_stage(nc, x2, x3, att_qkv, att_bias, att_out, att_out_bias, consts)
    expert_stage(nc, "moe2", groups(x3), groups(out), router, gate_proj, up_proj, down_proj, consts)


def layouts(i):
    import numpy as np

    a = {k: np.asarray(v) for k, v in i.items()}
    c = lambda t: np.ascontiguousarray(t, dtype=t.dtype)

    def rope_halves(t):
        t = t.reshape(HEADS, HS, -1)
        return np.concatenate([t[:, ::2].reshape(HEADS * ROT, -1), t[:, 1::2].reshape(HEADS * ROT, -1)])

    def as_y(t):
        t = t.reshape(2, 2, FW_HID, FW_D).transpose(1, 2, 0, 3).reshape(P, 1, 2 * FW_D)
        return np.tile(t, (1, BATCH, 1)).reshape(P, -1)

    def as_x(t):
        return np.tile(t.reshape(P, 1, FW_HID), (1, BATCH, 1)).reshape(P, -1)

    return {
        "x": c(a["L0_attn_a_hidden_states"]),
        "fast_qkv": c(np.concatenate([a["L0_attn_a_qkv_w"], a["L0_attn_a_lr_proj_w"]]).T),
        "fast_norm": c(np.concatenate([a["L0_attn_a_q_norm_w"], a["L0_attn_a_k_norm_w"]])[None]),
        "fast_lr_bias": c(a["L0_attn_a_lr_proj_b"][None]),
        "fast_start": c(np.stack([as_y(a["L0_attn_a_w0"]), as_y(a["L0_attn_a_w2"]), as_x(a["L0_attn_a_w1"])], 1)),
        "att_qkv": c(np.concatenate([rope_halves(a["L0_attn_b_Wq"]), rope_halves(a["L0_attn_b_Wk"]), a["L0_attn_b_Wv"]]).T),
        "att_bias": c(np.concatenate([rope_halves(a["L0_attn_b_bq"])[:, 0], rope_halves(a["L0_attn_b_bk"])[:, 0], a["L0_attn_b_bv"]])[None]),
        "att_out": c(a["L0_attn_b_Wo"].T),
        "att_out_bias": c(a["L0_attn_b_bo"][None]),
        "router": c(a["L0_ffn_gate_w"].T),
        "gate_proj": c(a["L0_ffn_gate_proj_w"].transpose(2, 0, 1)),
        "up_proj": c(a["L0_ffn_up_proj_w"].transpose(2, 0, 1)),
        "down_proj": c(a["L0_ffn_down_proj_w"].reshape(EXPERTS, D, 2, P).transpose(3, 0, 2, 1)),
    }


def constants():
    import numpy as np

    f = np.float32
    row, col = np.arange(P)[:, None], np.arange(P)[None]
    block_ones = np.stack([row // FW_D == col // FW_D] + [row // FW_D == 2 * k + col // FW_HID for k in range(2)], 1)
    time, pair = np.arange(1, SEQ + 1, dtype=f)[:, None], np.arange(ROT, dtype=f)
    angle = (time * (f(1.0 / 10000.0) ** (f(2.0) * pair / f(HS))).astype(f)).astype(f)
    cs = np.stack([np.cos(angle), np.sin(angle)], 1).astype(f).reshape(TILES, P, 2, ROT).transpose(1, 0, 2, 3)
    return {
        "ident": np.eye(P, dtype=f),
        "block_ones": block_ones.astype(f),
        "eye": np.tile(np.eye(FW_D, dtype=f), (P // FW_D, 1)),
        "tri": (row <= col).astype(f),
        "rev": np.tile(np.arange(EXPERTS, 0, -1, dtype=f), (P, GROUP // P, 1)),
        "mask": (np.stack([col > row, row > col], 1) * f(MASKED)).astype(f),
        "cs": np.ascontiguousarray(cs),
    }


def kernel(**inputs):
    import concourse.bacc as bacc
    from concourse.bass_utils import run_bass_kernel_spmd as run

    nc = bacc.Bacc("TRN2", target_bir_lowering=False, num_devices=1)
    arrays = {**layouts(inputs), **constants()}
    aps = {n: nc.dram_tensor(f"in_{n}", t.shape, mybir.dt.from_np(t.dtype), kind="ExternalInput").ap() for n, t in arrays.items()}
    out = nc.dram_tensor("out", (BATCH, SEQ, D), F32, kind="ExternalOutput").ap()
    block(nc, out=out, **aps)
    r = run(nc, [{f"in_{n}": t for n, t in arrays.items()}], core_ids=[0])
    return r.results[0]["out"]
```

```python
import concourse.bass as bass
from concourse import mybir
import math
from contextlib import ExitStack

F32, F32R, BF16 = mybir.dt.float32, mybir.dt.float32r, mybir.dt.bfloat16
ALU = mybir.AluOpType
ACT = mybir.ActivationFunctionType
AX = mybir.AxisListType

P = 128
BATCH, SEQ, D = 4, 1024, 128
TOKENS = BATCH * SEQ
LN_EPS = 1e-5
EXPERTS = 8
CAPACITY = int(1.25 * TOKENS / EXPERTS)
GROUP = 512

BUFFERS = 2
TILES = SEQ // P
HEADS, HS = 16, 8
ROT = HS // 2
QUAD = 4
SCORE_SCALE = float(HS) ** -0.5
FW_HEADS, FW_D, FW_HID = 4, 32, 64
CHUNK = 256
CHUNKS = SEQ // CHUNK
BASE_LR_INV = math.log(math.expm1(0.001))
NEWTON = ((4.0848, -6.8946, 2.927), (3.9505, -6.3029, 2.6377), (3.7418, -5.5913, 2.3037),
          (2.8769, -3.1427, 1.2046), (2.8366, -3.0525, 1.2012))
MASKED = -1e30


def fast_weight_inputs(nc, x_in, tok_out, t_out, w_in, lr_bias, norm_w, consts, expert):
    ctx = ExitStack()
    with ctx:
        sb = lambda n, shape, dt=F32: ctx.enter_context(nc.sbuf_tensor(f"prep_{n}", shape, dt))
        ps = lambda n, shape: ctx.enter_context(nc.psum_tensor(f"prep_{n}", shape, F32))
        sem = lambda n: ctx.enter_context(nc.semaphore(f"prep_{n}"))
        W = 3 * D + 3 * FW_HEADS
        w = sb("w", [P, W])
        bias = sb("bias", [P, 3 * FW_HEADS])
        nw = sb("nw", [P, 2 * D])
        ident = sb("ident", [P, P])
        half = sb("half", [P, TILES * 2 * FW_HEADS])
        negh = sb("negh", [P, TILES * 2])
        xb = sb("xb", [P, TILES, D])
        stats = sb("stats", [P, TILES, 6])
        mv = sb("mv", [P, TILES, 2])
        vareps = sb("vareps", [P, TILES])
        rstd = sb("rstd", [P, TILES])
        xn = sb("xn", [P, TILES, D])
        xT = sb("xT", [P, SEQ])
        raw = sb("raw", [P, TILES, W])
        sq = sb("sq", [P, TILES, 2 * D])
        qk = sb("qk", [P, TILES, 2 * D])
        qkn = sb("qkn", [P, TILES, 2 * D])
        ms = sb("ms", [P, TILES * 2])
        mse = sb("mse", [P, TILES * 2])
        rms = sb("rms", [P, TILES * 2])
        hs2 = sb("hs2", [P, TILES * 2 * FW_HEADS])
        hn = sb("hn", [P, TILES * 2 * FW_HEADS])
        rhn = sb("rhn", [P, TILES * 2 * FW_HEADS])
        L = 3 * FW_HEADS
        z = sb("z", [P, TILES, L])
        za = sb("za", [P, TILES, L])
        u = sb("u", [P, TILES, L])
        y1 = sb("y1", [P, TILES, L])
        ln = sb("ln", [P, TILES, L])
        dd = sb("dd", [P, TILES, L])
        one = sb("one", [P, TILES, L])
        lr = sb("lr", [P, TILES, L])
        tok = sb("tok", [P, CHUNKS, 2, 3 * D])
        tT = sb("tT", [P, CHUNKS, 3, CHUNK])
        psT = [ps(f"psT{s}", [P, 2, 512]) for s in range(2)]
        psW = [ps(f"psW{s}", [P, 512]) for s in range(4)]

        weights_in, setup, waits_passed = sem("weights_in"), sem("setup"), sem("waits_passed")
        x_loaded, stored = sem("x_loaded"), sem("stored")
        stats_done, rstd_done, xn_done, xt_psum, xt_done = sem("stats_done"), sem("rstd_done"), sem("xn_done"), sem("xt_psum"), sem("xt_done")
        w_psum, raw_done = sem("w_psum"), sem("raw_done")
        squares, sums, powers = sem("squares"), sem("sums"), sem("powers")
        scaled, heads_done, z_done, u_done, y1_done, ln_done, lr_done, tok_done = (sem(n) for n in ("scaled", "heads_done", "z_done", "u_done", "y1_done", "ln_done", "lr_done", "tok_done"))
        t_psum, t_done = sem("t_psum"), sem("t_done")
        SETUP = 2
        block = ctx.enter_context(nc.Block())

        def wait(engine, semaphore, value):
            engine.wait_ge(semaphore, value)
            engine.sem_inc(waits_passed, 1)

        @block.sync
        def _(sp):
            for count in (stored, t_done):
                sp.sem_inc(count, 1)
            for dst, src in ((w[:], w_in), (bias[:], lr_bias.broadcast_to([P, L])), (nw[:], norm_w.broadcast_to([P, 2 * D])), (ident[:], consts["ident"])):
                sp.dma_start(dst, src).then_inc(weights_in, 16)
            for dst, src in expert["loads"]:
                sp.dma_start(dst[:], src).then_inc(expert["loaded"], 16)
            with sp.Fori(0, BATCH) as b:
                sp.dma_start(xb[:], x_in[bass.ds(b, 1)].rearrange("a (j p) d -> p (a j) d", p=P)).then_inc(x_loaded, 16)
                wait(sp, tok_done, b + 1)
                sp.dma_start(tok_out.rearrange("c p (b j) n -> b p c (j n)", b=BATCH)[bass.ds(b, 1)].rearrange("a p c n -> (a p) c n"),
                             tok[:].rearrange("p c j n -> p c (j n)")).then_inc(stored, 16)
                wait(sp, t_done, 1 + (b + 1) * 3)
                sp.dma_start(t_out.rearrange("c p b k n -> b p c (k n)")[bass.ds(b, 1)].rearrange("a p c n -> (a p) c n"),
                             tT[:].rearrange("p c k n -> p c (k n)")).then_inc(stored, 16)
                wait(sp, stored, 1 + b * 32 + 32)

        @block.gpsimd
        def _(pool):
            pool.memset(negh[:], -0.5).then_inc(setup, 1)
            pool.memset(half[:], 0.5).then_inc(setup, 1)
            pool.wait_ge(setup, SETUP)
            with pool.Fori(0, BATCH) as b:
                wait(pool, stats_done, b + 1)
                nc.gpsimd.tensor_scalar(vareps[:], mv[:, :, 1], LN_EPS, None, ALU.add)
                pool.drain()
                nc.gpsimd.tensor_tensor(rstd[:], vareps[:], negh[:, 0:TILES], ALU.pow).then_inc(rstd_done, 1)
                wait(pool, sums, 2 * b + 1)
                nc.gpsimd.tensor_scalar(mse[:], ms[:], 1.0 / D, 1e-6, ALU.mult, ALU.add)
                pool.drain()
                nc.gpsimd.tensor_tensor(rms[:], mse[:], negh[:], ALU.pow).then_inc(powers, 1)
                wait(pool, sums, 2 * b + 2)
                nc.gpsimd.tensor_tensor(hn[:], hs2[:], half[:], ALU.pow).then_inc(powers, 1)
                pool.wait_ge(heads_done, b + 1)
                pool.wait_ge(lr_done, b + 1)
                wait(pool, stored, 1 + b * 32)
                for n, (source, i) in enumerate(((qkn[:, :, D:2 * D], 0), (qkn[:, :, D:2 * D], 2), (raw[:, :, 2 * D:3 * D], 1))):
                    rate = lr[:].rearrange("p j (h i) -> p j h i", i=3)[:, :, :, i].unsqueeze(3).broadcast_to([P, TILES, FW_HEADS, FW_D])
                    last = nc.gpsimd.tensor_tensor(tok[:].rearrange("p c j n -> p (c j) n")[:, :, n * D:(n + 1) * D].rearrange("p j (h d) -> p j h d", d=FW_D),
                                                   source.rearrange("p j (h d) -> p j h d", d=FW_D), rate, ALU.mult)
                last.then_inc(tok_done, 1)

        @block.scalar
        def _(act):
            act.wait_ge(weights_in, 4 * 16)
            with act.Fori(0, BATCH) as b:
                act.wait_ge(xt_psum, b + 1)
                nc.scalar.activation(xT[:], psT[0][:].rearrange("p a n -> p (a n)"), ACT.Copy).then_inc(xt_done, 1)
                for j in range(TILES):
                    act.wait_ge(w_psum, b * TILES + (j + 1))
                    nc.scalar.activation(raw[:, j], psW[j % 4][:, 0:W], ACT.Copy).then_inc(raw_done, 1)
                act.drain()
                nc.scalar.activation(sq[:], raw[:, :, 0:2 * D], ACT.Square).then_inc(squares, 1)
                act.wait_ge(z_done, b + 1)
                nc.scalar.activation(u[:], za[:], ACT.Exp, scale=-1.0).then_inc(u_done, 1)
                act.wait_ge(y1_done, b + 1)
                nc.scalar.activation(ln[:], y1[:], ACT.Ln).then_inc(ln_done, 1)
                act.wait_ge(scaled, b + 1)
                nc.scalar.activation(sq[:], qk[:], ACT.Square).then_inc(squares, 1)
                act.wait_ge(stored, 1 + b * 32)
                for k in range(3):
                    act.wait_ge(t_psum, b * 3 + (k + 1))
                    nc.scalar.activation(tT[:, :, k], psT[k % 2][:].rearrange("p a (c n) -> p (a c) n", n=CHUNK), ACT.Copy).then_inc(t_done, 1)

        @block.tensor
        def _(pe):
            pe.wait_ge(weights_in, 4 * 16)
            with pe.Fori(0, BATCH) as b:
                def transpose_all(out, source, done):
                    for j in range(TILES):
                        last = nc.tensor.transpose(out[:, j // 4, (j % 4) * P:(j % 4 + 1) * P], source(j), ident[:])
                    last.then_inc(done, 1)
                pe.wait_ge(xn_done, b + 1)
                pe.wait_ge(t_done, 1 + b * 3)
                transpose_all(psT[0], lambda j: xn[:, j], xt_psum)
                pe.wait_ge(xt_done, b + 1)
                for j in range(TILES):
                    if j >= 4:
                        pe.wait_ge(raw_done, b * TILES + (j - 3))
                    nc.tensor.matmul(psW[j % 4][:, 0:W], xT[:, j * P:(j + 1) * P], w[:], start=True, stop=True).then_inc(w_psum, 1)
                pe.wait_ge(heads_done, b + 1)
                transpose_all(psT[0], lambda j: qkn[:, j, 0:D], t_psum)
                transpose_all(psT[1], lambda j: qkn[:, j, D:2 * D], t_psum)
                pe.wait_ge(t_done, 1 + b * 3 + 1)
                transpose_all(psT[0], lambda j: raw[:, j, 2 * D:3 * D], t_psum)

        @block.vector
        def _(dve):
            dve.wait_ge(weights_in, 4 * 16)
            dve.wait_ge(setup, SETUP)
            nc.vector.tensor_scalar(bias[:], bias[:], BASE_LR_INV, None, ALU.add)
            with dve.Fori(0, BATCH) as b:
                dve.wait_ge(x_loaded, b * 16 + 16)
                for j in range(TILES):
                    nc.vector.bn_stats(stats[:, j], xb[:, j])
                dve.drain()
                for j in range(TILES):
                    last = nc.vector.bn_aggr(mv[:, j], stats[:, j])
                last.then_inc(stats_done, 1)
                dve.wait_ge(rstd_done, b + 1)
                for j in range(TILES):
                    last = nc.vector.tensor_scalar(xn[:, j], xb[:, j], mv[:, j, 0:1], rstd[:, j:j + 1], ALU.subtract, ALU.mult)
                last.then_inc(xn_done, 1)
                dve.wait_ge(raw_done, (b + 1) * TILES)
                nc.vector.tensor_tensor(z[:], raw[:, :, 3 * D:W], bias[:].unsqueeze(1).broadcast_to([P, TILES, L]), ALU.add)
                dve.drain()
                nc.vector.scalar_tensor_tensor(za[:], z[:], -1.0, z[:], ALU.mult, ALU.max).then_inc(z_done, 1)
                dve.wait_ge(squares, 2 * b + 1)
                nc.vector.reduce_sum(ms[:], sq[:].rearrange("p j (k d) -> p (j k) d", d=D), AX.X).then_inc(sums, 1)
                dve.wait_ge(u_done, b + 1)
                nc.vector.tensor_scalar(y1[:], u[:], 1.0, None, ALU.add).then_inc(y1_done, 1)
                dve.wait_ge(powers, 2 * b + 1)
                nc.vector.tensor_tensor(qk[:].rearrange("p j (k d) -> p j k d", d=D), raw[:, :, 0:2 * D].rearrange("p j (k d) -> p j k d", d=D),
                                        rms[:].rearrange("p (j k) -> p j k", k=2).unsqueeze(3).broadcast_to([P, TILES, 2, D]), ALU.mult)
                dve.drain()
                nc.vector.tensor_tensor(qk[:], qk[:], nw[:].unsqueeze(1).broadcast_to([P, TILES, 2 * D]), ALU.mult).then_inc(scaled, 1)
                nc.vector.tensor_scalar(dd[:], y1[:], -1.0, None, ALU.add)
                dve.drain()
                nc.vector.tensor_scalar(one[:], dd[:], 0.0, None, ALU.is_equal)
                wait(dve, ln_done, b + 1)
                dve.drain()
                nc.vector.tensor_tensor(dd[:], dd[:], one[:], ALU.add)
                nc.vector.tensor_tensor(ln[:], ln[:], one[:], ALU.add)
                dve.drain()
                nc.vector.reciprocal(dd[:], dd[:])
                nc.vector.tensor_tensor(ln[:], ln[:], u[:], ALU.mult)
                dve.drain()
                nc.vector.tensor_tensor(ln[:], ln[:], dd[:], ALU.mult)
                dve.drain()
                nc.vector.scalar_tensor_tensor(lr[:], z[:], 0.0, ln[:], ALU.max, ALU.add).then_inc(lr_done, 1)
                dve.wait_ge(squares, 2 * b + 2)
                nc.vector.reduce_sum(hs2[:], sq[:].rearrange("p j (k d) -> p (j k) d", d=FW_D), AX.X).then_inc(sums, 1)
                dve.wait_ge(powers, 2 * b + 2)
                nc.vector.tensor_scalar(hn[:], hn[:], 1e-5, None, ALU.add)
                dve.drain()
                nc.vector.reciprocal(rhn[:], hn[:])
                dve.drain()
                nc.vector.tensor_tensor(qkn[:].rearrange("p j (k d) -> p (j k) d", d=FW_D), qk[:].rearrange("p j (k d) -> p (j k) d", d=FW_D),
                                        rhn[:].unsqueeze(2).broadcast_to([P, TILES * 2 * FW_HEADS, FW_D]), ALU.mult).then_inc(heads_done, 1)


def fast_weight_stage(nc, x_in, x_out, tok_in, t_in, w_start, consts):
    H, HID, DH = FW_HEADS, FW_HID, FW_D
    ctx = ExitStack()
    with ctx:
        sb = lambda n, shape, dt=F32: ctx.enter_context(nc.sbuf_tensor(f"fw_{n}", shape, dt))
        sem = lambda n: ctx.enter_context(nc.semaphore(f"fw_{n}"))
        ident = sb("ident", [P, P])
        block_ones = sb("block_ones", [P, 3, P])
        eye = sb("eye", [P, DH])
        eyes = sb("eyes", [P, len(NEWTON), DH])
        half = sb("half", [P, 36])
        state = sb("state", [P, 3, 256])
        norm0 = sb("norm0", [P, 20])
        tok = sb("tok", [P, 2 * BATCH, 3 * D])
        T = sb("T", [P, BATCH, 3, CHUNK])
        xc = sb("xc", [P, 2 * BATCH, D])
        xo = sb("xo", [P, 2 * BATCH, D])
        wb = sb("wb", [P, BATCH, 3, 256])
        w1b = sb("w1b", [P, BATCH, 2, 2 * DH])
        two = lambda n: [sb(f"{n}{s}", [P, 2, 256]) for s in range(2)]
        th, hb, sig, sg, v, dhbm, dgate, hidden, ds, dgba = (two(n) for n in ("th", "hb", "sig", "sg", "v", "dhbm", "dgate", "hidden", "ds", "dgba"))
        xr = sb("xr", [P, 3, BATCH, HID])
        yr = sb("yr", [P, 3, BATCH, 2, DH])
        X = sb("X", [P, 3, BATCH, HID])
        Y = sb("Y", [P, 3, BATCH, 2, DH])
        sq = sb("sq", [P, 768])
        rs = sb("rs", [P, 12])
        fro = sb("fro", [P, 3, 12])
        froot = sb("froot", [P, 3, 12])
        rn = sb("rn", [P, 3, 12])
        A = [sb(f"A{g}", [P, BATCH, DH]) for g in range(3)]
        T1 = [sb(f"T1{g}", [P, BATCH, DH]) for g in range(3)]
        M = [sb(f"M{g}", [P, BATCH, DH]) for g in range(3)]
        ssq = sb("ssq", [P, 20])
        wn = sb("wn", [P, 20])
        wf = sb("wf", [P, 20])
        qth = sb("qth", [P, 512])
        qgated = sb("qgated", [P, 512])
        prod = sb("prod", [P, 2, CHUNK])
        banks = ctx.enter_context(nc.psum_tensor("fw_banks", [P, 8, 512], F32))

        weights_in, setup, waits_passed = sem("weights_in"), sem("setup"), sem("waits_passed")
        tok_in_s, t_in_s, x_in_s, x_stored = sem("tok_loaded"), sem("t_loaded"), sem("x_loaded"), sem("x_stored")
        norm_sq, norm_root, state_done, turned = sem("norm_sq"), sem("norm_root"), sem("state_done"), sem("turned")
        wb_act, wb_dve, wb_pool = sem("wb_act"), sem("wb_dve"), sem("wb_pool")
        kv_psum, tanh_done, sg_done, v_done, dgate_done, back_dve, back_pool = (sem(n) for n in ("kv_psum", "tanh_done", "sg_done", "v_done", "dgate_done", "back_dve", "back_pool"))
        dw_psum, xr_done, yr_done, rs_done, fro_psum, fro_done, start_done = (sem(n) for n in ("dw_psum", "xr_done", "yr_done", "rs_done", "fro_psum", "fro_done", "start_done"))
        a_psum, a_done, aa_psum, m_done, xy_psum, x_done, y_done = (sem(n) for n in ("a_psum", "a_done", "aa_psum", "m_done", "xy_psum", "x_done", "y_done"))
        q_psum, qth_done, prod_done, o_psum, o_done = (sem(n) for n in ("q_psum", "qth_done", "prod_done", "o_psum", "o_done"))
        IT = len(NEWTON)
        SETUP = 3
        block = ctx.enter_context(nc.Block())

        def quadrant(h):
            return slice(DH * h, DH * h + DH)

        def side(h):
            return slice(HID * (h % 2), HID * (h % 2) + HID)

        def wait(engine, semaphore, value):
            engine.wait_ge(semaphore, value)
            engine.sem_inc(waits_passed, 1)

        @block.sync
        def _(sp):
            for count in (x_stored, o_done, x_done, y_done):
                sp.sem_inc(count, 1)
            for dst, src in ((ident[:], consts["ident"]), (block_ones[:], consts["block_ones"]), (eye[:], consts["eye"]), (state[:], w_start)):
                sp.dma_start(dst, src).then_inc(weights_in, 16)

            def load_tok(c):
                sp.dma_start(tok[:], tok_in[bass.ds(c, 1)].rearrange("a p b n -> (a p) b n")).then_inc(tok_in_s, 16)

            def load_t(c):
                sp.dma_start(T[:], t_in[bass.ds(c, 1)].rearrange("a p b k n -> (a p) b k n")).then_inc(t_in_s, 16)

            def load_x(c):
                for b in range(BATCH):
                    sp.dma_start(xc[:, 2 * b:2 * b + 2], x_in[b].rearrange("(c j p) d -> c p j d", c=CHUNKS, p=P)[bass.ds(c, 1)].rearrange("a p j d -> (a p) j d")).then_inc(x_in_s, 16)

            def store_x(c):
                wait(sp, o_done, 1 + (c + 1) * BATCH)
                for b in range(BATCH):
                    sp.dma_start(x_out[b].rearrange("(c j p) d -> c p j d", c=CHUNKS, p=P)[bass.ds(c, 1)].rearrange("a p j d -> (a p) j d"), xo[:, 2 * b:2 * b + 2]).then_inc(x_stored, 16)
                wait(sp, x_stored, 1 + (c + 1) * BATCH * 16)

            load_tok(0)
            load_t(0)
            load_x(0)
            with sp.Fori(0, CHUNKS - 1) as c:
                wait(sp, dw_psum, c + 1)
                load_tok(c + 1)
                store_x(c)
                load_t(c + 1)
                load_x(c + 1)
            store_x(CHUNKS - 1)

        def root_of_squares(c):
            nc.gpsimd.tensor_tensor(wn[:], ssq[:], half[:, 0:20], ALU.pow).then_inc(norm_root, 1)

        @block.gpsimd
        def _(pool):
            pool.memset(half[:], 0.5).then_inc(setup, 1)
            pool.memset(wb[:], 0.0).then_inc(setup, 1)
            pool.memset(w1b[:], 0.0).then_inc(setup, 1)
            pool.wait_ge(setup, SETUP)
            pool.wait_ge(weights_in, 4 * 16)
            pool.wait_ge(norm_sq, 1)
            root_of_squares(0)

            def place(c):
                for h in range(H):
                    last = nc.gpsimd.tensor_copy(wb[quadrant(h), :, 2, HID * h:HID * h + HID], state[quadrant(h), 2, :].rearrange("p (b n) -> p b n", b=BATCH))
                last.then_inc(wb_pool, 1)

            with pool.Fori(0, CHUNKS - 1) as c:
                wait(pool, state_done, c + 1)
                place(c)
                for b in range(BATCH):
                    s = b % 2
                    wait(pool, sg_done, c * BATCH + b + 1)
                    nc.gpsimd.tensor_tensor(hidden[s][:], sg[s][:], hb[s][:], ALU.mult)
                    wait(pool, v_done, c * BATCH + b + 1)
                    nc.gpsimd.tensor_tensor(ds[s][:], v[s][:], sig[s][:], ALU.mult)
                    wait(pool, dgate_done, c * BATCH + b + 1)
                    pool.drain()
                    nc.gpsimd.tensor_tensor(dgba[s][:], ds[s][:], dgate[s][:], ALU.mult).then_inc(back_pool, 1)
                pool.wait_ge(fro_psum, c + 1)
                wait(pool, fro_done, c + 1)
                nc.gpsimd.tensor_tensor(froot[:], fro[:], half[:].rearrange("p (a n) -> p a n", a=3), ALU.pow).then_inc(start_done, 1)
                wait(pool, norm_sq, c + 2)
                root_of_squares(c + 1)
            pool.wait_ge(state_done, CHUNKS)
            place(CHUNKS - 1)

        @block.scalar
        def _(act):
            act.wait_ge(setup, SETUP)
            act.wait_ge(weights_in, 4 * 16)

            def distribute(c):
                act.wait_ge(turned, c + 1)
                for h in range(H):
                    nc.scalar.activation(wb[quadrant(h), :, 0, HID * h:HID * h + HID], banks[quadrant(h), 0, 0:256].rearrange("p (b n) -> p b n", b=BATCH), ACT.Copy)
                for m in range(2):
                    last = nc.scalar.activation(w1b[side(m), :, 0, DH * m:DH * m + DH], banks[side(m), 2, 0:P].rearrange("p (b n) -> p b n", b=BATCH), ACT.Copy)
                last.then_inc(wb_act, 1)

            def query_tanh(c, b):
                act.wait_ge(q_psum, c * BATCH + b + 1)
                nc.scalar.activation(qth[:], banks[:, 6], ACT.Tanh, scale=0.5).then_inc(qth_done, 1)

            with act.Fori(0, CHUNKS - 1) as c:
                distribute(c)
                for b in range(BATCH):
                    s = b % 2
                    act.wait_ge(kv_psum, c * BATCH + b + 1)
                    if b >= 2:
                        act.wait_ge(back_pool, c * BATCH + b - 1)
                        act.wait_ge(back_dve, c * BATCH + b - 1)
                    nc.scalar.activation(th[s][:], banks[:, 0:2, 0:256], ACT.Tanh, scale=0.5)
                    nc.scalar.activation(hb[s][:], banks[:, 0:2, 256:512], ACT.Copy).then_inc(tanh_done, 1)
                act.wait_ge(dw_psum, c + 1)
                for g in range(3):
                    src = banks[:, 5, 256 * g:256 * g + 256] if g < 2 else banks[:, 7, 0:256]
                    last = nc.scalar.activation(yr[:, g], src.rearrange("p (b k n) -> p b k n", b=BATCH, k=2), ACT.Copy)
                last.then_inc(yr_done, 1)
                for it in range(IT):
                    step = (c * IT + it) * 3
                    for g in range(3):
                        act.wait_ge(a_psum, step + g + 1)
                        nc.scalar.activation(A[g][:], banks[:, g, 0:P].rearrange("p (b n) -> p b n", b=BATCH), ACT.Copy).then_inc(a_done, 1)
                    if it < BATCH:
                        query_tanh(c, it)
                    for g in range(3):
                        act.wait_ge(xy_psum, step + g + 1)
                        nc.scalar.activation(X[:, g], banks[:, 3, 0:256].rearrange("p (b n) -> p b n", b=BATCH), ACT.Copy).then_inc(x_done, 1)
            distribute(CHUNKS - 1)
            for b in range(BATCH):
                query_tanh(CHUNKS - 1, b)

        @block.tensor
        def _(pe):
            pe.wait_ge(setup, SETUP)
            pe.wait_ge(weights_in, 4 * 16)

            def turn_state(c):
                wait(pe, state_done, c + 1)
                for g in range(2):
                    for b in range(BATCH):
                        for h in range(H):
                            k = (b * 2 + h // 2) * DH
                            nc.tensor.matmul(banks[quadrant(h), g, HID * b:HID * b + HID], state[side(h), g, k:k + DH], ident[side(h), side(h)], start=True, stop=True)
                for b in range(BATCH):
                    for h in range(H):
                        last = nc.tensor.matmul(banks[side(h), 2 + h // 2, DH * b:DH * b + DH], state[quadrant(h), 2, HID * b:HID * b + HID], ident[quadrant(h), quadrant(h)], start=True, stop=True)
                last.then_inc(turned, 1)

            def backward(c, b):
                if b == 0:
                    for w in (wb_act, wb_dve, wb_pool):
                        pe.wait_ge(w, c + 1)
                    wait(pe, t_in_s, (c + 1) * 16)
                else:
                    wait(pe, dgate_done, c * BATCH + b)
                for j in range(2):
                    nc.tensor.matmul(banks[:, j, :], T[:, b, 1, j * P:(j + 1) * P], wb[:, b, 0:2, :], start=True, stop=True)
                    last = nc.tensor.matmul(banks[:, 2, 256 * j:256 * j + 256], T[:, b, 2, j * P:(j + 1) * P], wb[:, b, 2, :], start=True, stop=True)
                last.then_inc(kv_psum, 1)

            def gradients(c, b):
                pe.wait_ge(back_dve, c * BATCH + b + 1)
                wait(pe, back_pool, c * BATCH + b + 1)
                if b == 0:
                    wait(pe, tok_in_s, (c + 1) * 16)
                s = b % 2
                for g, left in enumerate((dgba[s], dhbm[s], hidden[s])):
                    for h in range(H):
                        xb_ = banks[quadrant(h), 3, 256 * g + HID * b:256 * g + HID * (b + 1)] if g < 2 else banks[quadrant(h), 4, HID * b:HID * (b + 1)]
                        k = (b * 2 + h // 2) * DH
                        yb_ = banks[side(h), 5, 256 * g + k:256 * g + k + DH] if g < 2 else banks[side(h), 7, k:k + DH]
                        rows = lambda j: tok[:, 2 * b + j, D * g + DH * h:D * g + DH * h + DH]
                        cols = lambda j: left[:, j, HID * h:HID * h + HID]
                        for j in range(2):
                            nc.tensor.matmul(xb_, rows(j), cols(j), start=(j == 0), stop=(j == 1))
                        for j in range(2):
                            last = nc.tensor.matmul(yb_, cols(j), rows(j), start=(j == 0), stop=(j == 1))
                if b == BATCH - 1:
                    last.then_inc(dw_psum, 1)

            def query(c, b):
                if b == 0:
                    for w in (wb_act, wb_dve, wb_pool):
                        pe.wait_ge(w, c + 1)
                    pe.wait_ge(t_in_s, (c + 1) * 16)
                wait(pe, o_done, 1 + c * BATCH + b)
                for g in range(2):
                    for k in range(2):
                        last = nc.tensor.matmul(banks[:, 6 + g, CHUNK * k:CHUNK * (k + 1)], wb[:, b, g, P * k:P * k + P], T[:, b, 0, :], start=True, stop=True)
                last.then_inc(q_psum, 1)

            def output(c, b):
                wait(pe, prod_done, c * BATCH + b + 1)
                for j in range(2):
                    for k in range(2):
                        last = nc.tensor.matmul(banks[:, 7, D * j + 2 * DH * k:D * j + 2 * DH * (k + 1)], prod[:, k, j * P:(j + 1) * P], w1b[:, b, k, :], start=True, stop=True)
                last.then_inc(o_psum, 1)

            with pe.Fori(0, CHUNKS - 1) as c:
                turn_state(c)
                for b in range(BATCH):
                    backward(c, b)
                    if b == 0:
                        wait(pe, o_done, 1 + c * BATCH)
                    if b >= 1:
                        gradients(c, b - 1)
                gradients(c, BATCH - 1)
                wait(pe, rs_done, c + 1)
                for n in range(3):
                    last = nc.tensor.matmul(banks[:, 6, 16 * n:16 * n + 12], block_ones[:, n], rs[:], start=True, stop=True)
                last.then_inc(fro_psum, 1)
                wait(pe, yr_done, c + 1)
                for it in range(IT):
                    step = (c * IT + it) * 3
                    for g in range(3):
                        if it == 0:
                            wait(pe, m_done, c * (IT * 3 + 1) + 1)
                        else:
                            wait(pe, y_done, 1 + step - 3 + g + 1)
                        for b in range(BATCH):
                            for h in range(H):
                                y = Y[side(h), g, b, h // 2, :]
                                last = nc.tensor.matmul(banks[quadrant(h), g, DH * b:DH * b + DH], y, y, start=True, stop=True)
                        last.then_inc(a_psum, 1)
                    if it < BATCH:
                        query(c, it)
                    for g in range(3):
                        wait(pe, a_done, step + g + 1)
                        for b in range(BATCH):
                            for h in range(H):
                                a = A[g][quadrant(h), b, :]
                                last = nc.tensor.matmul(banks[quadrant(h), g, P + DH * b:P + DH * b + DH], a, a, start=True, stop=True)
                        last.then_inc(aa_psum, 1)
                    for g in range(3):
                        wait(pe, m_done, c * (IT * 3 + 1) + 1 + it * 3 + g + 1)
                        pe.wait_ge(x_done, 1 + step + g)
                        wait(pe, y_done, 1 + step + g)
                        for b in range(BATCH):
                            for h in range(H):
                                m, x = M[g][quadrant(h), b, :], X[quadrant(h), g, b, :]
                                nc.tensor.matmul(banks[quadrant(h), 3, HID * b:HID * b + HID], m, x, start=True, stop=True)
                                last = nc.tensor.matmul(banks[side(h), 4 + h // 2, DH * b:DH * b + DH], x, m, start=True, stop=True)
                        last.then_inc(xy_psum, 1)
                    if it < BATCH:
                        output(c, it)
            turn_state(CHUNKS - 1)
            for b in range(BATCH):
                query(CHUNKS - 1, b)
                output(CHUNKS - 1, b)

        @block.vector
        def _(dve):
            dve.wait_ge(setup, SETUP)
            dve.wait_ge(weights_in, 4 * 16)

            def sum_state_squares():
                nc.vector.tensor_tensor(sq[:], state[:].rearrange("p g n -> p (g n)"), state[:].rearrange("p g n -> p (g n)"), ALU.mult)
                dve.drain()
                nc.vector.reduce_sum(ssq[:, 0:16], sq[:, 0:512].rearrange("p (a n) -> p a n", n=DH), AX.X)
                nc.vector.reduce_sum(ssq[:, 16:20], sq[:, 512:768].rearrange("p (a n) -> p a n", n=HID), AX.X).then_inc(norm_sq, 1)

            def distribute(c):
                dve.wait_ge(turned, c + 1)
                for h in range(H):
                    nc.vector.tensor_copy(wb[quadrant(h), :, 1, HID * h:HID * h + HID], banks[quadrant(h), 1, 0:256].rearrange("p (b n) -> p b n", b=BATCH))
                for m in range(2):
                    last = nc.vector.tensor_copy(w1b[side(m), :, 1, DH * m:DH * m + DH], banks[side(m), 3, 0:P].rearrange("p (b n) -> p b n", b=BATCH))
                last.then_inc(wb_dve, 1)

            def query_product(c, b):
                dve.wait_ge(qth_done, c * BATCH + b + 1)
                nc.vector.scalar_tensor_tensor(qgated[:], qth[:], 1.0, banks[:, 6], ALU.add, ALU.mult)
                dve.drain()
                nc.vector.tensor_tensor(prod[:].rearrange("p k n -> p (k n)"), qgated[:], banks[:, 7], ALU.mult).then_inc(prod_done, 1)

            def add_output(c, b):
                if b == 0:
                    dve.wait_ge(x_in_s, (c + 1) * BATCH * 16)
                    dve.wait_ge(x_stored, 1 + c * BATCH * 16)
                dve.wait_ge(o_psum, c * BATCH + b + 1)
                nc.vector.scalar_tensor_tensor(xo[:, 2 * b:2 * b + 2], banks[:, 7, 0:2 * D].rearrange("p (j d) -> p j d", d=D), 0.5, xc[:, 2 * b:2 * b + 2],
                                               ALU.mult, ALU.add).then_inc(o_done, 1)

            for n, (a, _, _) in enumerate(NEWTON):
                nc.vector.tensor_scalar(eyes[:, n], eye[:], a, None, ALU.mult)
            sum_state_squares()
            dve.wait_ge(norm_root, 1)
            nc.vector.tensor_copy(norm0[:], wn[:]).then_inc(state_done, 1)

            with dve.Fori(0, CHUNKS - 1) as c:
                distribute(c)
                for b in range(BATCH):
                    s = b % 2
                    dve.wait_ge(tanh_done, c * BATCH + b + 1)
                    gba, dhid = banks[:, 0:2, 0:256], banks[:, 2].rearrange("p (j n) -> p j n", j=2)
                    nc.vector.tensor_scalar(sig[s][:], th[s][:], 0.5, 0.5, ALU.mult, ALU.add)
                    dve.drain()
                    nc.vector.tensor_tensor(sg[s][:], gba, sig[s][:], ALU.mult).then_inc(sg_done, 1)
                    dve.drain()
                    nc.vector.scalar_tensor_tensor(v[s][:], gba, 1.0, sg[s][:], ALU.add, ALU.subtract).then_inc(v_done, 1)
                    nc.vector.tensor_tensor(dhbm[s][:], dhid, sg[s][:], ALU.mult).then_inc(back_dve, 1)
                    nc.vector.tensor_tensor(dgate[s][:], dhid, hb[s][:], ALU.mult).then_inc(dgate_done, 1)
                dve.wait_ge(dw_psum, c + 1)
                for g in range(3):
                    src = banks[:, 3, 256 * g:256 * g + 256] if g < 2 else banks[:, 4, 0:256]
                    nc.vector.tensor_copy(xr[:, g], src.rearrange("p (b n) -> p b n", b=BATCH))
                dve.drain()
                nc.vector.tensor_tensor(sq[:], xr[:].rearrange("p g b n -> p (g b n)"), xr[:].rearrange("p g b n -> p (g b n)"), ALU.mult)
                dve.drain()
                nc.vector.reduce_sum(rs[:], sq[:].rearrange("p (a n) -> p a n", n=HID), AX.X).then_inc(rs_done, 1)
                dve.wait_ge(fro_psum, c + 1)
                nc.vector.tensor_copy(fro[:], banks[:, 6, 0:48].rearrange("p (a n) -> p a n", n=16)[:, :, 0:12]).then_inc(fro_done, 1)
                dve.wait_ge(start_done, c + 1)
                nc.vector.tensor_scalar(froot[:], froot[:], 1e-7, None, ALU.add)
                dve.drain()
                nc.vector.reciprocal(rn[:], froot[:])
                wait(dve, yr_done, c + 1)
                dve.drain()
                nc.vector.tensor_tensor(X[:].rearrange("p g b n -> p (g b) n"), xr[:].rearrange("p g b n -> p (g b) n"), rn[:, 0].unsqueeze(2).broadcast_to([P, 12, HID]), ALU.mult)
                nc.vector.tensor_tensor(Y[:].rearrange("p g b k n -> p (g b) k n"), yr[:].rearrange("p g b k n -> p (g b) k n"),
                                        rn[:, 1:3].rearrange("p k a -> p a k").unsqueeze(3).broadcast_to([P, 12, 2, DH]), ALU.mult).then_inc(m_done, 1)
                for it, (_, b_, c_) in enumerate(NEWTON):
                    step = (c * IT + it) * 3
                    for g in range(3):
                        dve.wait_ge(a_done, step + g + 1)
                        nc.vector.scalar_tensor_tensor(T1[g][:], A[g][:], b_, eyes[:, it].unsqueeze(1).broadcast_to([P, BATCH, DH]), ALU.mult, ALU.add)
                    dve.drain()
                    for g in range(3):
                        dve.wait_ge(aa_psum, step + g + 1)
                        nc.vector.scalar_tensor_tensor(M[g][:], banks[:, g, P:2 * P].rearrange("p (b n) -> p b n", b=BATCH), c_, T1[g][:], ALU.mult, ALU.add).then_inc(m_done, 1)
                    if it < BATCH:
                        query_product(c, it)
                    for g in range(3):
                        dve.wait_ge(xy_psum, step + g + 1)
                        nc.vector.tensor_copy(Y[:, g].rearrange("p b k n -> p k b n"), banks[:, 4:6, 0:P].rearrange("p k (b n) -> p k b n", b=BATCH)).then_inc(y_done, 1)
                    if it < BATCH:
                        add_output(c, it)
                wait(dve, x_done, 1 + (c + 1) * IT * 3)
                dve.drain()
                nc.vector.tensor_tensor(state[:, 0:2].rearrange("p g n -> p (g n)"), state[:, 0:2].rearrange("p g n -> p (g n)"), Y[:, 0:2].rearrange("p g b k n -> p (g b k n)"), ALU.add)
                nc.vector.tensor_tensor(state[:, 2], state[:, 2], X[:, 2].rearrange("p b n -> p (b n)"), ALU.add)
                dve.drain()
                sum_state_squares()
                dve.wait_ge(norm_root, c + 2)
                nc.vector.tensor_scalar(wn[:], wn[:], 1e-5, None, ALU.add)
                dve.drain()
                nc.vector.reciprocal(wf[:], wn[:])
                dve.drain()
                nc.vector.tensor_tensor(wf[:], wf[:], norm0[:], ALU.mult)
                dve.drain()
                nc.vector.tensor_tensor(state[:, 0:2].rearrange("p g (a n) -> p (g a) n", n=DH), state[:, 0:2].rearrange("p g (a n) -> p (g a) n", n=DH),
                                        wf[:, 0:16].unsqueeze(2).broadcast_to([P, 16, DH]), ALU.mult)
                nc.vector.tensor_tensor(state[:, 2].rearrange("p (a n) -> p a n", n=HID), state[:, 2].rearrange("p (a n) -> p a n", n=HID),
                                        wf[:, 16:20].unsqueeze(2).broadcast_to([P, 4, HID]), ALU.mult).then_inc(state_done, 1)
            distribute(CHUNKS - 1)
            for b in range(BATCH):
                query_product(CHUNKS - 1, b)
                add_output(CHUNKS - 1, b)


def expert_weights(nc, ctx, gate_proj, up_proj, down_proj):
    sb = lambda n, dt=F32: ctx.enter_context(nc.sbuf_tensor(f"expert_{n}", [P, EXPERTS, 2 * P], dt))
    wg, wu, wd = sb("wg"), sb("wu"), sb("wd")
    return {
        "wg": wg, "wu": wu, "wd": wd[:].rearrange("p e (k d) -> p e k d", k=2),
        "loads": ((wg, gate_proj), (wu, up_proj), (wd, down_proj.rearrange("p e k d -> p e (k d)"))),
        "loaded": ctx.enter_context(nc.semaphore("expert_weights_loaded")),
    }


def expert_stage(nc, name, x_in, x_out, gate_w, weights, consts):
    groups, tiles = TOKENS // GROUP, GROUP // P
    units = 2 * EXPERTS
    ctx = ExitStack()
    with ctx:
        sb = lambda n, shape, dt=F32: ctx.enter_context(nc.sbuf_tensor(f"{name}_{n}", shape, dt))
        ps = lambda n, shape: ctx.enter_context(nc.psum_tensor(f"{name}_{n}", shape, F32))
        sem = lambda n: ctx.enter_context(nc.semaphore(f"{name}_{n}"))

        wg, wu, wd = weights["wg"], weights["wu"], weights["wd"]
        wg_hi, wg_lo, wu_hi, wu_lo = (sb(n, [P, EXPERTS, 2 * P], F32R) for n in ("wg_hi", "wg_lo", "wu_hi", "wu_lo"))
        wr = sb("wr", [P, EXPERTS])
        ident = sb("ident", [P, P])
        tri_f = sb("tri_f", [P, P])
        tri = sb("tri", [P, P], BF16)
        ones = sb("ones", [P, P], BF16)
        rev = sb("rev", [P, tiles, EXPERTS])
        negh = sb("negh", [P, tiles])
        acc = [sb(f"acc{s}", [P, tiles, P]) for s in range(2)]
        x = [sb(f"x{s}", [P, tiles, P]) for s in range(2)]
        stats = sb("stats", [P, tiles, 6])
        mv = sb("mv", [P, tiles, 2])
        vareps = sb("vareps", [P, tiles])
        rstd = sb("rstd", [P, tiles])
        xn = sb("xn", [P, tiles, P])
        xT = sb("xT", [P, GROUP])
        xT_hi = [sb(f"xT_hi{s}", [P, GROUP], F32R) for s in range(2)]
        xT_lo = [sb(f"xT_lo{s}", [P, GROUP], F32R) for s in range(2)]
        gated = [sb(f"gated{k}", [P, GROUP]) for k in range(2)]
        hid = [[sb(f"hid{s}{k}", [P, GROUP]) for k in range(2)] for s in range(2)]
        lmax = sb("lmax", [P, tiles])
        lsub = sb("lsub", [P, tiles, EXPERTS])
        prob = sb("prob", [P, tiles, EXPERTS])
        probs2 = sb("probs2", [P, tiles, EXPERTS])
        psum_ = sb("psum_", [P, tiles])
        eq = sb("eq", [P, tiles, EXPERTS])
        pick = sb("pick", [P, tiles])
        top = sb("top", [P, 2, tiles])
        chosen = sb("chosen", [P, tiles + 1, 2, EXPERTS], BF16)
        wsum = sb("wsum", [P, tiles])
        rank = sb("rank", [P, tiles, 2, EXPERTS])
        carry = sb("carry", [P, 2, EXPERTS])
        comb2 = sb("comb2", [P, tiles, 2, EXPERTS])
        comb = [sb(f"comb{s}", [P, tiles, EXPERTS]) for s in range(2)]

        ps_g = [ps(f"ps_g{s}", [P, GROUP]) for s in range(2)]
        ps_u = [ps(f"ps_u{s}", [P, GROUP]) for s in range(2)]
        ps_y = [ps(f"ps_y{s}", [P, tiles, P]) for s in range(2)]
        ps_t = ps("ps_t", [P, GROUP])
        ps_r = ps("ps_r", [P, 512])
        logits = ps_r[:, 0:tiles * EXPERTS].rearrange("p (j e) -> p j e", e=EXPERTS)
        counts_all = ps_r[:, 128:128 + (tiles + 1) * 2 * EXPERTS].rearrange("p (j k e) -> p j k e", k=2, e=EXPERTS)
        counts, total = counts_all[:, 0:tiles], counts_all[:, tiles]

        weights_in, x_loaded, x_stored = sem("weights_in"), [sem("x_loaded0"), sem("x_loaded1")], sem("x_stored")
        stats_done, rstd_done, xn_done = sem("stats_done"), sem("rstd_done"), sem("xn_done")
        xt_psum, xt_done, xt_split, weights_hi, weights_lo = sem("xt_psum"), sem("xt_done"), sem("xt_split"), sem("weights_hi"), sem("weights_lo")
        logits_done, lsub_done, exp_done, chosen_done, ranks_done = sem("logits_done"), sem("lsub_done"), sem("exp_done"), sem("chosen_done"), sem("ranks_done")
        gu_done, silu_done, hid_done, y_done, y_free = sem("gu_done"), sem("silu_done"), sem("hid_done"), sem("y_done"), sem("y_free")
        setup, waits_passed = sem("setup"), sem("waits_passed")

        SETUP = 4
        block = ctx.enter_context(nc.Block())

        def both(engine, body):
            with engine.Fori(0, groups // 2 - 1) as i:
                body(i * 2, 0, True)
                body(i * 2 + 1, 1, True)
            body(groups - 2, 0, True)
            body(groups - 1, 1, False)

        def wait(engine, semaphore, value):
            engine.wait_ge(semaphore, value)
            engine.sem_inc(waits_passed, 1)

        @block.sync
        def _(sp):
            sp.sem_inc(x_stored, 1 + 16)
            sp.dma_start(x[0][:], x_in[0:1].rearrange("a (j p) d -> p (a j) d", p=P)).then_inc(x_loaded[0], 16)
            for dst, src in ((wr, gate_w), (ident, consts["ident"]), (tri_f, consts["tri"]), (rev, consts["rev"])):
                sp.dma_start(dst[:], src).then_inc(weights_in, 16)

            def load(g, s):
                sp.dma_start(x[s][:], x_in[bass.ds(g, 1)].rearrange("a (j p) d -> p (a j) d", p=P)).then_inc(x_loaded[s], 16)

            def group(g, s, more):
                if more:
                    wait(sp, y_free, g * EXPERTS + BUFFERS)
                    load(g + 1, 1 - s)
                wait(sp, y_free, (g + 1) * EXPERTS + BUFFERS)
                sp.dma_start(x_out[bass.ds(g, 1)].rearrange("a (j p) d -> p (a j) d", p=P), acc[s][:]).then_inc(x_stored, 16)

            both(sp, group)
            sp.wait_ge(x_stored, 1 + 16 + groups * 16)

        @block.gpsimd
        def _(pool):
            pool.memset(negh[:], -0.5).then_inc(setup, 1)
            pool.memset(ones[:], 1.0).then_inc(setup, 1)
            pool.memset(carry[:], 0.0).then_inc(setup, 1)
            pool.memset(chosen[:], 0.0).then_inc(setup, 1)
            pool.wait_ge(setup, SETUP)

            def rsqrt(g):
                wait(pool, stats_done, g + 1)
                nc.gpsimd.tensor_scalar(vareps[:], mv[:, :, 1], LN_EPS, None, ALU.add)
                pool.drain()
                nc.gpsimd.tensor_tensor(rstd[:], vareps[:], negh[:], ALU.pow).then_inc(rstd_done, 1)

            rsqrt(0)
            for e in range(EXPERTS):
                pool.wait_ge(weights_hi, 1 + 2 * (e + 1))
                nc.gpsimd.tensor_tensor(wg_lo[:, e], wg[:, e], wg_hi[:, e].bitcast(F32), ALU.subtract)
                nc.gpsimd.tensor_tensor(wu_lo[:, e], wu[:, e], wu_hi[:, e].bitcast(F32), ALU.subtract).then_inc(weights_lo, 1)

            def group(g, s, more):
                if more:
                    rsqrt(g + 1)

            both(pool, group)

        @block.scalar
        def _(act):
            def copy_xt(g, s):
                act.wait_ge(xt_psum, g + 1)
                nc.scalar.activation(xT_hi[s][:], ps_t[:], ACT.Copy)
                nc.scalar.activation(xT[:], ps_t[:], ACT.Copy).then_inc(xt_done, 1)

            def exp_logits(g):
                act.wait_ge(lsub_done, g + 1)
                nc.scalar.activation(prob[:], lsub[:], ACT.Exp).then_inc(exp_done, 1)

            def group(g, s, more):
                for u in range(units):
                    act.wait_ge(gu_done, g * units + (u + 1))
                    nc.scalar.activation(gated[u % 2][:], ps_g[u % 2][:], ACT.Silu).then_inc(silu_done, 1)
                    if more and u == 7:
                        copy_xt(g + 1, 1 - s)
                    if more and u == 10:
                        exp_logits(g + 1)

            act.wait_ge(weights_in, 4 * 16)
            nc.scalar.activation(tri[:], tri_f[:], ACT.Copy).then_inc(weights_hi, 1)
            act.wait_ge(weights["loaded"], 3 * 16)
            for e in range(EXPERTS):
                nc.scalar.activation(wg_hi[:, e], wg[:, e], ACT.Copy).then_inc(weights_hi, 1)
                nc.scalar.activation(wu_hi[:, e], wu[:, e], ACT.Copy).then_inc(weights_hi, 1)
            copy_xt(0, 0)
            exp_logits(0)
            both(act, group)

        @block.tensor
        def _(pe):
            def transposes(g):
                pe.wait_ge(xn_done, g + 1)
                for j in range(tiles):
                    last = nc.tensor.transpose(ps_t[:, j * P:(j + 1) * P], xn[:, j, :], ident[:])
                last.then_inc(xt_psum, 1)

            def router(g):
                pe.wait_ge(xt_done, g + 1)
                for j in range(tiles):
                    last = nc.tensor.matmul(logits[:, j, :], xT[:, j * P:(j + 1) * P], wr[:], start=True, stop=True)
                last.then_inc(logits_done, 1)

            def ranks(g):
                pe.wait_ge(chosen_done, g + 1)
                nc.tensor.matmul(counts_all, tri[:], chosen[:], start=True, stop=False)
                for i in range(tiles):
                    last = nc.tensor.matmul(counts_all[:, i + 1:tiles + 1], ones[:],
                                            chosen[:, i].unsqueeze(1).broadcast_to([P, tiles - i, 2, EXPERTS]), start=False, stop=(i == tiles - 1))
                last.then_inc(ranks_done, 1)

            def gate_up(g, s, u):
                e, k = u // 2, u % 2
                pe.wait_ge(hid_done, g * units + (u + 1))
                half = slice(k * P, (k + 1) * P)
                if k == 0:
                    pe.wait_ge(weights_lo, e + 1)
                for out, w_hi, w_lo in ((ps_g[k], wg_hi, wg_lo), (ps_u[k], wu_hi, wu_lo)):
                    nc.tensor.matmul(out[:], w_hi[:, e, half], xT_hi[s][:], start=True, stop=False)
                    nc.tensor.matmul(out[:], w_hi[:, e, half], xT_lo[s][:], start=False, stop=False)
                    last = nc.tensor.matmul(out[:], w_lo[:, e, half], xT_hi[s][:], start=False, stop=True)
                last.then_inc(gu_done, 1)

            def down(g, e):
                pe.wait_ge(hid_done, g * units + 2 * (e + 1) + BUFFERS)
                pe.wait_ge(y_free, g * EXPERTS + (e + 1))
                for j in range(tiles):
                    for k in range(2):
                        last = nc.tensor.matmul(ps_y[e % 2][:, j], hid[e % 2][k][:, j * P:(j + 1) * P], wd[:, e, k],
                                                start=(k == 0), stop=(k == 1))
                last.then_inc(y_done, 1)

            def group(g, s, more):
                for e in range(EXPERTS):
                    if e + 1 < EXPERTS:
                        gate_up(g, s, 2 * e + 2)
                        if e == 0:
                            ranks(g)
                        gate_up(g, s, 2 * e + 3)
                    elif more:
                        first_expert(g + 1, 1 - s)
                    if more and e == 2:
                        transposes(g + 1)
                    if more and e == 3:
                        router(g + 1)
                    down(g, e)

            def first_expert(g, s):
                pe.wait_ge(xt_split, g + 1)
                gate_up(g, s, 0)
                gate_up(g, s, 1)

            pe.wait_ge(weights_in, 4 * 16)
            pe.wait_ge(setup, SETUP)
            transposes(0)
            router(0)
            pe.wait_ge(weights_hi, 1)
            first_expert(0, 0)
            both(pe, group)

        @block.vector
        def _(dve):
            def statistics(g, s):
                dve.wait_ge(x_loaded[s], (g - s) * 8 + 16)
                for j in range(tiles):
                    nc.vector.bn_stats(stats[:, j], x[s][:, j])
                dve.drain()
                for j in range(tiles):
                    last = nc.vector.bn_aggr(mv[:, j], stats[:, j])
                last.then_inc(stats_done, 1)

            def normalize(g, s):
                dve.wait_ge(rstd_done, g + 1)
                for j in range(tiles):
                    last = nc.vector.tensor_scalar(xn[:, j], x[s][:, j], mv[:, j, 0:1], rstd[:, j:j + 1], ALU.subtract, ALU.mult)
                last.then_inc(xn_done, 1)

            def split(g, s):
                dve.wait_ge(xt_done, g + 1)
                nc.vector.tensor_tensor(xT_lo[s][:], ps_t[:], xT_hi[s][:].bitcast(F32), ALU.subtract).then_inc(xt_split, 1)

            def row(t):
                return t.unsqueeze(2).broadcast_to([P, tiles, EXPERTS])

            def shift_logits(g):
                dve.wait_ge(logits_done, g + 1)
                nc.vector.reduce_max(lmax[:], logits, AX.X)
                dve.drain()
                nc.vector.tensor_tensor(lsub[:], logits, row(lmax[:]), ALU.subtract).then_inc(lsub_done, 1)

            def probabilities(g):
                dve.wait_ge(exp_done, g + 1)
                nc.vector.reduce_sum(psum_[:], prob[:], AX.X)
                dve.drain()
                nc.vector.reciprocal(psum_[:], psum_[:])
                dve.drain()
                nc.vector.tensor_tensor(prob[:], prob[:], row(psum_[:]), ALU.mult)

            def exclude_first():
                dve.drain()
                nc.vector.scalar_tensor_tensor(probs2[:], chosen[:, 0:tiles, 0], -2.0, prob[:], ALU.mult, ALU.add)

            def find_largest(k):
                p = (prob, probs2)[k]
                dve.drain()
                nc.vector.reduce_max(top[:, k], p[:], AX.X)
                dve.drain()
                nc.vector.tensor_tensor(eq[:], p[:], row(top[:, k]), ALU.is_equal)

            def choose_expert(k):
                dve.drain()
                nc.vector.tensor_tensor(eq[:], eq[:], rev[:], ALU.mult)
                dve.drain()
                nc.vector.reduce_max(pick[:], eq[:], AX.X)
                dve.drain()
                return nc.vector.tensor_tensor(chosen[:, 0:tiles, k], eq[:], row(pick[:]), ALU.is_equal)

            def share():
                nc.vector.tensor_tensor(wsum[:], top[:, 0], top[:, 1], ALU.add)
                dve.drain()
                nc.vector.tensor_scalar(wsum[:], wsum[:], 1e-9, None, ALU.add)
                dve.drain()
                nc.vector.reciprocal(wsum[:], wsum[:])
                dve.drain()
                nc.vector.tensor_tensor(top[:], top[:], wsum[:].unsqueeze(1).broadcast_to([P, 2, tiles]), ALU.mult)

            def rank_tokens(g):
                dve.wait_ge(ranks_done, g + 1)
                nc.vector.tensor_tensor(rank[:], counts, carry[:].unsqueeze(1).broadcast_to([P, tiles, 2, EXPERTS]), ALU.add)

            def weigh(g, s):
                dve.drain()
                nc.vector.tensor_tensor(carry[:], carry[:], total, ALU.add)
                nc.vector.scalar_tensor_tensor(rank[:], rank[:], float(CAPACITY), chosen[:, 0:tiles], ALU.is_le, ALU.mult)
                dve.drain()
                for k in range(2):
                    nc.vector.tensor_tensor(comb2[:, :, k], rank[:, :, k], row(top[:, k]), ALU.mult)
                dve.drain()
                nc.vector.tensor_tensor(comb[s][:], comb2[:, :, 0], comb2[:, :, 1], ALU.add)

            def hidden(g, u):
                e, k = u // 2, u % 2
                dve.wait_ge(silu_done, g * units + u + 1)
                nc.vector.tensor_tensor(hid[e % 2][k][:], gated[k][:], ps_u[k][:], ALU.mult).then_inc(hid_done, 1)

            def combine(g, s, e):
                before = acc[s] if e else x[s]
                if e == 0:
                    wait(dve, x_stored, 1 + g * 16)
                dve.drain()
                dve.wait_ge(y_done, g * EXPERTS + (e + 1))
                for j in range(tiles):
                    last = nc.vector.scalar_tensor_tensor(acc[s][:, j], ps_y[e % 2][:, j], comb[s][:, j, e:e + 1], before[:, j],
                                                          ALU.mult, ALU.add)
                last.then_inc(y_free, 1)

            def route_next(g, s, u):
                if u == 3:
                    statistics(g + 1, 1 - s)
                if u == 5:
                    normalize(g + 1, 1 - s)
                if u == 8:
                    split(g + 1, 1 - s)
                if u == 9:
                    shift_logits(g + 1)
                if u == 11:
                    probabilities(g + 1)
                if u == 12:
                    find_largest(0)
                if u == 13:
                    choose_expert(0)
                if u == 14:
                    exclude_first()
                    find_largest(1)
                if u == 15:
                    choose_expert(1).then_inc(chosen_done, 1)
                if u == 16:
                    share()

            def group(g, s, more):
                for e in range(EXPERTS):
                    for u in (2 * e + 2, 2 * e + 3):
                        if u < units:
                            hidden(g, u)
                        elif more:
                            hidden(g + 1, u - units)
                        if u == 2:
                            rank_tokens(g)
                        if u == 3:
                            weigh(g, s)
                        if more:
                            route_next(g, s, u)
                    combine(g, s, e)

            nc.vector.engine_nop().then_inc(hid_done, BUFFERS)
            nc.vector.engine_nop().then_inc(y_free, BUFFERS)
            dve.wait_ge(weights_in, 4 * 16)
            dve.wait_ge(setup, SETUP)
            statistics(0, 0)
            normalize(0, 0)
            shift_logits(0)
            split(0, 0)
            probabilities(0)
            find_largest(0)
            choose_expert(0)
            exclude_first()
            find_largest(1)
            choose_expert(1).then_inc(chosen_done, 1)
            share()
            hidden(0, 0)
            hidden(0, 1)
            both(dve, group)


def causal_attention_stage(nc, x_in, x_out, w_qkv, b_qkv, w_o, b_o, consts):
    ctx = ExitStack()
    with ctx:
        sb = lambda n, shape, dt=F32: ctx.enter_context(nc.sbuf_tensor(f"att_{n}", shape, dt))
        ps = lambda n, shape: ctx.enter_context(nc.psum_tensor(f"att_{n}", shape, F32))
        sem = lambda n: ctx.enter_context(nc.semaphore(f"att_{n}"))

        wqkv = sb("wqkv", [P, 3 * D])
        wo = sb("wo", [P, D])
        bias = sb("bias", [P, 3 * D])
        bo = sb("bo", [P, D])
        ident = sb("ident", [P, P])
        identb = sb("identb", [P, P], BF16)
        mask_f = sb("mask_f", [P, 2, P])
        mask = sb("mask", [P, 2, P], BF16)
        cs = sb("cs", [P, TILES, 2, ROT])
        negh = sb("negh", [P, TILES])
        xb = sb("xb", [P, TILES, D])
        res = sb("res", [P, TILES, D])
        stats = sb("stats", [P, TILES, 6])
        mv = sb("mv", [P, TILES, 2])
        vareps = sb("vareps", [P, TILES])
        rstd = sb("rstd", [P, TILES])
        xn = sb("xn", [P, TILES, D])
        xT = sb("xT", [P, SEQ])
        qkv = sb("qkv", [P, TILES, 3 * D])
        JH = TILES * HEADS
        turned = [sb(f"turned{k}", [P, JH, ROT]) for k in range(2)]
        turned2 = [sb(f"turned2{k}", [P, JH, ROT]) for k in range(2)]
        parts = [sb(f"parts{k}", [P, JH, 3, ROT], BF16) for k in range(2)]
        q_rows, k_rows = (sb(n, [P, JH, 32], BF16) for n in ("q_rows", "k_rows"))
        qm_rows = [sb(f"qm_rows{s}", [P, TILES, QUAD, 32], BF16) for s in range(2)]
        v1 = sb("v1", [P, JH, 32])
        kT = [[sb(f"kT{s}{h}", [P, SEQ], BF16) for h in range(QUAD)] for s in range(HEADS // QUAD)]
        kT_all = sb("kT_all", [P, SEQ], BF16)
        q1T = [sb(f"q1T{s}", [P, SEQ], BF16) for s in range(2)]
        q2T = [sb(f"q2T{s}", [P, SEQ], BF16) for s in range(2)]
        mx = sb("mx", [P, 2, TILES, QUAD])
        nm = sb("nm", [P, TILES, QUAD])
        nm2 = sb("nm2", [P, TILES, QUAD])
        prob = [sb(f"prob{s}", [P, 2, 512]) for s in range(4)]
        oT = sb("oT", [P, 2, 512])
        rden = sb("rden", [P, 4, QUAD])
        y = sb("y", [P, TILES, D])
        yT = sb("yT", [P, SEQ])

        ps1 = [ps(f"ps1{s}", [P, 512]) for s in range(2)]
        ps2 = [ps(f"ps2{s}", [P, 2, 512]) for s in range(2)]
        pso = ps("pso", [P, 512])
        psm = ps("psm", [P, 512])
        psm_b = psm[:].bitcast(BF16)

        weights_in, setup, casts, waits_passed = sem("weights_in"), sem("setup"), sem("casts"), sem("waits_passed")
        x_loaded, res_loaded, res_biased, x_stored = sem("x_loaded"), sem("res_loaded"), sem("res_biased"), sem("x_stored")
        stats_done, rstd_done, xn_done, q_split, k_split = sem("stats_done"), sem("rstd_done"), sem("xn_done"), sem("q_split"), sem("k_split")
        q_stacked, k_stacked, q_copied, k_placed, v_placed = sem("q_stacked"), sem("k_stacked"), sem("q_copied"), sem("k_placed"), sem("v_placed")
        misc_full, misc_free = sem("misc_full"), sem("misc_free")
        s1_done, max_done, quad_max, max_stacked = sem("s1_done"), sem("max_done"), sem("quad_max"), sem("max_stacked")
        s2_done, exp_done, pv_done, o_copied, out_done = sem("s2_done"), sem("exp_done"), sem("pv_done"), sem("o_copied"), sem("out_done")

        QUADS = HEADS // QUAD
        MAX_STEPS = [(j, c) for j in range(TILES) for c in range(1 + (j >= 4))]
        EXP_STEPS = [(c, i) for c in range(2) for i in range(4 * c + 4)]
        STEPS = len(MAX_STEPS)
        assert len(EXP_STEPS) == STEPS

        LEAD = 4
        COMMON = {(1, "end"): "o1", (5, "end"): "k", (6, "end"): "q1", (7, "end"): "o0", (10, "end"): "q2"}
        PREP = {(3, "mid"): "x0", (3, "end"): "x1", (4, "mid"): "qk0", (4, "end"): "qk1", (5, "mid"): "qk2", (6, "mid"): "qk3",
                (7, "mid"): "v0", (8, "mid"): "v1"}
        OUTPUT = {(2, "end"): "y0", (3, "mid"): "y1", (3, "end"): "out0", (4, "mid"): "out1"}
        IN_ORDER = lambda place: (place[0], place[1] == "end")

        class Slot:

            def __init__(self, b, t, start, first=False, prep=False, output=False, last=False):
                self.b, self.t, self.G, self.start, self.first, self.prep, self.output = b, t, b * QUADS + t, start, first, prep, output
                self.more1, self.more2 = not (last and t == QUADS - 1), not (last and t >= QUADS - 2)
                places = {**COMMON, **(PREP if prep else {}), **(OUTPUT if output else {})}
                absent = (["o1"] if first else []) + ([] if self.more2 else ["k", "q1"]) + ([] if self.more1 else ["q2"])
                self.uses = {place: places[place] for place in sorted(places, key=IN_ORDER) if places[place] not in absent}

            def count(self, use):
                return self.start + list(self.uses.values()).index(use)

            def maxima_of(self, n):
                if n < STEPS - LEAD:
                    return (self.G + 1, (self.t + 1) % QUADS, n + LEAD) if self.more1 else None
                return (self.G + 2, (self.t + 2) % QUADS, n + LEAD - STEPS) if self.more2 else None

        FIRST_USES = ["x0", "x1", "qk0", "qk1", "qk2", "qk3", "v0", "v1", "k", "q1", "k next", "q1 next", "q2"]
        first_count = FIRST_USES.index
        first_slot = Slot(0, 0, len(FIRST_USES), first=True)
        AHEAD = len(FIRST_USES) + len(first_slot.uses)

        def batch_slots(b, last=False, body=None):
            slots = []
            start = AHEAD + b * (BODY if body is None else body)
            for t in range(1, QUADS):
                slots.append(Slot(b, t, start, prep=(t == 1 and not last), last=last))
                start = start + len(slots[-1].uses)
            if not last:
                slots.append(Slot(b + 1, 0, start, output=True))
            return slots

        BODY = sum(len(slot.uses) for slot in batch_slots(0, body=0))
        TAIL_USES = ["o1", "y0", "y1", "out0", "out1"]
        last_slots = batch_slots(BATCH - 1, last=True)
        tail_count = lambda use: last_slots[-1].start + len(last_slots[-1].uses) + TAIL_USES.index(use)

        SETUP = 4
        block = ctx.enter_context(nc.Block())

        def wait(engine, semaphore, value):
            engine.wait_ge(semaphore, value)
            engine.sem_inc(waits_passed, 1)

        @block.sync
        def _(sp):
            for count in (misc_free, o_copied):
                sp.sem_inc(count, 1)
            batch = lambda x, b: x[bass.ds(b, 1)].rearrange("a (j p) d -> p (a j) d", p=P)
            sp.dma_start(xb[:], batch(x_in, 0)).then_inc(x_loaded, 16)
            for dst, src in ((wqkv[:], w_qkv), (wo[:], w_o), (bias[:], b_qkv.broadcast_to([P, 3 * D])), (bo[:], b_o.broadcast_to([P, D])),
                             (ident[:], consts["ident"]), (mask_f[:], consts["mask"]), (cs[:], consts["cs"])):
                sp.dma_start(dst, src).then_inc(weights_in, 16)
            sp.dma_start(res[:], batch(x_in, 0)).then_inc(res_loaded, 16)

            def place_keys(count, t):
                wait(sp, misc_free, 1 + count + 1)
                for h in range(QUAD):
                    rows = slice(32 * h, 32 * h + 32)
                    sp.dma_start(kT[t][h][rows, :], kT_all[rows, :]).then_inc(k_placed, 16)

            sp.wait_ge(setup, SETUP)
            place_keys(first_count("k"), 0)
            place_keys(first_count("k next"), 1)
            place_keys(first_slot.count("k"), 2)
            with sp.Fori(0, BATCH - 1) as b:
                wait(sp, xn_done, b + 1)
                sp.dma_start(xb[:], batch(x_in, b + 1)).then_inc(x_loaded, 16)
                for S in batch_slots(b):
                    if S.output:
                        wait(sp, out_done, 2 * b + 2)
                        sp.dma_start(batch(x_out, b), res[:]).then_inc(x_stored, 16)
                    place_keys(S.count("k"), (S.t + 2) % QUADS)
                wait(sp, x_stored, b * 16 + 16)
                sp.dma_start(res[:], batch(x_in, b + 1)).then_inc(res_loaded, 16)
            for S in last_slots:
                if S.more2:
                    place_keys(S.count("k"), (S.t + 2) % QUADS)
            sp.wait_ge(out_done, 2 * BATCH)
            sp.dma_start(batch(x_out, BATCH - 1), res[:]).then_inc(x_stored, 16)
            sp.wait_ge(x_stored, BATCH * 16)

        def rotate(engine, k):
            even = qkv[:, :, 128 * k:128 * k + 64].rearrange("p j (h r) -> p j h r", r=ROT)
            odd = qkv[:, :, 128 * k + 64:128 * k + 128].rearrange("p j (h r) -> p j h r", r=ROT)
            for t, half, factor in ((turned[k], even, cs[:, :, 0]), (turned2[k], odd, cs[:, :, 1])):
                engine.tensor_tensor(t[:].rearrange("p (j h) r -> p j h r", h=HEADS), half, factor.unsqueeze(2).broadcast_to([P, TILES, HEADS, ROT]), ALU.mult)

        def split(engine, k, n):
            rest = turned2[k] if n == 0 else parts[k][:, :, n - 1]
            engine.drain()
            engine.tensor_tensor(turned[k][:], turned[k][:], rest[:] if n == 0 else rest, ALU.subtract)
            engine.drain()
            return engine.tensor_copy(parts[k][:, :, n], turned[k][:])

        @block.gpsimd
        def _(pool):
            pool.memset(negh[:], -0.5).then_inc(setup, 1)
            pool.memset(v1[:], 0.0).then_inc(setup, 1)
            pool.memset(q_rows[:], 0.0)
            for rows in qm_rows:
                pool.memset(rows[:], 0.0)
            for s in range(QUADS):
                for h in range(QUAD):
                    pool.memset(kT[s][h][:], 0.0)
            pool.drain()
            pool.memset(k_rows[:], 0.0)
            pool.drain()
            pool.wait_ge(setup, 2)
            pool.memset(v1[:, :, HS:HS + 1], 1.0).then_inc(setup, 1)
            pool.memset(k_rows[:, :, 24:27], 1.0).then_inc(setup, 1)
            pool.wait_ge(setup, SETUP)

            def rsqrt(batch):
                wait(pool, stats_done, batch + 1)
                nc.gpsimd.tensor_scalar(vareps[:], mv[:, :, 1], LN_EPS, None, ALU.add)
                pool.drain()
                nc.gpsimd.tensor_tensor(rstd[:], vareps[:], negh[:], ALU.pow).then_inc(rstd_done, 1)

            def copy_queries(G, t):
                of_quad = q_rows[:].rearrange("p (j h) r -> p j h r", h=HEADS)[:, :, QUAD * t:QUAD * (t + 1), 0:24]
                nc.gpsimd.tensor_copy(qm_rows[t % 2][:, :, :, 0:24], of_quad).then_inc(q_copied, 1)

            def stack_maxima(G, t):
                wait(pool, quad_max, G + 1)
                source = nm
                for n in range(3):
                    place = qm_rows[t % 2][:, :, :, 24 + n]
                    nc.gpsimd.tensor_copy(place, source[:])
                    pool.drain()
                    if n < 2:
                        nc.gpsimd.tensor_tensor(nm2[:], source[:], place, ALU.subtract)
                        pool.drain()
                        source = nm2
                pool.engine_nop().then_inc(max_stacked, 1)

            def add_output_bias(batch):
                wait(pool, res_loaded, batch * 16 + 16)
                nc.gpsimd.tensor_tensor(res[:], res[:], bo[:].unsqueeze(1).broadcast_to([P, TILES, D]), ALU.add).then_inc(res_biased, 1)

            def slot(S):
                if S.prep:
                    rsqrt(S.b + 1)
                if S.more2:
                    if S.t == 2:
                        wait(pool, q_stacked, S.b + 2)
                    wait(pool, misc_full, S.start)
                    copy_queries(S.G + 2, (S.t + 2) % QUADS)
                if S.prep:
                    wait(pool, misc_free, 1 + S.count("qk3") + 1)
                    rotate(nc.gpsimd, 1)
                if S.more1:
                    stack_maxima(S.G + 1, (S.t + 1) % QUADS)
                if S.prep:
                    for n in range(3):
                        last = split(nc.gpsimd, 1, n)
                    last.then_inc(k_split, 1)
                if S.t == 1:
                    add_output_bias(S.b)

            rsqrt(0)
            pool.wait_ge(misc_free, 1 + first_count("qk3") + 1)
            rotate(nc.gpsimd, 1)
            for n in range(3):
                last = split(nc.gpsimd, 1, n)
            last.then_inc(k_split, 1)
            pool.wait_ge(q_stacked, 1)
            copy_queries(0, 0)
            copy_queries(1, 1)
            stack_maxima(0, 0)
            slot(first_slot)
            with pool.Fori(0, BATCH - 1) as b:
                for S in batch_slots(b):
                    slot(S)
            for S in last_slots:
                slot(S)

        @block.scalar
        def _(act):
            act.wait_ge(weights_in, 7 * 16)
            nc.scalar.activation(identb[:], ident[:], ACT.Copy).then_inc(casts, 1)
            nc.scalar.activation(mask[:], mask_f[:], ACT.Copy).then_inc(casts, 1)
            act.wait_ge(setup, SETUP)

            def from_misc(count, dst, source=psm):
                act.wait_ge(misc_full, count + 1)
                nc.scalar.activation(dst, source, ACT.Copy).then_inc(misc_free, 1)

            def keys_from_misc(count, G):
                if G is not None:
                    act.wait_ge(k_placed, G * (QUAD * 16))
                act.wait_ge(misc_full, count + 1)
                nc.scalar.activation(kT_all[:], psm_b, ACT.Copy).then_inc(misc_free, 1)

            def evacuate(use, count, t, G):
                if use == "k":
                    keys_from_misc(count, G + 2)
                if use == "q1":
                    from_misc(count, q1T[t % 2][:], psm_b)
                if use == "q2":
                    from_misc(count, q2T[(t + 1) % 2][:], psm_b)
                if use in ("x0", "x1", "y0", "y1"):
                    half = slice(512 * int(use[1]), 512 * int(use[1]) + 512)
                    from_misc(count, (xT if use[0] == "x" else yT)[:, half], psm[:])

            def stack_queries(n):
                first, last = ((0, 3), (3, 5), (5, 6))[n]
                return nc.scalar.activation(q_rows[:, :, ROT * first:ROT * last].rearrange("p a (n r) -> p a n r", r=ROT),
                                            parts[0][:, :, n].unsqueeze(2).broadcast_to([P, JH, last - first, ROT]), ACT.Copy)

            def stack_keys(n):
                first, last = ((0, 3), (3, 5), (5, 6))[n]
                return nc.scalar.activation(k_rows[:, :, ROT * first:ROT * last].rearrange("p a (n r) -> p a n r", r=ROT),
                                            parts[1][:, :, 0:last - first], ACT.Copy)

            def place_values(batch):
                nc.scalar.activation(v1[:].rearrange("p (j h) r -> p j h r", h=HEADS)[:, :, :, 0:HS],
                                     qkv[:, :, 2 * D:3 * D].rearrange("p j (h r) -> p j h r", r=HS), ACT.Copy).then_inc(v_placed, 1)

            def copy_output(G, c):
                act.wait_ge(pv_done, G * STEPS + (STEPS if c else 4))
                nc.scalar.activation(oT[:, c], pso[:], ACT.Copy).then_inc(o_copied, 1)

            def exponential(G, n, pair):
                c, i = EXP_STEPS[n]
                size = 512 - max(0, i - 4 * c) * P
                act.wait_ge(s2_done, G * (2 * STEPS) + (2 * n + pair) + 1)
                nc.scalar.activation(prob[(2 * n + pair) % 4][:, :, 0:size], ps2[pair][:, :, 0:size], ACT.Exp, scale=SCORE_SCALE).then_inc(exp_done, 1)

            def slot(S):
                for n in range(STEPS):
                    exponential(S.G, n, 0)
                    if (n - 1, "end") in S.uses:
                        evacuate(S.uses[n - 1, "end"], S.count(S.uses[n - 1, "end"]), S.t, S.G)
                    exponential(S.G, n, 1)
                    if n == 0 and not S.first:
                        copy_output(S.G - 1, 1)
                    if n == 0 and S.t == 0:
                        act.wait_ge(misc_free, 1 + S.start)
                        place_values(S.b)
                    if n == LEAD + 1:
                        copy_output(S.G, 0)
                    if (n, "mid") in S.uses:
                        evacuate(S.uses[n, "mid"], S.count(S.uses[n, "mid"]), S.t, S.G)
                    if S.prep and n == STEPS - 1:
                        act.wait_ge(q_copied, S.G + 3)
                        act.wait_ge(q_split, S.b + 2)
                        stack_queries(0)
                    if S.t == 2 and S.more2 and n == 0:
                        stack_queries(1)
                        stack_queries(2).then_inc(q_stacked, 1)
                    if S.t == 2 and S.more2 and 1 <= n <= 3:
                        if n == 1:
                            act.wait_ge(k_split, S.b + 2)
                        last = stack_keys(n - 1)
                        if n == 3:
                            last.then_inc(k_stacked, 1)

            for use in ("x0", "x1"):
                evacuate(use, first_count(use), 0, 0)
            act.wait_ge(q_split, 1)
            stack_queries(0)
            stack_queries(1)
            stack_queries(2).then_inc(q_stacked, 1)
            act.wait_ge(k_split, 1)
            stack_keys(0)
            stack_keys(1)
            stack_keys(2).then_inc(k_stacked, 1)
            keys_from_misc(first_count("k"), None)
            from_misc(first_count("q1"), q1T[0][:], psm_b)
            keys_from_misc(first_count("k next"), 1)
            from_misc(first_count("q1 next"), q1T[1][:], psm_b)
            from_misc(first_count("q2"), q2T[0][:], psm_b)
            slot(first_slot)
            with act.Fori(0, BATCH - 1) as b:
                for S in batch_slots(b):
                    slot(S)
            for S in last_slots:
                slot(S)
            copy_output(QUADS * BATCH - 1, 1)
            for use in ("y0", "y1"):
                evacuate(use, tail_count(use), 0, 0)

        @block.tensor
        def _(pe):
            def to_misc(count, rows):
                pe.wait_ge(misc_free, 1 + count)
                for j in range(TILES):
                    last = nc.tensor.transpose(psm_b[:, j * P:(j + 1) * P], rows(j), identb[:])
                last.then_inc(misc_full, 1)

            def quad_rows(rows, t):
                return lambda j: rows[:].rearrange("p (j h) r -> p j (h r)", h=HEADS)[:, j, P * t:P * (t + 1)]

            def quad_rows_with_maxima(t):
                return lambda j: qm_rows[t % 2][:, j].rearrange("p h r -> p (h r)")

            def produce(use, count, t, G):
                if use == "k":
                    to_misc(count, quad_rows(k_rows, (t + 2) % QUADS))
                elif use == "q1":
                    to_misc(count, quad_rows(q_rows, (t + 2) % QUADS))
                elif use == "q2":
                    pe.wait_ge(max_stacked, G + 2)
                    to_misc(count, quad_rows_with_maxima(t + 1))
                elif use[0] == "o" and use[1:] in "01":
                    c = int(use[1])
                    pe.wait_ge(o_copied, 1 + (G * 2 + 1 if c == 0 else G * 2))
                    pe.wait_ge(misc_free, 1 + count)
                    for j in range(4):
                        last = nc.tensor.transpose(psm[:, j * P:(j + 1) * P], oT[:, c, j * P:(j + 1) * P], ident[:])
                    last.then_inc(misc_full, 1)
                else:
                    pe.wait_ge(misc_free, 1 + count)
                    n = int(use[-1])
                    for j in range(4):
                        out = psm[:, j * P:(j + 1) * P]
                        if use[0] in "xy":
                            last = nc.tensor.transpose(out, (xn if use[0] == "x" else y)[:, 4 * n + j], ident[:])
                        elif use[0] == "o":
                            last = nc.tensor.matmul(out, yT[:, (4 * n + j) * P:(4 * n + j + 1) * P], wo[:], start=True, stop=True)
                        elif use[0] == "v":
                            last = nc.tensor.matmul(out, xT[:, (4 * n + j) * P:(4 * n + j + 1) * P], wqkv[:, 2 * D:3 * D], start=True, stop=True)
                        elif j < 2:
                            last = nc.tensor.matmul(psm[:, j * 2 * D:(j + 1) * 2 * D], xT[:, (2 * n + j) * P:(2 * n + j + 1) * P], wqkv[:, 0:2 * D],
                                                    start=True, stop=True)
                    last.then_inc(misc_full, 1)

            def max_step(G, t, n, heads=range(QUAD)):
                j, c = MAX_STEPS[n]
                size = min(512, P * (j + 1) - 512 * c)
                for h in heads:
                    u = G * (STEPS * QUAD) + (n * QUAD + h)
                    out = ps1[(n * QUAD + h) % 2]
                    diagonal = P * (j + 1) == 512 * c + size
                    pe.wait_ge(max_done, u + 1)
                    last = nc.tensor.matmul(out[:, 0:size], q1T[t % 2][:, j * P:(j + 1) * P], kT[t][h][:, 512 * c:512 * c + size],
                                            start=True, stop=not diagonal)
                    if diagonal:
                        last = nc.tensor.matmul(out[:, size - P:size], identb[:], mask[:, 0], start=False, stop=True)
                    last.then_inc(s1_done, 1)

            def exp_step(G, t, n, pair):
                c, i = EXP_STEPS[n]
                first = max(512 * c, P * i)
                size = 512 * (c + 1) - first
                pe.wait_ge(exp_done, G * (2 * STEPS) + (2 * n + pair) + 1)
                for h in range(2):
                    last = nc.tensor.matmul(ps2[pair][:, h, 0:size], kT[t][2 * pair + h][:, i * P:(i + 1) * P], q2T[t % 2][:, first:first + size],
                                            start=True, stop=(i < 4 * c))
                    if i >= 4 * c:
                        last = nc.tensor.matmul(ps2[pair][:, h, 0:P], identb[:], mask[:, 1], start=False, stop=True)
                last.then_inc(s2_done, 1)

            def value_step(G, t, n):
                c, i = EXP_STEPS[n]
                first = max(0, P * i - 512 * c)
                pe.wait_ge(exp_done, G * (2 * STEPS) + 2 * (n + 1) + BUFFERS)
                if i == 0:
                    pe.wait_ge(o_copied, 1 + G * 2 + c)
                for h in range(QUAD):
                    last = nc.tensor.matmul(pso[32 * h:32 * h + 32, first:512], v1[:, i * HEADS + QUAD * t + h, :],
                                            prob[(2 * n + h // 2) % 4][:, h % 2, 0:512 - first], start=(i == 0), stop=(i == 4 * c + 3))
                last.then_inc(pv_done, 1)

            def serve(S, use):
                if use == "x0":
                    pe.wait_ge(xn_done, S.b + 2)
                if use == "k" and S.t == 2:
                    pe.wait_ge(k_stacked, S.b + 2)
                    pe.wait_ge(q_stacked, S.b + 2)
                produce(use, S.count(use), S.t, S.G)

            def slot(S):
                pe.wait_ge(misc_free, 1 + S.start)
                for n in range(STEPS):
                    quad = S.maxima_of(n)
                    if quad and n == STEPS - LEAD:
                        pe.wait_ge(misc_free, 1 + S.count("q1") + 1)
                        pe.wait_ge(k_placed, (S.G + 3) * (QUAD * 16))
                    if quad:
                        max_step(*quad, [0])
                    exp_step(S.G, S.t, n, 0)
                    if quad:
                        max_step(*quad, [1])
                    exp_step(S.G, S.t, n, 1)
                    if quad:
                        max_step(*quad, [2])
                    if (n, "mid") in S.uses:
                        serve(S, S.uses[n, "mid"])
                    if n >= 1:
                        if n == 1 and S.t == 0:
                            pe.wait_ge(v_placed, S.b + 1)
                        value_step(S.G, S.t, n - 1)
                    elif not S.first:
                        value_step(S.G - 1, (S.t - 1) % QUADS, STEPS - 1)
                    if quad:
                        max_step(*quad, [3])
                    if (n, "end") in S.uses:
                        serve(S, S.uses[n, "end"])

            pe.wait_ge(xn_done, 1)
            for use in FIRST_USES[0:first_count("k")]:
                produce(use, first_count(use), 0, 0)
            pe.wait_ge(q_stacked, 1)
            pe.wait_ge(k_stacked, 1)
            to_misc(first_count("k"), quad_rows(k_rows, 0))
            to_misc(first_count("q1"), quad_rows(q_rows, 0))
            pe.wait_ge(misc_free, 1 + first_count("q1") + 1)
            pe.wait_ge(k_placed, QUAD * 16)
            for n in range(STEPS):
                max_step(0, 0, n)
                if n == 5:
                    to_misc(first_count("k next"), quad_rows(k_rows, 1))
                if n == 6:
                    to_misc(first_count("q1 next"), quad_rows(q_rows, 1))
            pe.wait_ge(misc_free, 1 + first_count("q1 next") + 1)
            pe.wait_ge(k_placed, 2 * QUAD * 16)
            for n in range(LEAD):
                max_step(1, 1, n)
            pe.wait_ge(max_stacked, 1)
            to_misc(first_count("q2"), quad_rows_with_maxima(0))
            slot(first_slot)
            with pe.Fori(0, BATCH - 1) as b:
                for S in batch_slots(b):
                    slot(S)
            for S in last_slots:
                slot(S)
            value_step(QUADS * BATCH - 1, QUADS - 1, STEPS - 1)
            for use in TAIL_USES:
                produce(use, tail_count(use), 0, QUADS * BATCH)

        @block.vector
        def _(dve):
            def maxima(G, t, n, heads=range(QUAD)):
                j, c = MAX_STEPS[n]
                size = min(512, P * (j + 1) - 512 * c)
                for h in heads:
                    dve.wait_ge(s1_done, G * (STEPS * QUAD) + (n * QUAD + h + 1))
                    nc.vector.reduce_max(mx[:, c, j, h:h + 1], ps1[(n * QUAD + h) % 2][:, 0:size], AX.X).then_inc(max_done, 1)

            def negate_maxima(G, first=False):
                dve.drain()
                nc.vector.tensor_tensor(mx[:, 0, 4:8], mx[:, 0, 4:8], mx[:, 1, 4:8], ALU.max)
                if not first:
                    wait(dve, max_stacked, G)
                dve.drain()
                nc.vector.tensor_scalar(nm[:], mx[:, 0], -1.0, None, ALU.mult).then_inc(quad_max, 1)
                dve.drain()

            def statistics(batch):
                dve.wait_ge(x_loaded, batch * 16 + 16)
                for j in range(TILES):
                    nc.vector.bn_stats(stats[:, j], xb[:, j])
                dve.drain()
                for j in range(TILES):
                    last = nc.vector.bn_aggr(mv[:, j], stats[:, j])
                last.then_inc(stats_done, 1)

            def normalize(batch):
                dve.wait_ge(rstd_done, batch + 1)
                for j in range(TILES):
                    last = nc.vector.tensor_scalar(xn[:, j], xb[:, j], mv[:, j, 0:1], rstd[:, j:j + 1], ALU.subtract, ALU.mult)
                last.then_inc(xn_done, 1)

            def consume(use, count, t, batch):
                n = int(use[-1]) if use[-1] in "0123" else 0
                if use in ("o0", "o1"):
                    heads = psm[:].rearrange("p (j h r) -> p j h r", h=QUAD, r=32)
                    quad = (t - n) % QUADS
                    dve.wait_ge(misc_full, count + 1)
                    nc.vector.reciprocal(rden[:], heads[:, :, :, HS])
                    dve.drain()
                    nc.vector.tensor_tensor(y[:, 4 * n:4 * n + 4, 32 * quad:32 * quad + 32].rearrange("p j (h r) -> p j h r", r=HS), heads[:, :, :, 0:HS],
                                            rden[:].unsqueeze(3).broadcast_to([P, 4, QUAD, HS]), ALU.mult).then_inc(misc_free, 1)
                elif use[0:2] == "qk":
                    dve.wait_ge(misc_full, count + 1)
                    nc.vector.tensor_tensor(qkv[:, 2 * n:2 * n + 2, 0:2 * D], psm[:].rearrange("p (j d) -> p j d", j=2),
                                            bias[:, 0:2 * D].unsqueeze(1).broadcast_to([P, 2, 2 * D]), ALU.add).then_inc(misc_free, 1)
                elif use[0] == "v":
                    dve.wait_ge(misc_full, count + 1)
                    nc.vector.tensor_tensor(qkv[:, 4 * n:4 * n + 4, 2 * D:3 * D], psm[:].rearrange("p (j d) -> p j d", j=4),
                                            bias[:, 2 * D:3 * D].unsqueeze(1).broadcast_to([P, 4, D]), ALU.add).then_inc(misc_free, 1)
                elif use[0:3] == "out":
                    if n == 0:
                        dve.wait_ge(res_biased, batch + 1)
                    dve.wait_ge(misc_full, count + 1)
                    nc.vector.tensor_tensor(res[:, 4 * n:4 * n + 4], res[:, 4 * n:4 * n + 4], psm[:].rearrange("p (j d) -> p j d", j=4), ALU.add).then_inc(misc_free, 1)
                    dve.drain()
                    nc.vector.engine_nop().then_inc(out_done, 1)

            def slot(S):
                for n in range(STEPS):
                    quad = S.maxima_of(n)
                    if quad:
                        maxima(*quad, [0])
                    if (n - 1, "end") in S.uses:
                        use = S.uses[n - 1, "end"]
                        consume(use, S.count(use), S.t, S.b - 1)
                    if quad:
                        maxima(*quad, [1, 2])
                    if (n, "mid") in S.uses:
                        consume(S.uses[n, "mid"], S.count(S.uses[n, "mid"]), S.t, S.b - 1)
                    if quad:
                        maxima(*quad, [3])
                    if n == STEPS - LEAD - 1 and S.more1:
                        negate_maxima(S.G + 1)
                    if S.prep and n == 0:
                        statistics(S.b + 1)
                    if S.prep and n == 2:
                        normalize(S.b + 1)
                    if S.prep and n == 7:
                        dve.drain()
                        rotate(nc.vector, 0)
                    if S.prep and 8 <= n <= 10:
                        last = split(nc.vector, 0, n - 8)
                        if n == 10:
                            last.then_inc(q_split, 1)

            dve.wait_ge(weights_in, 7 * 16)
            dve.wait_ge(setup, SETUP)
            nc.vector.engine_nop().then_inc(exp_done, BUFFERS)
            nc.vector.engine_nop().then_inc(max_done, BUFFERS)
            statistics(0)
            normalize(0)
            for use in FIRST_USES[0:first_count("k")]:
                consume(use, first_count(use), 0, 0)
            dve.drain()
            rotate(nc.vector, 0)
            for n in range(3):
                last = split(nc.vector, 0, n)
            last.then_inc(q_split, 1)
            for n in range(STEPS):
                maxima(0, 0, n)
            negate_maxima(0, first=True)
            for n in range(LEAD):
                maxima(1, 1, n)
            slot(first_slot)
            with dve.Fori(0, BATCH - 1) as b:
                for S in batch_slots(b):
                    slot(S)
            for S in last_slots:
                slot(S)
            for use in TAIL_USES:
                consume(use, tail_count(use), 0, BATCH - 1)


def block(nc, x, out, fast_qkv, fast_norm, fast_lr_bias, fast_start, att_qkv, att_bias, att_out, att_out_bias,
          router, gate_proj, up_proj, down_proj, ident, block_ones, eye, tri, rev, mask, cs):
    consts = {"ident": ident, "block_ones": block_ones, "eye": eye, "tri": tri, "rev": rev, "mask": mask, "cs": cs}
    scratch = lambda n, shape: nc.dram_tensor(n, shape, F32, kind="Internal").ap()
    tok = scratch("tok", [CHUNKS, P, 2 * BATCH, 3 * D])
    turned = scratch("turned", [CHUNKS, P, BATCH, 3, CHUNK])
    x1, x2, x3 = (scratch(f"x{n}", [BATCH, SEQ, D]) for n in (1, 2, 3))
    groups = lambda t: t.rearrange("b (g n) d -> (b g) n d", n=GROUP)
    with ExitStack() as ctx:
        weights = expert_weights(nc, ctx, gate_proj, up_proj, down_proj)
        fast_weight_inputs(nc, x, tok, turned, fast_qkv, fast_lr_bias, fast_norm, consts, weights)
        fast_weight_stage(nc, x, x1, tok, turned, fast_start, consts)
        expert_stage(nc, "moe1", groups(x1), groups(x2), router, weights, consts)
        causal_attention_stage(nc, x2, x3, att_qkv, att_bias, att_out, att_out_bias, consts)
        expert_stage(nc, "moe2", groups(x3), groups(out), router, weights, consts)


def layouts(i):
    import numpy as np

    a = {k: np.asarray(v) for k, v in i.items()}
    c = lambda t: np.ascontiguousarray(t, dtype=t.dtype)

    def rope_halves(t):
        t = t.reshape(HEADS, HS, -1)
        return np.concatenate([t[:, ::2].reshape(HEADS * ROT, -1), t[:, 1::2].reshape(HEADS * ROT, -1)])

    def as_y(t):
        t = t.reshape(2, 2, FW_HID, FW_D).transpose(1, 2, 0, 3).reshape(P, 1, 2 * FW_D)
        return np.tile(t, (1, BATCH, 1)).reshape(P, -1)

    def as_x(t):
        return np.tile(t.reshape(P, 1, FW_HID), (1, BATCH, 1)).reshape(P, -1)

    return {
        "x": c(a["L0_attn_a_hidden_states"]),
        "fast_qkv": c(np.concatenate([a["L0_attn_a_qkv_w"], a["L0_attn_a_lr_proj_w"]]).T),
        "fast_norm": c(np.concatenate([a["L0_attn_a_q_norm_w"], a["L0_attn_a_k_norm_w"]])[None]),
        "fast_lr_bias": c(a["L0_attn_a_lr_proj_b"][None]),
        "fast_start": c(np.stack([as_y(a["L0_attn_a_w0"]), as_y(a["L0_attn_a_w2"]), as_x(a["L0_attn_a_w1"])], 1)),
        "att_qkv": c(np.concatenate([rope_halves(a["L0_attn_b_Wq"]), rope_halves(a["L0_attn_b_Wk"]), a["L0_attn_b_Wv"]]).T),
        "att_bias": c(np.concatenate([rope_halves(a["L0_attn_b_bq"])[:, 0], rope_halves(a["L0_attn_b_bk"])[:, 0], a["L0_attn_b_bv"]])[None]),
        "att_out": c(a["L0_attn_b_Wo"].T),
        "att_out_bias": c(a["L0_attn_b_bo"][None]),
        "router": c(a["L0_ffn_gate_w"].T),
        "gate_proj": c(a["L0_ffn_gate_proj_w"].transpose(2, 0, 1)),
        "up_proj": c(a["L0_ffn_up_proj_w"].transpose(2, 0, 1)),
        "down_proj": c(a["L0_ffn_down_proj_w"].reshape(EXPERTS, D, 2, P).transpose(3, 0, 2, 1)),
    }


def constants():
    import numpy as np

    f = np.float32
    row, col = np.arange(P)[:, None], np.arange(P)[None]
    block_ones = np.stack([row // FW_D == col // FW_D] + [row // FW_D == 2 * k + col // FW_HID for k in range(2)], 1)
    time, pair = np.arange(1, SEQ + 1, dtype=f)[:, None], np.arange(ROT, dtype=f)
    angle = (time * (f(1.0 / 10000.0) ** (f(2.0) * pair / f(HS))).astype(f)).astype(f)
    cs = np.stack([np.cos(angle), np.sin(angle)], 1).astype(f).reshape(TILES, P, 2, ROT).transpose(1, 0, 2, 3)
    return {
        "ident": np.eye(P, dtype=f),
        "block_ones": block_ones.astype(f),
        "eye": np.tile(np.eye(FW_D, dtype=f), (P // FW_D, 1)),
        "tri": (row <= col).astype(f),
        "rev": np.tile(np.arange(EXPERTS, 0, -1, dtype=f), (P, GROUP // P, 1)),
        "mask": (np.stack([col > row, row > col], 1) * f(MASKED)).astype(f),
        "cs": np.ascontiguousarray(cs),
    }


def kernel(**inputs):
    import concourse.bacc as bacc
    from concourse.bass_utils import run_bass_kernel_spmd as run

    nc = bacc.Bacc("TRN2", target_bir_lowering=False, num_devices=1)
    arrays = {**layouts(inputs), **constants()}
    aps = {n: nc.dram_tensor(f"in_{n}", t.shape, mybir.dt.from_np(t.dtype), kind="ExternalInput").ap() for n, t in arrays.items()}
    out = nc.dram_tensor("out", (BATCH, SEQ, D), F32, kind="ExternalOutput").ap()
    block(nc, out=out, **aps)
    r = run(nc, [{f"in_{n}": t for n, t in arrays.items()}], core_ids=[0])
    return r.results[0]["out"]
```

```python
import concourse.bass as bass
from concourse import mybir
import math
from contextlib import ExitStack

F32, F32R, BF16 = mybir.dt.float32, mybir.dt.float32r, mybir.dt.bfloat16
ALU = mybir.AluOpType
ACT = mybir.ActivationFunctionType
AX = mybir.AxisListType

P = 128
BATCH, SEQ, D = 4, 1024, 128
TOKENS = BATCH * SEQ
LN_EPS = 1e-5
EXPERTS = 8
CAPACITY = int(1.25 * TOKENS / EXPERTS)
GROUP = 512

BUFFERS = 2
TILES = SEQ // P
HEADS, HS = 16, 8
ROT = HS // 2
QUAD = 4
SCORE_SCALE = float(HS) ** -0.5
FW_HEADS, FW_D, FW_HID = 4, 32, 64
CHUNK = 256
CHUNKS = SEQ // CHUNK
BASE_LR_INV = math.log(math.expm1(0.001))
NEWTON = ((4.0848, -6.8946, 2.927), (3.9505, -6.3029, 2.6377), (3.7418, -5.5913, 2.3037),
          (2.8769, -3.1427, 1.2046), (2.8366, -3.0525, 1.2012))
MASKED = -1e30


def fast_weight_inputs(nc, x_in, tok_out, t_out, w_in, lr_bias, norm_w, consts):
    ctx = ExitStack()
    with ctx:
        sb = lambda n, shape, dt=F32: ctx.enter_context(nc.sbuf_tensor(f"prep_{n}", shape, dt))
        ps = lambda n, shape: ctx.enter_context(nc.psum_tensor(f"prep_{n}", shape, F32))
        sem = lambda n: ctx.enter_context(nc.semaphore(f"prep_{n}"))
        W = 3 * D + 3 * FW_HEADS
        w = sb("w", [P, W])
        bias = sb("bias", [P, 3 * FW_HEADS])
        nw = sb("nw", [P, 2 * D])
        ident = sb("ident", [P, P])
        negh = sb("negh", [P, TILES * 2])
        xb = sb("xb", [P, TILES, D])
        stats = sb("stats", [P, TILES, 6])
        mv = sb("mv", [P, TILES, 2])
        vareps = sb("vareps", [P, TILES])
        rstd = sb("rstd", [P, TILES])
        xn = sb("xn", [P, TILES, D])
        xT = sb("xT", [P, SEQ])
        raw = [sb(f"raw{s}", [P, TILES, W]) for s in range(2)]
        raw_sq = sb("raw_sq", [P, TILES, 2 * D])
        qk = sb("qk", [P, TILES, 2 * D])
        qk_sq = sb("qk_sq", [P, TILES, 2 * D])
        qkn = sb("qkn", [P, TILES, 2 * D])
        ms = sb("ms", [P, TILES * 2])
        mse = sb("mse", [P, TILES * 2])
        rms = sb("rms", [P, TILES * 2])
        hs2 = sb("hs2", [P, TILES * 2, FW_HEADS])
        hn = sb("hn", [P, TILES * 2, FW_HEADS])
        factor = sb("factor", [P, TILES * 2, FW_HEADS])
        L = 3 * FW_HEADS
        z = sb("z", [P, TILES, L])
        za = sb("za", [P, TILES, L])
        u = sb("u", [P, TILES, L])
        y1 = sb("y1", [P, TILES, L])
        ln = sb("ln", [P, TILES, L])
        dd = sb("dd", [P, TILES, L])
        one = sb("one", [P, TILES, L])
        lr = sb("lr", [P, TILES, L])
        tok = sb("tok", [P, CHUNKS, 2, 3 * D])
        tT = sb("tT", [P, CHUNKS, 3, CHUNK])
        psT = [ps(f"psT{s}", [P, 2, 512]) for s in range(2)]
        psW = [ps(f"psW{s}", [P, 512]) for s in range(4)]

        weights_in, setup, waits_passed = sem("weights_in"), sem("setup"), sem("waits_passed")
        x_loaded, tok_stored, t_stored = sem("x_loaded"), sem("tok_stored"), sem("t_stored")
        stats_done, rstd_done, xn_done, xt_psum, xt_done = sem("stats_done"), sem("rstd_done"), sem("xn_done"), sem("xt_psum"), sem("xt_done")
        w_psum, raw_done = sem("w_psum"), sem("raw_done")
        raw_squares, qk_squares, raw_sums, qk_sums, rms_done, roots_done = (sem(n) for n in ("raw_squares", "qk_squares", "raw_sums", "qk_sums", "rms_done", "roots_done"))
        scaled, heads_done, z_done, u_done, y1_done, ln_done, lr_done, tok_done = (sem(n) for n in ("scaled", "heads_done", "z_done", "u_done", "y1_done", "ln_done", "lr_done", "tok_done"))
        t_psum, t_done = sem("t_psum"), sem("t_done")
        SETUP = 1
        block = ctx.enter_context(nc.Block())

        def wait(engine, semaphore, value):
            engine.wait_ge(semaphore, value)
            engine.sem_inc(waits_passed, 1)

        def batches(engine, body):
            with engine.Fori(0, BATCH // 2 - 1) as i:
                body(i * 2, 0, 2)
                body(i * 2 + 1, 1, 2)
            body(BATCH - 2, 0, 1)
            body(BATCH - 1, 1, 0)

        @block.sync
        def _(sp):
            for count in (tok_stored, t_stored, tok_done, t_done):
                sp.sem_inc(count, 1)

            sp.dma_start(xb[:], x_in[0:1].rearrange("a (j p) d -> p (a j) d", p=P)).then_inc(x_loaded, 16)
            for dst, src in ((w[:], w_in), (bias[:], lr_bias.broadcast_to([P, L])), (nw[:], norm_w.broadcast_to([P, 2 * D])), (ident[:], consts["ident"])):
                sp.dma_start(dst, src).then_inc(weights_in, 16)

            def batch(b, s, left):
                wait(sp, tok_done, 1 + b + 1)
                sp.dma_start(tok_out.rearrange("c p (b j) n -> b p c (j n)", b=BATCH)[bass.ds(b, 1)].rearrange("a p c n -> (a p) c n"),
                             tok[:].rearrange("p c j n -> p c (j n)")).then_inc(tok_stored, 16)
                wait(sp, t_done, 1 + (b + 1) * 3)
                sp.dma_start(t_out.rearrange("c p b k n -> b p c (k n)")[bass.ds(b, 1)].rearrange("a p c n -> (a p) c n"),
                             tT[:].rearrange("p c k n -> p c (k n)")).then_inc(t_stored, 16)

            batches(sp, batch)
            sp.wait_ge(tok_stored, 1 + BATCH * 16)
            sp.wait_ge(t_stored, 1 + BATCH * 16)

        @block.gpsimd
        def _(pool):
            pool.memset(negh[:], -0.5).then_inc(setup, 1)
            pool.wait_ge(setup, SETUP)

            def rsqrt(b):
                wait(pool, stats_done, b + 1)
                nc.gpsimd.tensor_scalar(vareps[:], mv[:, :, 1], LN_EPS, None, ALU.add)
                pool.drain()
                nc.gpsimd.tensor_tensor(rstd[:], vareps[:], negh[:, 0:TILES], ALU.pow).then_inc(rstd_done, 1)

            def batch(b, s, left):
                wait(pool, raw_sums, b + 1)
                nc.gpsimd.tensor_scalar(mse[:], ms[:], 1.0 / D, 1e-6, ALU.mult, ALU.add)
                pool.drain()
                nc.gpsimd.tensor_tensor(rms[:], mse[:], negh[:], ALU.pow).then_inc(rms_done, 1)
                if left > 1:
                    rsqrt(b + 2)
                wait(pool, lr_done, b + 1)
                wait(pool, tok_stored, 1 + b * 16)
                for source, n, i in ((raw[s][:, :, 2 * D:3 * D], 2, 1), (qkn[:, :, D:2 * D], 0, 0), (qkn[:, :, D:2 * D], 1, 2)):
                    if n == 0:
                        wait(pool, heads_done, b + 1)
                    rate = lr[:].rearrange("p j (h i) -> p j h i", i=3)[:, :, :, i].unsqueeze(3).broadcast_to([P, TILES, FW_HEADS, FW_D])
                    last = nc.gpsimd.tensor_tensor(tok[:].rearrange("p c j n -> p (c j) n")[:, :, n * D:(n + 1) * D].rearrange("p j (h d) -> p j h d", d=FW_D),
                                                   source.rearrange("p j (h d) -> p j h d", d=FW_D), rate, ALU.mult)
                last.then_inc(tok_done, 1)

            rsqrt(0)
            rsqrt(1)
            batches(pool, batch)

        @block.scalar
        def _(act):
            def load(b):
                wait(act, xn_done, b)
                act.dma_start(xb[:], x_in[bass.ds(b, 1)].rearrange("a (j p) d -> p (a j) d", p=P)).then_inc(x_loaded, 16)

            def copy_xt(b):
                act.wait_ge(xt_psum, b + 1)
                nc.scalar.activation(xT[:], psT[0][:].rearrange("p a n -> p (a n)"), ACT.Copy).then_inc(xt_done, 1)

            def copy_projections(b, s, tiles=range(TILES)):
                for j in tiles:
                    act.wait_ge(w_psum, b * TILES + (j + 1))
                    nc.scalar.activation(raw[s][:, j], psW[j % 4][:, 0:W], ACT.Copy).then_inc(raw_done, 1)

            def batch(b, s, left):
                if left > 1:
                    load(b + 2)
                act.drain()
                nc.scalar.activation(raw_sq[:], raw[s][:, :, 0:2 * D], ACT.Square).then_inc(raw_squares, 1)
                if left:
                    copy_xt(b + 1)
                act.wait_ge(scaled, b + 1)
                nc.scalar.activation(qk_sq[:], qk[:], ACT.Square).then_inc(qk_squares, 1)
                act.wait_ge(z_done, b + 1)
                nc.scalar.activation(u[:], za[:], ACT.Exp, scale=-1.0).then_inc(u_done, 1)
                act.wait_ge(y1_done, b + 1)
                nc.scalar.activation(ln[:], y1[:], ACT.Ln).then_inc(ln_done, 1)
                if left:
                    act.wait_ge(tok_done, 1 + b)
                    copy_projections(b + 1, 1 - s, range(4))
                act.wait_ge(qk_sums, b + 1)
                nc.scalar.activation(hn[:], hs2[:], ACT.Sqrt).then_inc(roots_done, 1)
                if left:
                    copy_projections(b + 1, 1 - s, range(4, TILES))
                act.wait_ge(t_stored, 1 + b * 16)
                for n, k in enumerate((2, 0, 1)):
                    act.wait_ge(t_psum, b * 3 + (n + 1))
                    nc.scalar.activation(tT[:, :, k], psT[(n + 1) % 2][:].rearrange("p a (c n) -> p (a c) n", n=CHUNK), ACT.Copy).then_inc(t_done, 1)

            load(1)
            act.wait_ge(weights_in, 4 * 16)
            copy_xt(0)
            copy_projections(0, 0)
            batches(act, batch)

        @block.tensor
        def _(pe):
            def transpose_all(out, source, done):
                for j in range(TILES):
                    last = nc.tensor.transpose(out[:, j // 4, (j % 4) * P:(j % 4 + 1) * P], source(j), ident[:])
                last.then_inc(done, 1)

            def project(b, started):
                pe.wait_ge(xn_done, b + 1)
                pe.wait_ge(t_done, 1 + started * 3)
                transpose_all(psT[0], lambda j: xn[:, j], xt_psum)
                pe.wait_ge(xt_done, b + 1)
                for j in range(TILES):
                    if j >= 4:
                        pe.wait_ge(raw_done, b * TILES + (j - 3))
                    nc.tensor.matmul(psW[j % 4][:, 0:W], xT[:, j * P:(j + 1) * P], w[:], start=True, stop=True).then_inc(w_psum, 1)

            def batch(b, s, left):
                if left:
                    project(b + 1, b)
                pe.wait_ge(t_done, 1 + b * 3)
                transpose_all(psT[1], lambda j: raw[s][:, j, 2 * D:3 * D], t_psum)
                pe.wait_ge(heads_done, b + 1)
                transpose_all(psT[0], lambda j: qkn[:, j, 0:D], t_psum)
                pe.wait_ge(t_done, 1 + b * 3 + 1)
                transpose_all(psT[1], lambda j: qkn[:, j, D:2 * D], t_psum)

            pe.wait_ge(weights_in, 4 * 16)
            project(0, 0)
            pe.wait_ge(raw_done, TILES)
            batches(pe, batch)

        @block.vector
        def _(dve):
            def statistics(b):
                dve.wait_ge(x_loaded, b * 16 + 16)
                for j in range(TILES):
                    nc.vector.bn_stats(stats[:, j], xb[:, j])
                dve.drain()
                for j in range(TILES):
                    last = nc.vector.bn_aggr(mv[:, j], stats[:, j])
                last.then_inc(stats_done, 1)

            def normalize(b, after_transposes=True):
                dve.wait_ge(rstd_done, b + 1)
                if after_transposes:
                    dve.wait_ge(xt_psum, b)
                for j in range(TILES):
                    last = nc.vector.tensor_scalar(xn[:, j], xb[:, j], mv[:, j, 0:1], rstd[:, j:j + 1], ALU.subtract, ALU.mult)
                last.then_inc(xn_done, 1)

            def batch(b, s, left):
                dve.wait_ge(raw_done, (b + 1) * TILES)
                nc.vector.tensor_tensor(z[:], raw[s][:, :, 3 * D:W], bias[:].unsqueeze(1).broadcast_to([P, TILES, L]), ALU.add)
                dve.drain()
                nc.vector.scalar_tensor_tensor(za[:], z[:], -1.0, z[:], ALU.mult, ALU.max).then_inc(z_done, 1)
                nc.vector.tensor_tensor(qk[:], raw[s][:, :, 0:2 * D], nw[:].unsqueeze(1).broadcast_to([P, TILES, 2 * D]), ALU.mult).then_inc(scaled, 1)
                dve.wait_ge(raw_squares, b + 1)
                nc.vector.reduce_sum(ms[:], raw_sq[:].rearrange("p j (k d) -> p (j k) d", d=D), AX.X).then_inc(raw_sums, 1)
                if left > 1:
                    statistics(b + 2)
                dve.wait_ge(qk_squares, b + 1)
                nc.vector.reduce_sum(hs2[:].rearrange("p a h -> p (a h)"), qk_sq[:].rearrange("p j (k d) -> p (j k) d", d=FW_D), AX.X).then_inc(qk_sums, 1)
                dve.wait_ge(u_done, b + 1)
                nc.vector.tensor_scalar(y1[:], u[:], 1.0, None, ALU.add).then_inc(y1_done, 1)
                dve.drain()
                nc.vector.tensor_scalar(dd[:], y1[:], -1.0, None, ALU.add)
                if left > 1:
                    normalize(b + 2)
                dve.drain()
                nc.vector.tensor_scalar(one[:], dd[:], 0.0, None, ALU.is_equal)
                wait(dve, ln_done, b + 1)
                dve.drain()
                nc.vector.tensor_tensor(dd[:], dd[:], one[:], ALU.add)
                nc.vector.tensor_tensor(ln[:], ln[:], one[:], ALU.add)
                dve.drain()
                nc.vector.reciprocal(dd[:], dd[:])
                nc.vector.tensor_tensor(ln[:], ln[:], u[:], ALU.mult)
                dve.drain()
                nc.vector.tensor_tensor(ln[:], ln[:], dd[:], ALU.mult)
                wait(dve, tok_done, 1 + b)
                wait(dve, t_done, 1 + b * 3)
                dve.drain()
                nc.vector.scalar_tensor_tensor(lr[:], z[:], 0.0, ln[:], ALU.max, ALU.add).then_inc(lr_done, 1)
                dve.wait_ge(roots_done, b + 1)
                dve.wait_ge(rms_done, b + 1)
                by_head = rms[:].unsqueeze(2).broadcast_to([P, TILES * 2, FW_HEADS])
                nc.vector.tensor_scalar(factor[:], hn[:], 1e-30, None, ALU.max)
                dve.drain()
                nc.vector.reciprocal(factor[:], factor[:])
                dve.drain()
                nc.vector.tensor_tensor(factor[:], factor[:], hs2[:], ALU.mult)
                dve.drain()
                nc.vector.tensor_tensor(factor[:], factor[:], hn[:], ALU.add)
                dve.drain()
                nc.vector.tensor_tensor(factor[:], factor[:], by_head, ALU.mult)
                dve.drain()
                nc.vector.tensor_scalar(factor[:], factor[:], 0.5, 1e-5, ALU.mult, ALU.add)
                dve.drain()
                nc.vector.reciprocal(factor[:], factor[:])
                dve.drain()
                nc.vector.tensor_tensor(factor[:], factor[:], by_head, ALU.mult)
                dve.drain()
                nc.vector.tensor_tensor(qkn[:].rearrange("p j (k d) -> p (j k) d", d=FW_D), qk[:].rearrange("p j (k d) -> p (j k) d", d=FW_D),
                                        factor[:].rearrange("p a h -> p (a h)").unsqueeze(2).broadcast_to([P, TILES * 2 * FW_HEADS, FW_D]), ALU.mult).then_inc(heads_done, 1)

            statistics(0)
            normalize(0, after_transposes=False)
            statistics(1)
            normalize(1)
            dve.wait_ge(weights_in, 4 * 16)
            nc.vector.tensor_scalar(bias[:], bias[:], BASE_LR_INV, None, ALU.add)
            dve.drain()
            batches(dve, batch)


def fast_weight_stage(nc, x_in, x_out, tok_in, t_in, w_start, consts, expert):
    H, HID, DH = FW_HEADS, FW_HID, FW_D
    ctx = ExitStack()
    with ctx:
        sb = lambda n, shape, dt=F32: ctx.enter_context(nc.sbuf_tensor(f"fw_{n}", shape, dt))
        sem = lambda n: ctx.enter_context(nc.semaphore(f"fw_{n}"))
        ident = sb("ident", [P, P])
        block_ones = sb("block_ones", [P, P])
        eyes = sb("eyes", [P, len(NEWTON), P])
        half = sb("half", [P, 20])
        state = sb("state", [P, 3, 256])
        norm0 = sb("norm0", [P, 20])
        tok = sb("tok", [P, 2 * BATCH, 3 * D])
        Tq = sb("Tq", [P, BATCH, CHUNK])
        Tkv = sb("Tkv", [P, BATCH, 2, CHUNK])
        xc = sb("xc", [P, 2 * BATCH, D])
        xo = sb("xo", [P, 2 * BATCH, D])
        wb = sb("wb", [P, BATCH, 3, 256])
        w1b = sb("w1b", [P, BATCH, 2, 2 * DH])
        two = lambda n: [sb(f"{n}{s}", [P, 2, 256]) for s in range(2)]
        th, hb, sig, sg, v, dgate, ds = (two(n) for n in ("th", "hb", "sig", "sg", "v", "dgate", "ds"))
        dhbm, hidden, dgba = ([sb(f"{n}{s}", [P, 2, 256]) for s in range(3)] for n in ("dhbm", "hidden", "dgba"))
        xr = sb("xr", [P, 3, BATCH, HID])
        X = sb("X", [P, 3, BATCH, HID])
        Y = [sb(f"Y{e}", [P, 3, BATCH // 2, P]) for e in range(2)]
        sq = sb("sq", [P, 768])
        rs = sb("rs", [P, 12])
        fro = sb("fro", [P, 12])
        froot = sb("froot", [P, 12])
        rn = sb("rn", [P, 12])
        A = [sb(f"A{g}", [P, BATCH, P]) for g in range(3)]
        T1 = [sb(f"T1{g}", [P, BATCH, P]) for g in range(3)]
        M = [sb(f"M{g}", [P, BATCH, P]) for g in range(3)]
        ssq = sb("ssq", [P, 20])
        wn = sb("wn", [P, 20])
        wf = sb("wf", [P, 20])
        qth = sb("qth", [P, 512])
        qgated = sb("qgated", [P, 512])
        prod = sb("prod", [P, 2, CHUNK])
        banks = ctx.enter_context(nc.psum_tensor("fw_banks", [P, 8, 512], F32))

        weights_in, setup, waits_passed = sem("weights_in"), sem("setup"), sem("waits_passed")
        tok_in_s, kv_in_s, q_in_s, x_in_s, x_stored = sem("tok_loaded"), sem("kv_loaded"), sem("q_loaded"), sem("x_loaded"), sem("x_stored")
        norm_sq, norm_root, state_done, turned = sem("norm_sq"), sem("norm_root"), sem("state_done"), sem("turned")
        wb_act, wb_dve = sem("wb_act"), sem("wb_dve")
        kv_psum, tanh_done, sg_done, v_done, dgate_done, back_dve, back_pool = (sem(n) for n in ("kv_psum", "tanh_done", "sg_done", "v_done", "dgate_done", "back_dve", "back_pool"))
        dw_psum, rs_done, fro_psum, fro_done, root_done, start_done = (sem(n) for n in ("dw_psum", "rs_done", "fro_psum", "fro_done", "root_done", "start_done"))
        a_psum, a_done, aa_psum, m_done, xy_psum, xy_done = (sem(n) for n in ("a_psum", "a_done", "aa_psum", "m_done", "xy_psum", "xy_done"))
        q_psum, qth_done, prod_done, o_psum, o_done = (sem(n) for n in ("q_psum", "qth_done", "prod_done", "o_psum", "o_done"))
        IT = len(NEWTON)
        QUERY_AT = {1: 1, 3: 2}
        BANKS = (0, 5)
        SETUP = 5
        block = ctx.enter_context(nc.Block())

        def quadrant(h):
            return slice(DH * h, DH * h + DH)

        def side(h):
            return slice(HID * (h % 2), HID * (h % 2) + HID)

        def wait(engine, semaphore, value):
            engine.wait_ge(semaphore, value)
            engine.sem_inc(waits_passed, 1)

        @block.sync
        def _(sp):
            for count in (x_stored, o_done):
                sp.sem_inc(count, 1)
            for dst, src in ((ident[:], consts["ident"]), (block_ones[:], consts["block_ones"]), (state[:], w_start)):
                sp.dma_start(dst, src).then_inc(weights_in, 16)

            def load_tok(c):
                sp.dma_start(tok[:], tok_in[bass.ds(c, 1)].rearrange("a p b n -> (a p) b n")).then_inc(tok_in_s, 16)

            def load_kv(c):
                sp.dma_start(Tkv[:], t_in[bass.ds(c, 1)].rearrange("a p b k n -> (a p) b k n")[:, :, 1:3]).then_inc(kv_in_s, 16)

            def load_q(c):
                sp.dma_start(Tq[:], t_in[bass.ds(c, 1)].rearrange("a p b k n -> (a p) b k n")[:, :, 0]).then_inc(q_in_s, 16)

            def load_x(c):
                for b in range(BATCH):
                    sp.dma_start(xc[:, 2 * b:2 * b + 2], x_in[b].rearrange("(c j p) d -> c p j d", c=CHUNKS, p=P)[bass.ds(c, 1)].rearrange("a p j d -> (a p) j d")).then_inc(x_in_s, 16)

            def store_x(c):
                wait(sp, o_done, 1 + (c + 1) * BATCH)
                for b in range(BATCH):
                    sp.dma_start(x_out[b].rearrange("(c j p) d -> c p j d", c=CHUNKS, p=P)[bass.ds(c, 1)].rearrange("a p j d -> (a p) j d"), xo[:, 2 * b:2 * b + 2]).then_inc(x_stored, 16)
                wait(sp, x_stored, 1 + (c + 1) * BATCH * 16)

            load_kv(0)
            load_tok(0)
            load_q(0)
            load_x(0)
            for dst, src in expert["loads"]:
                sp.dma_start(dst[:], src).then_inc(expert["loaded"], 16)
            with sp.Fori(0, CHUNKS - 1) as c:
                wait(sp, dw_psum, c + 1)
                load_kv(c + 1)
                load_tok(c + 1)
                store_x(c)
                load_q(c + 1)
                load_x(c + 1)
            store_x(CHUNKS - 1)

        def root_of_squares(norms):
            nc.gpsimd.tensor_tensor(norms[:], ssq[:], half[:], ALU.pow).then_inc(norm_root, 1)

        @block.gpsimd
        def _(pool):
            pool.memset(half[:], 0.5).then_inc(setup, 1)
            pool.wait_ge(setup, SETUP)
            pool.wait_ge(norm_sq, 1)
            root_of_squares(norm0)

            with pool.Fori(0, CHUNKS - 1) as c:
                for b in range(BATCH):
                    s = b % 2
                    wait(pool, sg_done, c * BATCH + b + 1)
                    nc.gpsimd.tensor_tensor(hidden[b % 3][:], sg[s][:], hb[s][:], ALU.mult)
                    wait(pool, v_done, c * BATCH + b + 1)
                    nc.gpsimd.tensor_tensor(ds[s][:], v[s][:], sig[s][:], ALU.mult)
                    wait(pool, dgate_done, c * BATCH + b + 1)
                    pool.drain()
                    nc.gpsimd.tensor_tensor(dgba[b % 3][:], ds[s][:], dgate[s][:], ALU.mult).then_inc(back_pool, 1)
                wait(pool, fro_done, c + 1)
                nc.gpsimd.tensor_tensor(froot[:], fro[:], half[:, 0:12], ALU.pow).then_inc(root_done, 1)
                wait(pool, norm_sq, c + 2)
                root_of_squares(wn)

        @block.scalar
        def _(act):
            act.wait_ge(setup, SETUP)
            act.wait_ge(weights_in, 3 * 16)

            def distribute(c):
                act.wait_ge(state_done, c + 1)
                for h in range(H):
                    nc.scalar.activation(wb[quadrant(h), :, 2, HID * h:HID * h + HID], state[quadrant(h), 2, :].rearrange("p (b n) -> p b n", b=BATCH), ACT.Copy)
                act.wait_ge(turned, c + 1)
                for h in range(H):
                    nc.scalar.activation(wb[quadrant(h), :, 0, HID * h:HID * h + HID], banks[quadrant(h), 0, 0:256].rearrange("p (b n) -> p b n", b=BATCH), ACT.Copy)
                for m in range(2):
                    last = nc.scalar.activation(w1b[side(m), :, 0, DH * m:DH * m + DH], banks[side(m), 2, 0:P].rearrange("p (b n) -> p b n", b=BATCH), ACT.Copy)
                last.then_inc(wb_act, 1)

            def query_tanh(c, b):
                act.wait_ge(q_psum, c * BATCH + b + 1)
                nc.scalar.activation(qth[:], banks[:, 6], ACT.Tanh, scale=0.5).then_inc(qth_done, 1)

            with act.Fori(0, CHUNKS - 1) as c:
                distribute(c)
                for b in range(BATCH):
                    s = b % 2
                    act.wait_ge(kv_psum, c * BATCH + b + 1)
                    if b >= 2:
                        act.wait_ge(back_pool, c * BATCH + b - 1)
                        act.wait_ge(back_dve, c * BATCH + b - 1)
                    gate_up = banks[:, BANKS[s]:BANKS[s] + 2]
                    nc.scalar.activation(th[s][:], gate_up[:, :, 0:256], ACT.Tanh, scale=0.5)
                    nc.scalar.activation(hb[s][:], gate_up[:, :, 256:512], ACT.Copy).then_inc(tanh_done, 1)
                query_tanh(c, 0)
                for it in range(IT):
                    for g in range(3):
                        act.wait_ge(xy_psum, c * (IT * 3 + 3) + it * 3 + g + 1)
                        if it > 0:
                            nc.scalar.activation(X[:, g], banks[:, 3 + g, 0:256].rearrange("p (b n) -> p b n", b=BATCH), ACT.Copy)
                        for e in range(2):
                            last = nc.scalar.activation(Y[e][side(e), g], banks[side(e), 3 + g, 256:512].rearrange("p (k n) -> p k n", k=2), ACT.Copy)
                        last.then_inc(xy_done, 1)
                    if it in QUERY_AT:
                        query_tanh(c, QUERY_AT[it])
                query_tanh(c, BATCH - 1)
            distribute(CHUNKS - 1)
            for b in range(BATCH):
                query_tanh(CHUNKS - 1, b)

        @block.tensor
        def _(pe):
            pe.wait_ge(setup, SETUP)
            pe.wait_ge(weights_in, 3 * 16)

            def turn_state(c):
                wait(pe, state_done, c + 1)
                for g in range(2):
                    for k in range(BATCH // 2):
                        nc.tensor.transpose(banks[:, g, P * k:P * k + P], state[:, g, P * k:P * k + P], ident[:])
                for b in range(BATCH):
                    for h in range(H):
                        last = nc.tensor.matmul(banks[side(h), 2 + h // 2, DH * b:DH * b + DH], state[quadrant(h), 2, HID * b:HID * b + HID], ident[quadrant(h), quadrant(h)], start=True, stop=True)
                last.then_inc(turned, 1)

            def backward(c, b):
                if b == 0:
                    for w in (wb_act, wb_dve):
                        pe.wait_ge(w, c + 1)
                    wait(pe, kv_in_s, (c + 1) * 16)
                if b == 1:
                    wait(pe, o_done, 1 + c * BATCH)
                if b >= 2:
                    wait(pe, dgate_done, c * BATCH + b - 1)
                first = BANKS[b % 2]
                for j in range(2):
                    nc.tensor.matmul(banks[:, first + j, :], Tkv[:, b, 0, j * P:(j + 1) * P], wb[:, b, 0:2, :], start=True, stop=True)
                    last = nc.tensor.matmul(banks[:, first + 2, 256 * j:256 * j + 256], Tkv[:, b, 1, j * P:(j + 1) * P], wb[:, b, 2, :], start=True, stop=True)
                last.then_inc(kv_psum, 1)

            def gradients(c, b):
                pe.wait_ge(back_dve, c * BATCH + b + 1)
                wait(pe, back_pool, c * BATCH + b + 1)
                if b == 0:
                    wait(pe, tok_in_s, (c + 1) * 16)
                for g, left in enumerate((dgba[b % 3], dhbm[b % 3], hidden[b % 3])):
                    for j in range(2):
                        for h in range(H):
                            out = banks[quadrant(h), 3, 256 * g + HID * b:256 * g + HID * (b + 1)] if g < 2 else banks[quadrant(h), 4, HID * b:HID * (b + 1)]
                            last = nc.tensor.matmul(out, tok[:, 2 * b + j, D * g + DH * h:D * g + DH * h + DH], left[:, j, HID * h:HID * h + HID],
                                                    start=(j == 0), stop=(j == 1))
                if b == BATCH - 1:
                    last.then_inc(dw_psum, 1)

            def query(c, b):
                if b == 0:
                    for w in (wb_act, wb_dve):
                        pe.wait_ge(w, c + 1)
                    pe.wait_ge(q_in_s, (c + 1) * 16)
                wait(pe, o_done, 1 + c * BATCH + b)
                for g in range(2):
                    for k in range(2):
                        last = nc.tensor.matmul(banks[:, 6 + g, CHUNK * k:CHUNK * (k + 1)], wb[:, b, g, P * k:P * k + P], Tq[:, b, :], start=True, stop=True)
                last.then_inc(q_psum, 1)

            def output(c, b):
                wait(pe, prod_done, c * BATCH + b + 1)
                for j in range(2):
                    for k in range(2):
                        last = nc.tensor.matmul(banks[:, 7, D * j + 2 * DH * k:D * j + 2 * DH * (k + 1)], prod[:, k, j * P:(j + 1) * P], w1b[:, b, k, :], start=True, stop=True)
                last.then_inc(o_psum, 1)

            def new_y(g, m):
                for b in range(BATCH):
                    k = 256 + P * (b // 2)
                    last = nc.tensor.matmul(banks[side(b), 3 + g, k:k + P], X[:, g, b, :], m(b), start=True, stop=True)
                return last

            with pe.Fori(0, CHUNKS - 1) as c:
                turn_state(c)
                for b in range(BATCH):
                    backward(c, b)
                    if b >= 2:
                        gradients(c, b - 2)
                gradients(c, BATCH - 2)
                gradients(c, BATCH - 1)
                wait(pe, rs_done, c + 1)
                nc.tensor.matmul(banks[:, 0, 0:12], block_ones[:], rs[:], start=True, stop=True).then_inc(fro_psum, 1)
                query(c, 0)
                output(c, 0)
                wait(pe, start_done, c + 1)
                for g in range(3):
                    new_y(g, lambda b: ident[:]).then_inc(xy_psum, 1)
                for it in range(IT):
                    step = (c * IT + it) * 3
                    for g in range(3):
                        wait(pe, xy_done, step + g + 1)
                        for b in range(BATCH):
                            y = Y[b % 2][:, g, b // 2, :]
                            last = nc.tensor.matmul(banks[:, g, P * b:P * b + P], y, y, start=True, stop=True)
                        last.then_inc(a_psum, 1)
                    if it in QUERY_AT:
                        query(c, QUERY_AT[it])
                    for g in range(3):
                        wait(pe, a_done, step + g + 1)
                        for b in range(BATCH):
                            last = nc.tensor.matmul(banks[:, g, P * b:P * b + P], A[g][:, b], A[g][:, b], start=True, stop=True)
                        last.then_inc(aa_psum, 1)
                    if it in QUERY_AT:
                        output(c, QUERY_AT[it])
                    for g in range(3):
                        wait(pe, m_done, step + g + 1)
                        if it < IT - 1 or g == 2:
                            for b in range(BATCH):
                                last = nc.tensor.matmul(banks[:, 3 + g, HID * b:HID * b + HID], M[g][:, b], X[:, g, b, :], start=True, stop=True)
                        if it < IT - 1 or g < 2:
                            last = new_y(g, lambda b: M[g][:, b])
                        last.then_inc(xy_psum, 1)
                query(c, BATCH - 1)
                output(c, BATCH - 1)
            turn_state(CHUNKS - 1)
            for b in range(BATCH):
                query(CHUNKS - 1, b)
                output(CHUNKS - 1, b)

        @block.vector
        def _(dve):
            for zeros in [wb, w1b] + Y:
                nc.vector.memset(zeros[:], 0.0).then_inc(setup, 1)
            dve.wait_ge(setup, SETUP)
            dve.wait_ge(weights_in, 3 * 16)

            def sum_state_squares():
                nc.vector.tensor_tensor(sq[:], state[:].rearrange("p g n -> p (g n)"), state[:].rearrange("p g n -> p (g n)"), ALU.mult)
                dve.drain()
                nc.vector.reduce_sum(ssq[:, 0:16], sq[:, 0:512].rearrange("p (a n) -> p a n", n=DH), AX.X)
                nc.vector.reduce_sum(ssq[:, 16:20], sq[:, 512:768].rearrange("p (a n) -> p a n", n=HID), AX.X).then_inc(norm_sq, 1)

            def distribute(c):
                dve.wait_ge(turned, c + 1)
                for h in range(H):
                    nc.vector.tensor_copy(wb[quadrant(h), :, 1, HID * h:HID * h + HID], banks[quadrant(h), 1, 0:256].rearrange("p (b n) -> p b n", b=BATCH))
                for m in range(2):
                    last = nc.vector.tensor_copy(w1b[side(m), :, 1, DH * m:DH * m + DH], banks[side(m), 3, 0:P].rearrange("p (b n) -> p b n", b=BATCH))
                last.then_inc(wb_dve, 1)

            def query_product(c, b):
                dve.wait_ge(qth_done, c * BATCH + b + 1)
                nc.vector.scalar_tensor_tensor(qgated[:], qth[:], 1.0, banks[:, 6], ALU.add, ALU.mult)
                dve.drain()
                nc.vector.tensor_tensor(prod[:].rearrange("p k n -> p (k n)"), qgated[:], banks[:, 7], ALU.mult).then_inc(prod_done, 1)

            def add_output(c, b):
                if b == 0:
                    dve.wait_ge(x_in_s, (c + 1) * BATCH * 16)
                    dve.wait_ge(x_stored, 1 + c * BATCH * 16)
                dve.wait_ge(o_psum, c * BATCH + b + 1)
                nc.vector.scalar_tensor_tensor(xo[:, 2 * b:2 * b + 2], banks[:, 7, 0:2 * D].rearrange("p (j d) -> p j d", d=D), 0.5, xc[:, 2 * b:2 * b + 2],
                                               ALU.mult, ALU.add).then_inc(o_done, 1)

            def keep_own(step, g):
                dve.wait_ge(a_psum, step + g + 1)
                nc.vector.tensor_tensor(A[g][:], banks[:, g].rearrange("p (b n) -> p b n", b=BATCH), block_ones[:].unsqueeze(1).broadcast_to([P, BATCH, P]),
                                        ALU.mult).then_inc(a_done, 1)

            def add_scaled(it, g):
                nc.vector.scalar_tensor_tensor(T1[g][:], A[g][:], NEWTON[it][1], eyes[:, it].unsqueeze(1).broadcast_to([P, BATCH, P]), ALU.mult, ALU.add)

            def polynomial(it, step, g):
                dve.wait_ge(aa_psum, step + g + 1)
                nc.vector.scalar_tensor_tensor(M[g][:], banks[:, g].rearrange("p (b n) -> p b n", b=BATCH), NEWTON[it][2], T1[g][:],
                                               ALU.mult, ALU.add).then_inc(m_done, 1)

            for n, (a, _, _) in enumerate(NEWTON):
                nc.vector.tensor_scalar(eyes[:, n], ident[:], a, None, ALU.mult)
            sum_state_squares()
            nc.vector.engine_nop().then_inc(state_done, 1)

            with dve.Fori(0, CHUNKS - 1) as c:
                distribute(c)
                for b in range(BATCH):
                    s = b % 2
                    dve.wait_ge(tanh_done, c * BATCH + b + 1)
                    gba, dhid = banks[:, BANKS[s]:BANKS[s] + 2, 0:256], banks[:, BANKS[s] + 2].rearrange("p (j n) -> p j n", j=2)
                    nc.vector.tensor_scalar(sig[s][:], th[s][:], 0.5, 0.5, ALU.mult, ALU.add)
                    dve.drain()
                    nc.vector.tensor_tensor(sg[s][:], gba, sig[s][:], ALU.mult).then_inc(sg_done, 1)
                    dve.drain()
                    nc.vector.scalar_tensor_tensor(v[s][:], gba, 1.0, sg[s][:], ALU.add, ALU.subtract).then_inc(v_done, 1)
                    nc.vector.tensor_tensor(dhbm[b % 3][:], dhid, sg[s][:], ALU.mult).then_inc(back_dve, 1)
                    nc.vector.tensor_tensor(dgate[s][:], dhid, hb[s][:], ALU.mult).then_inc(dgate_done, 1)
                dve.wait_ge(dw_psum, c + 1)
                nc.vector.tensor_copy(xr[:, 0:2].rearrange("p g b n -> p (g b n)"), banks[:, 3])
                nc.vector.tensor_copy(xr[:, 2].rearrange("p b n -> p (b n)"), banks[:, 4, 0:256])
                dve.drain()
                nc.vector.tensor_tensor(sq[:], xr[:].rearrange("p g b n -> p (g b n)"), xr[:].rearrange("p g b n -> p (g b n)"), ALU.mult)
                dve.drain()
                nc.vector.reduce_sum(rs[:], sq[:].rearrange("p (a n) -> p a n", n=HID), AX.X).then_inc(rs_done, 1)
                dve.wait_ge(fro_psum, c + 1)
                nc.vector.tensor_copy(fro[:], banks[:, 0, 0:12]).then_inc(fro_done, 1)
                query_product(c, 0)
                dve.wait_ge(root_done, c + 1)
                nc.vector.tensor_scalar(froot[:], froot[:], 1e-7, None, ALU.add)
                dve.drain()
                nc.vector.reciprocal(rn[:], froot[:])
                dve.drain()
                nc.vector.tensor_tensor(X[:].rearrange("p g b n -> p (g b) n"), xr[:].rearrange("p g b n -> p (g b) n"), rn[:].unsqueeze(2).broadcast_to([P, 12, HID]),
                                        ALU.mult).then_inc(start_done, 1)
                add_output(c, 0)
                for it in range(IT):
                    step = (c * IT + it) * 3
                    for g in range(3):
                        keep_own(step, g)
                    dve.drain()
                    for g in range(3):
                        add_scaled(it, g)
                        dve.drain()
                        polynomial(it, step, g)
                        if g == 0 and it in QUERY_AT:
                            query_product(c, QUERY_AT[it])
                    if it in QUERY_AT:
                        add_output(c, QUERY_AT[it])
                for g in range(3):
                    dve.wait_ge(xy_psum, c * (IT * 3 + 3) + IT * 3 + g + 1)
                    nc.vector.tensor_tensor(state[:, g], state[:, g], banks[:, 3 + g, 256:512] if g < 2 else banks[:, 5, 0:256], ALU.add)
                wait(dve, norm_root, c + 1)
                dve.drain()
                sum_state_squares()
                query_product(c, BATCH - 1)
                dve.wait_ge(norm_root, c + 2)
                nc.vector.tensor_scalar(wn[:], wn[:], 1e-5, None, ALU.add)
                dve.drain()
                nc.vector.reciprocal(wf[:], wn[:])
                dve.drain()
                nc.vector.tensor_tensor(wf[:], wf[:], norm0[:], ALU.mult)
                dve.drain()
                nc.vector.tensor_tensor(state[:, 0:2].rearrange("p g (a n) -> p (g a) n", n=DH), state[:, 0:2].rearrange("p g (a n) -> p (g a) n", n=DH),
                                        wf[:, 0:16].unsqueeze(2).broadcast_to([P, 16, DH]), ALU.mult)
                nc.vector.tensor_tensor(state[:, 2].rearrange("p (a n) -> p a n", n=HID), state[:, 2].rearrange("p (a n) -> p a n", n=HID),
                                        wf[:, 16:20].unsqueeze(2).broadcast_to([P, 4, HID]), ALU.mult).then_inc(state_done, 1)
                add_output(c, BATCH - 1)
            distribute(CHUNKS - 1)
            for b in range(BATCH):
                query_product(CHUNKS - 1, b)
                add_output(CHUNKS - 1, b)


def expert_weights(nc, ctx, gate_proj, up_proj, down_proj):
    sb = lambda n, dt=F32: ctx.enter_context(nc.sbuf_tensor(f"expert_{n}", [P, EXPERTS, 2 * P], dt))
    wg, wu, wd = sb("wg"), sb("wu"), sb("wd")
    return {
        "wg": wg, "wu": wu, "wd": wd[:].rearrange("p e (k d) -> p e k d", k=2),
        "loads": ((wg, gate_proj), (wu, up_proj), (wd, down_proj.rearrange("p e k d -> p e (k d)"))),
        "loaded": ctx.enter_context(nc.semaphore("expert_weights_loaded")),
    }


def expert_stage(nc, name, x_in, x_out, gate_w, weights, consts):
    groups, tiles = TOKENS // GROUP, GROUP // P
    units = 2 * EXPERTS
    ctx = ExitStack()
    with ctx:
        sb = lambda n, shape, dt=F32: ctx.enter_context(nc.sbuf_tensor(f"{name}_{n}", shape, dt))
        ps = lambda n, shape: ctx.enter_context(nc.psum_tensor(f"{name}_{n}", shape, F32))
        sem = lambda n: ctx.enter_context(nc.semaphore(f"{name}_{n}"))

        wg, wu, wd = weights["wg"], weights["wu"], weights["wd"]
        wg_hi, wg_lo, wu_hi, wu_lo = (sb(n, [P, EXPERTS, 2 * P], F32R) for n in ("wg_hi", "wg_lo", "wu_hi", "wu_lo"))
        wr = sb("wr", [P, EXPERTS])
        ident = sb("ident", [P, P])
        tri_f = sb("tri_f", [P, P])
        tri = sb("tri", [P, P], BF16)
        ones = sb("ones", [P, P], BF16)
        rev = sb("rev", [P, tiles, EXPERTS])
        negh = sb("negh", [P, tiles])
        acc = [sb(f"acc{s}", [P, tiles, P]) for s in range(2)]
        x = [sb(f"x{s}", [P, tiles, P]) for s in range(2)]
        stats = sb("stats", [P, tiles, 6])
        mv = sb("mv", [P, tiles, 2])
        vareps = sb("vareps", [P, tiles])
        rstd = sb("rstd", [P, tiles])
        xn = sb("xn", [P, tiles, P])
        xT = sb("xT", [P, GROUP])
        xT_hi = [sb(f"xT_hi{s}", [P, GROUP], F32R) for s in range(2)]
        xT_lo = [sb(f"xT_lo{s}", [P, GROUP], F32R) for s in range(2)]
        gated = [sb(f"gated{k}", [P, GROUP]) for k in range(2)]
        hid = [[sb(f"hid{s}{k}", [P, GROUP]) for k in range(2)] for s in range(2)]
        lmax = sb("lmax", [P, tiles])
        lsub = sb("lsub", [P, tiles, EXPERTS])
        prob = sb("prob", [P, tiles, EXPERTS])
        probs2 = sb("probs2", [P, tiles, EXPERTS])
        psum_ = sb("psum_", [P, tiles])
        eq = sb("eq", [P, tiles, EXPERTS])
        pick = sb("pick", [P, tiles])
        top = sb("top", [P, 2, tiles])
        chosen = sb("chosen", [P, tiles + 1, 2, EXPERTS], BF16)
        wsum = sb("wsum", [P, tiles])
        rank = sb("rank", [P, tiles, 2, EXPERTS])
        carry = sb("carry", [P, 2, EXPERTS])
        comb2 = sb("comb2", [P, tiles, 2, EXPERTS])
        comb = [sb(f"comb{s}", [P, tiles, EXPERTS]) for s in range(2)]

        ps_g = [ps(f"ps_g{s}", [P, GROUP]) for s in range(2)]
        ps_u = [ps(f"ps_u{s}", [P, GROUP]) for s in range(2)]
        ps_y = [ps(f"ps_y{s}", [P, tiles, P]) for s in range(2)]
        ps_t = ps("ps_t", [P, GROUP])
        ps_r = ps("ps_r", [P, 512])
        logits = ps_r[:, 0:tiles * EXPERTS].rearrange("p (j e) -> p j e", e=EXPERTS)
        counts_all = ps_r[:, 128:128 + (tiles + 1) * 2 * EXPERTS].rearrange("p (j k e) -> p j k e", k=2, e=EXPERTS)
        counts, total = counts_all[:, 0:tiles], counts_all[:, tiles]

        weights_in, x_loaded, x_stored = sem("weights_in"), [sem("x_loaded0"), sem("x_loaded1")], sem("x_stored")
        stats_done, rstd_done, xn_done = sem("stats_done"), sem("rstd_done"), sem("xn_done")
        xt_psum, xt_done, xt_split, weights_hi, weights_lo = sem("xt_psum"), sem("xt_done"), sem("xt_split"), sem("weights_hi"), sem("weights_lo")
        logits_done, lsub_done, exp_done, chosen_done, ranks_done = sem("logits_done"), sem("lsub_done"), sem("exp_done"), sem("chosen_done"), sem("ranks_done")
        gu_done, silu_done, hid_done, y_done, y_free = sem("gu_done"), sem("silu_done"), sem("hid_done"), sem("y_done"), sem("y_free")
        setup, waits_passed = sem("setup"), sem("waits_passed")

        SETUP = 4
        block = ctx.enter_context(nc.Block())

        def both(engine, body):
            with engine.Fori(0, groups // 2 - 1) as i:
                body(i * 2, 0, True)
                body(i * 2 + 1, 1, True)
            body(groups - 2, 0, True)
            body(groups - 1, 1, False)

        def wait(engine, semaphore, value):
            engine.wait_ge(semaphore, value)
            engine.sem_inc(waits_passed, 1)

        @block.sync
        def _(sp):
            sp.sem_inc(x_stored, 1 + 16)
            sp.dma_start(x[0][:], x_in[0:1].rearrange("a (j p) d -> p (a j) d", p=P)).then_inc(x_loaded[0], 16)
            for dst, src in ((wr, gate_w), (ident, consts["ident"]), (tri_f, consts["tri"]), (rev, consts["rev"])):
                sp.dma_start(dst[:], src).then_inc(weights_in, 16)

            def load(g, s):
                sp.dma_start(x[s][:], x_in[bass.ds(g, 1)].rearrange("a (j p) d -> p (a j) d", p=P)).then_inc(x_loaded[s], 16)

            def group(g, s, more):
                if more:
                    wait(sp, y_free, g * EXPERTS + BUFFERS)
                    load(g + 1, 1 - s)
                wait(sp, y_free, (g + 1) * EXPERTS + BUFFERS)
                sp.dma_start(x_out[bass.ds(g, 1)].rearrange("a (j p) d -> p (a j) d", p=P), acc[s][:]).then_inc(x_stored, 16)

            both(sp, group)
            sp.wait_ge(x_stored, 1 + 16 + groups * 16)

        @block.gpsimd
        def _(pool):
            pool.memset(negh[:], -0.5).then_inc(setup, 1)
            pool.memset(ones[:], 1.0).then_inc(setup, 1)
            pool.memset(carry[:], 0.0).then_inc(setup, 1)
            pool.memset(chosen[:], 0.0).then_inc(setup, 1)
            pool.wait_ge(setup, SETUP)

            def rsqrt(g):
                wait(pool, stats_done, g + 1)
                nc.gpsimd.tensor_scalar(vareps[:], mv[:, :, 1], LN_EPS, None, ALU.add)
                pool.drain()
                nc.gpsimd.tensor_tensor(rstd[:], vareps[:], negh[:], ALU.pow).then_inc(rstd_done, 1)

            rsqrt(0)
            for e in range(EXPERTS):
                pool.wait_ge(weights_hi, 1 + 2 * (e + 1))
                nc.gpsimd.tensor_tensor(wg_lo[:, e], wg[:, e], wg_hi[:, e].bitcast(F32), ALU.subtract)
                nc.gpsimd.tensor_tensor(wu_lo[:, e], wu[:, e], wu_hi[:, e].bitcast(F32), ALU.subtract).then_inc(weights_lo, 1)

            def group(g, s, more):
                if more:
                    rsqrt(g + 1)

            both(pool, group)

        @block.scalar
        def _(act):
            def copy_xt(g, s):
                act.wait_ge(xt_psum, g + 1)
                nc.scalar.activation(xT_hi[s][:], ps_t[:], ACT.Copy)
                nc.scalar.activation(xT[:], ps_t[:], ACT.Copy).then_inc(xt_done, 1)

            def exp_logits(g):
                act.wait_ge(lsub_done, g + 1)
                nc.scalar.activation(prob[:], lsub[:], ACT.Exp).then_inc(exp_done, 1)

            def group(g, s, more):
                for u in range(units):
                    act.wait_ge(gu_done, g * units + (u + 1))
                    nc.scalar.activation(gated[u % 2][:], ps_g[u % 2][:], ACT.Silu).then_inc(silu_done, 1)
                    if more and u == 7:
                        copy_xt(g + 1, 1 - s)
                    if more and u == 10:
                        exp_logits(g + 1)

            act.wait_ge(weights_in, 4 * 16)
            nc.scalar.activation(tri[:], tri_f[:], ACT.Copy).then_inc(weights_hi, 1)
            act.wait_ge(weights["loaded"], 3 * 16)
            for e in range(EXPERTS):
                nc.scalar.activation(wg_hi[:, e], wg[:, e], ACT.Copy).then_inc(weights_hi, 1)
                nc.scalar.activation(wu_hi[:, e], wu[:, e], ACT.Copy).then_inc(weights_hi, 1)
            copy_xt(0, 0)
            exp_logits(0)
            both(act, group)

        @block.tensor
        def _(pe):
            def transposes(g):
                pe.wait_ge(xn_done, g + 1)
                for j in range(tiles):
                    last = nc.tensor.transpose(ps_t[:, j * P:(j + 1) * P], xn[:, j, :], ident[:])
                last.then_inc(xt_psum, 1)

            def router(g):
                pe.wait_ge(xt_done, g + 1)
                for j in range(tiles):
                    last = nc.tensor.matmul(logits[:, j, :], xT[:, j * P:(j + 1) * P], wr[:], start=True, stop=True)
                last.then_inc(logits_done, 1)

            def ranks(g):
                pe.wait_ge(chosen_done, g + 1)
                nc.tensor.matmul(counts_all, tri[:], chosen[:], start=True, stop=False)
                for i in range(tiles):
                    last = nc.tensor.matmul(counts_all[:, i + 1:tiles + 1], ones[:],
                                            chosen[:, i].unsqueeze(1).broadcast_to([P, tiles - i, 2, EXPERTS]), start=False, stop=(i == tiles - 1))
                last.then_inc(ranks_done, 1)

            def gate_up(g, s, u):
                e, k = u // 2, u % 2
                pe.wait_ge(hid_done, g * units + (u + 1))
                half = slice(k * P, (k + 1) * P)
                if k == 0:
                    pe.wait_ge(weights_lo, e + 1)
                for out, w_hi, w_lo in ((ps_g[k], wg_hi, wg_lo), (ps_u[k], wu_hi, wu_lo)):
                    nc.tensor.matmul(out[:], w_hi[:, e, half], xT_hi[s][:], start=True, stop=False)
                    nc.tensor.matmul(out[:], w_hi[:, e, half], xT_lo[s][:], start=False, stop=False)
                    last = nc.tensor.matmul(out[:], w_lo[:, e, half], xT_hi[s][:], start=False, stop=True)
                last.then_inc(gu_done, 1)

            def down(g, e):
                pe.wait_ge(hid_done, g * units + 2 * (e + 1) + BUFFERS)
                pe.wait_ge(y_free, g * EXPERTS + (e + 1))
                for j in range(tiles):
                    for k in range(2):
                        last = nc.tensor.matmul(ps_y[e % 2][:, j], hid[e % 2][k][:, j * P:(j + 1) * P], wd[:, e, k],
                                                start=(k == 0), stop=(k == 1))
                last.then_inc(y_done, 1)

            def group(g, s, more):
                for e in range(EXPERTS):
                    if e + 1 < EXPERTS:
                        gate_up(g, s, 2 * e + 2)
                        if e == 0:
                            ranks(g)
                        gate_up(g, s, 2 * e + 3)
                    elif more:
                        first_expert(g + 1, 1 - s)
                    if more and e == 2:
                        transposes(g + 1)
                    if more and e == 3:
                        router(g + 1)
                    down(g, e)

            def first_expert(g, s):
                pe.wait_ge(xt_split, g + 1)
                gate_up(g, s, 0)
                gate_up(g, s, 1)

            pe.wait_ge(weights_in, 4 * 16)
            pe.wait_ge(setup, SETUP)
            transposes(0)
            router(0)
            pe.wait_ge(weights_hi, 1)
            first_expert(0, 0)
            both(pe, group)

        @block.vector
        def _(dve):
            def statistics(g, s):
                dve.wait_ge(x_loaded[s], (g - s) * 8 + 16)
                for j in range(tiles):
                    nc.vector.bn_stats(stats[:, j], x[s][:, j])
                dve.drain()
                for j in range(tiles):
                    last = nc.vector.bn_aggr(mv[:, j], stats[:, j])
                last.then_inc(stats_done, 1)

            def normalize(g, s):
                dve.wait_ge(rstd_done, g + 1)
                for j in range(tiles):
                    last = nc.vector.tensor_scalar(xn[:, j], x[s][:, j], mv[:, j, 0:1], rstd[:, j:j + 1], ALU.subtract, ALU.mult)
                last.then_inc(xn_done, 1)

            def split(g, s):
                dve.wait_ge(xt_done, g + 1)
                nc.vector.tensor_tensor(xT_lo[s][:], ps_t[:], xT_hi[s][:].bitcast(F32), ALU.subtract).then_inc(xt_split, 1)

            def row(t):
                return t.unsqueeze(2).broadcast_to([P, tiles, EXPERTS])

            def shift_logits(g):
                dve.wait_ge(logits_done, g + 1)
                nc.vector.reduce_max(lmax[:], logits, AX.X)
                dve.drain()
                nc.vector.tensor_tensor(lsub[:], logits, row(lmax[:]), ALU.subtract).then_inc(lsub_done, 1)

            def probabilities(g):
                dve.wait_ge(exp_done, g + 1)
                nc.vector.reduce_sum(psum_[:], prob[:], AX.X)
                dve.drain()
                nc.vector.reciprocal(psum_[:], psum_[:])
                dve.drain()
                nc.vector.tensor_tensor(prob[:], prob[:], row(psum_[:]), ALU.mult)

            def exclude_first():
                dve.drain()
                nc.vector.scalar_tensor_tensor(probs2[:], chosen[:, 0:tiles, 0], -2.0, prob[:], ALU.mult, ALU.add)

            def find_largest(k):
                p = (prob, probs2)[k]
                dve.drain()
                nc.vector.reduce_max(top[:, k], p[:], AX.X)
                dve.drain()
                nc.vector.tensor_tensor(eq[:], p[:], row(top[:, k]), ALU.is_equal)

            def choose_expert(k):
                dve.drain()
                nc.vector.tensor_tensor(eq[:], eq[:], rev[:], ALU.mult)
                dve.drain()
                nc.vector.reduce_max(pick[:], eq[:], AX.X)
                dve.drain()
                return nc.vector.tensor_tensor(chosen[:, 0:tiles, k], eq[:], row(pick[:]), ALU.is_equal)

            def share():
                nc.vector.tensor_tensor(wsum[:], top[:, 0], top[:, 1], ALU.add)
                dve.drain()
                nc.vector.tensor_scalar(wsum[:], wsum[:], 1e-9, None, ALU.add)
                dve.drain()
                nc.vector.reciprocal(wsum[:], wsum[:])
                dve.drain()
                nc.vector.tensor_tensor(top[:], top[:], wsum[:].unsqueeze(1).broadcast_to([P, 2, tiles]), ALU.mult)

            def rank_tokens(g):
                dve.wait_ge(ranks_done, g + 1)
                nc.vector.tensor_tensor(rank[:], counts, carry[:].unsqueeze(1).broadcast_to([P, tiles, 2, EXPERTS]), ALU.add)

            def weigh(g, s):
                dve.drain()
                nc.vector.tensor_tensor(carry[:], carry[:], total, ALU.add)
                nc.vector.scalar_tensor_tensor(rank[:], rank[:], float(CAPACITY), chosen[:, 0:tiles], ALU.is_le, ALU.mult)
                dve.drain()
                for k in range(2):
                    nc.vector.tensor_tensor(comb2[:, :, k], rank[:, :, k], row(top[:, k]), ALU.mult)
                dve.drain()
                nc.vector.tensor_tensor(comb[s][:], comb2[:, :, 0], comb2[:, :, 1], ALU.add)

            def hidden(g, u):
                e, k = u // 2, u % 2
                dve.wait_ge(silu_done, g * units + u + 1)
                nc.vector.tensor_tensor(hid[e % 2][k][:], gated[k][:], ps_u[k][:], ALU.mult).then_inc(hid_done, 1)

            def combine(g, s, e):
                before = acc[s] if e else x[s]
                if e == 0:
                    wait(dve, x_stored, 1 + g * 16)
                dve.drain()
                dve.wait_ge(y_done, g * EXPERTS + (e + 1))
                for j in range(tiles):
                    last = nc.vector.scalar_tensor_tensor(acc[s][:, j], ps_y[e % 2][:, j], comb[s][:, j, e:e + 1], before[:, j],
                                                          ALU.mult, ALU.add)
                last.then_inc(y_free, 1)

            def route_next(g, s, u):
                if u == 3:
                    statistics(g + 1, 1 - s)
                if u == 5:
                    normalize(g + 1, 1 - s)
                if u == 8:
                    split(g + 1, 1 - s)
                if u == 9:
                    shift_logits(g + 1)
                if u == 11:
                    probabilities(g + 1)
                if u == 12:
                    find_largest(0)
                if u == 13:
                    choose_expert(0)
                if u == 14:
                    exclude_first()
                    find_largest(1)
                if u == 15:
                    choose_expert(1).then_inc(chosen_done, 1)
                if u == 16:
                    share()

            def group(g, s, more):
                for e in range(EXPERTS):
                    for u in (2 * e + 2, 2 * e + 3):
                        if u < units:
                            hidden(g, u)
                        elif more:
                            hidden(g + 1, u - units)
                        if u == 2:
                            rank_tokens(g)
                        if u == 3:
                            weigh(g, s)
                        if more:
                            route_next(g, s, u)
                    combine(g, s, e)

            nc.vector.engine_nop().then_inc(hid_done, BUFFERS)
            nc.vector.engine_nop().then_inc(y_free, BUFFERS)
            dve.wait_ge(weights_in, 4 * 16)
            dve.wait_ge(setup, SETUP)
            statistics(0, 0)
            normalize(0, 0)
            shift_logits(0)
            split(0, 0)
            probabilities(0)
            find_largest(0)
            choose_expert(0)
            exclude_first()
            find_largest(1)
            choose_expert(1).then_inc(chosen_done, 1)
            share()
            hidden(0, 0)
            hidden(0, 1)
            both(dve, group)


def causal_attention_stage(nc, x_in, x_out, w_qkv, b_qkv, w_o, b_o, consts):
    ctx = ExitStack()
    with ctx:
        sb = lambda n, shape, dt=F32: ctx.enter_context(nc.sbuf_tensor(f"att_{n}", shape, dt))
        ps = lambda n, shape: ctx.enter_context(nc.psum_tensor(f"att_{n}", shape, F32))
        sem = lambda n: ctx.enter_context(nc.semaphore(f"att_{n}"))

        wqkv = sb("wqkv", [P, 3 * D])
        wo = sb("wo", [P, D])
        bias = sb("bias", [P, 3 * D])
        bo = sb("bo", [P, D])
        ident = sb("ident", [P, P])
        identb = sb("identb", [P, P], BF16)
        mask_f = sb("mask_f", [P, 2, P])
        mask = sb("mask", [P, 2, P], BF16)
        cs = sb("cs", [P, TILES, 2, ROT])
        negh = sb("negh", [P, TILES])
        xb = sb("xb", [P, TILES, D])
        res = sb("res", [P, TILES, D])
        stats = sb("stats", [P, TILES, 6])
        mv = sb("mv", [P, TILES, 2])
        vareps = sb("vareps", [P, TILES])
        rstd = sb("rstd", [P, TILES])
        xn = sb("xn", [P, TILES, D])
        xT = sb("xT", [P, SEQ])
        qkv = sb("qkv", [P, TILES, 3 * D])
        JH = TILES * HEADS
        turned = [sb(f"turned{k}", [P, JH, ROT]) for k in range(2)]
        turned2 = [sb(f"turned2{k}", [P, JH, ROT]) for k in range(2)]
        parts = [sb(f"parts{k}", [P, JH, 3, ROT], BF16) for k in range(2)]
        q_rows, k_rows = (sb(n, [P, JH, 32], BF16) for n in ("q_rows", "k_rows"))
        qm_rows = [sb(f"qm_rows{s}", [P, TILES, QUAD, 32], BF16) for s in range(2)]
        v1 = sb("v1", [P, JH, 32])
        kT = [[sb(f"kT{s}{h}", [P, SEQ], BF16) for h in range(QUAD)] for s in range(HEADS // QUAD)]
        kT_all = sb("kT_all", [P, SEQ], BF16)
        q1T = [sb(f"q1T{s}", [P, SEQ], BF16) for s in range(2)]
        q2T = [sb(f"q2T{s}", [P, SEQ], BF16) for s in range(2)]
        mx = sb("mx", [P, 2, TILES, QUAD])
        nm = sb("nm", [P, TILES, QUAD])
        nm2 = sb("nm2", [P, TILES, QUAD])
        prob = [sb(f"prob{s}", [P, 2, 512]) for s in range(4)]
        oT = sb("oT", [P, 2, 512])
        rden = sb("rden", [P, 4, QUAD])
        y = sb("y", [P, TILES, D])
        yT = sb("yT", [P, SEQ])

        ps1 = [ps(f"ps1{s}", [P, 512]) for s in range(2)]
        ps2 = [ps(f"ps2{s}", [P, 2, 512]) for s in range(2)]
        pso = ps("pso", [P, 512])
        psm = ps("psm", [P, 512])
        psm_b = psm[:].bitcast(BF16)

        weights_in, setup, zeroed, casts, waits_passed = sem("weights_in"), sem("setup"), sem("zeroed"), sem("casts"), sem("waits_passed")
        x_loaded, res_loaded, res_biased, x_stored = sem("x_loaded"), sem("res_loaded"), sem("res_biased"), sem("x_stored")
        stats_done, rstd_done, xn_done, q_split, k_split = sem("stats_done"), sem("rstd_done"), sem("xn_done"), sem("q_split"), sem("k_split")
        q_stacked, k_stacked, q_copied, k_placed, v_placed = sem("q_stacked"), sem("k_stacked"), sem("q_copied"), sem("k_placed"), sem("v_placed")
        misc_full, misc_free = sem("misc_full"), sem("misc_free")
        s1_done, max_done, quad_max, max_stacked = sem("s1_done"), sem("max_done"), sem("quad_max"), sem("max_stacked")
        s2_done, exp_done, pv_done, o_copied, out_done = sem("s2_done"), sem("exp_done"), sem("pv_done"), sem("o_copied"), sem("out_done")

        QUADS = HEADS // QUAD
        MAX_STEPS = [(j, c) for j in range(TILES) for c in range(1 + (j >= 4))]
        EXP_STEPS = [(c, i) for c in range(2) for i in range(4 * c + 4)]
        STEPS = len(MAX_STEPS)
        assert len(EXP_STEPS) == STEPS

        LEAD = 4
        COMMON = {(1, "end"): "o1", (5, "end"): "k", (6, "end"): "q1", (7, "end"): "o0", (10, "end"): "q2"}
        PREP = {(4, "mid"): "x0", (5, "mid"): "x1", (7, "mid"): "qk0", (8, "mid"): "qk1", (9, "mid"): "qk2", (10, "mid"): "qk3"}
        VALUES = {(2, "mid"): "v0", (3, "mid"): "v1"}
        OUTPUT = {(2, "end"): "y0", (3, "mid"): "y1", (3, "end"): "out0", (4, "mid"): "out1"}
        IN_ORDER = lambda place: (place[0], place[1] == "end")

        class Slot:

            def __init__(self, b, t, start, first=False, prep=False, output=False, last=False):
                self.b, self.t, self.G, self.start, self.first, self.prep, self.output = b, t, b * QUADS + t, start, first, prep, output
                self.more1, self.more2 = not (last and t == QUADS - 1), not (last and t >= QUADS - 2)
                places = {**COMMON, **(PREP if prep else {}), **(VALUES if t == QUADS - 1 and not last else {}), **(OUTPUT if output else {})}
                absent = (["o1"] if first else []) + ([] if self.more2 else ["k", "q1"]) + ([] if self.more1 else ["q2"])
                self.uses = {place: places[place] for place in sorted(places, key=IN_ORDER) if places[place] not in absent}

            def count(self, use):
                return self.start + list(self.uses.values()).index(use)

            def maxima_of(self, n):
                if n < STEPS - LEAD:
                    return (self.G + 1, (self.t + 1) % QUADS, n + LEAD) if self.more1 else None
                return (self.G + 2, (self.t + 2) % QUADS, n + LEAD - STEPS) if self.more2 else None

        FIRST_USES = ["x0", "x1", "qk0", "qk1", "qk2", "qk3", "v0", "v1", "k", "q1", "k next", "q1 next", "q2"]
        first_count = FIRST_USES.index
        first_slot = Slot(0, 0, len(FIRST_USES), first=True)
        AHEAD = len(FIRST_USES) + len(first_slot.uses)

        def batch_slots(b, last=False, body=None):
            slots = []
            start = AHEAD + b * (BODY if body is None else body)
            for t in range(1, QUADS):
                slots.append(Slot(b, t, start, prep=(t == 1 and not last), last=last))
                start = start + len(slots[-1].uses)
            if not last:
                slots.append(Slot(b + 1, 0, start, output=True))
            return slots

        BODY = sum(len(slot.uses) for slot in batch_slots(0, body=0))
        TAIL_USES = ["o1", "y0", "y1", "out0", "out1"]
        last_slots = batch_slots(BATCH - 1, last=True)
        tail_count = lambda use: last_slots[-1].start + len(last_slots[-1].uses) + TAIL_USES.index(use)

        SETUP = 3
        block = ctx.enter_context(nc.Block())

        def wait(engine, semaphore, value):
            engine.wait_ge(semaphore, value)
            engine.sem_inc(waits_passed, 1)

        @block.sync
        def _(sp):
            for count in (misc_free, o_copied):
                sp.sem_inc(count, 1)
            batch = lambda x, b: x[bass.ds(b, 1)].rearrange("a (j p) d -> p (a j) d", p=P)
            sp.dma_start(xb[:], batch(x_in, 0)).then_inc(x_loaded, 16)
            for dst, src in ((wqkv[:], w_qkv), (wo[:], w_o), (bias[:], b_qkv.broadcast_to([P, 3 * D])), (bo[:], b_o.broadcast_to([P, D])),
                             (ident[:], consts["ident"]), (mask_f[:], consts["mask"]), (cs[:], consts["cs"])):
                sp.dma_start(dst, src).then_inc(weights_in, 16)
            sp.dma_start(res[:], batch(x_in, 0)).then_inc(res_loaded, 16)

            def place_keys(count, t):
                wait(sp, misc_free, 1 + count + 1)
                for h in range(QUAD):
                    rows = slice(32 * h, 32 * h + 32)
                    sp.dma_start(kT[t][h][rows, :], kT_all[rows, :]).then_inc(k_placed, 16)

            sp.wait_ge(zeroed, 1)
            place_keys(first_count("k"), 0)
            place_keys(first_count("k next"), 1)
            place_keys(first_slot.count("k"), 2)
            with sp.Fori(0, BATCH - 1) as b:
                wait(sp, xn_done, b + 1)
                sp.dma_start(xb[:], batch(x_in, b + 1)).then_inc(x_loaded, 16)
                for S in batch_slots(b):
                    if S.output:
                        wait(sp, out_done, 2 * b + 2)
                        sp.dma_start(batch(x_out, b), res[:]).then_inc(x_stored, 16)
                    place_keys(S.count("k"), (S.t + 2) % QUADS)
                wait(sp, x_stored, b * 16 + 16)
                sp.dma_start(res[:], batch(x_in, b + 1)).then_inc(res_loaded, 16)
            for S in last_slots:
                if S.more2:
                    place_keys(S.count("k"), (S.t + 2) % QUADS)
            sp.wait_ge(out_done, 2 * BATCH)
            sp.dma_start(batch(x_out, BATCH - 1), res[:]).then_inc(x_stored, 16)
            sp.wait_ge(x_stored, BATCH * 16)

        def rotate(engine, k):
            even = qkv[:, :, 128 * k:128 * k + 64].rearrange("p j (h r) -> p j h r", r=ROT)
            odd = qkv[:, :, 128 * k + 64:128 * k + 128].rearrange("p j (h r) -> p j h r", r=ROT)
            for t, half, factor in ((turned[k], even, cs[:, :, 0]), (turned2[k], odd, cs[:, :, 1])):
                engine.tensor_tensor(t[:].rearrange("p (j h) r -> p j h r", h=HEADS), half, factor.unsqueeze(2).broadcast_to([P, TILES, HEADS, ROT]), ALU.mult)

        def split(engine, k, n):
            rest = turned2[k] if n == 0 else parts[k][:, :, n - 1]
            engine.drain()
            engine.tensor_tensor(turned[k][:], turned[k][:], rest[:] if n == 0 else rest, ALU.subtract)
            engine.drain()
            return engine.tensor_copy(parts[k][:, :, n], turned[k][:])

        @block.gpsimd
        def _(pool):
            pool.memset(negh[:], -0.5).then_inc(setup, 1)
            pool.memset(v1[:], 0.0).then_inc(setup, 1)
            pool.drain()
            pool.memset(v1[:, :, HS:HS + 1], 1.0).then_inc(setup, 1)
            pool.wait_ge(setup, SETUP)

            def rsqrt(batch):
                wait(pool, stats_done, batch + 1)
                nc.gpsimd.tensor_scalar(vareps[:], mv[:, :, 1], LN_EPS, None, ALU.add)
                pool.drain()
                nc.gpsimd.tensor_tensor(rstd[:], vareps[:], negh[:], ALU.pow).then_inc(rstd_done, 1)

            def copy_queries(G, t):
                of_quad = q_rows[:].rearrange("p (j h) r -> p j h r", h=HEADS)[:, :, QUAD * t:QUAD * (t + 1), 0:24]
                nc.gpsimd.tensor_copy(qm_rows[t % 2][:, :, :, 0:24], of_quad).then_inc(q_copied, 1)

            def stack_maxima(G, t):
                wait(pool, quad_max, G + 1)
                source = nm
                for n in range(3):
                    place = qm_rows[t % 2][:, :, :, 24 + n]
                    nc.gpsimd.tensor_copy(place, source[:])
                    pool.drain()
                    if n < 2:
                        nc.gpsimd.tensor_tensor(nm2[:], source[:], place, ALU.subtract)
                        pool.drain()
                        source = nm2
                pool.engine_nop().then_inc(max_stacked, 1)

            def add_output_bias(batch):
                wait(pool, res_loaded, batch * 16 + 16)
                nc.gpsimd.tensor_tensor(res[:], res[:], bo[:].unsqueeze(1).broadcast_to([P, TILES, D]), ALU.add).then_inc(res_biased, 1)

            def slot(S):
                if S.prep:
                    rsqrt(S.b + 1)
                if S.more2:
                    if S.t == 2:
                        wait(pool, q_stacked, S.b + 2)
                    wait(pool, misc_full, S.start)
                    copy_queries(S.G + 2, (S.t + 2) % QUADS)
                if S.more1:
                    stack_maxima(S.G + 1, (S.t + 1) % QUADS)
                if S.prep:
                    wait(pool, misc_free, 1 + S.count("qk3") + 1)
                    rotate(nc.gpsimd, 1)
                    for n in range(3):
                        last = split(nc.gpsimd, 1, n)
                    last.then_inc(k_split, 1)
                if S.t == 1:
                    add_output_bias(S.b)

            rsqrt(0)
            pool.wait_ge(misc_free, 1 + first_count("qk3") + 1)
            rotate(nc.gpsimd, 1)
            for n in range(3):
                last = split(nc.gpsimd, 1, n)
            last.then_inc(k_split, 1)
            pool.wait_ge(q_stacked, 1)
            copy_queries(0, 0)
            copy_queries(1, 1)
            stack_maxima(0, 0)
            slot(first_slot)
            with pool.Fori(0, BATCH - 1) as b:
                for S in batch_slots(b):
                    slot(S)
            for S in last_slots:
                slot(S)

        @block.scalar
        def _(act):
            act.wait_ge(weights_in, 7 * 16)
            nc.scalar.activation(identb[:], ident[:], ACT.Copy).then_inc(casts, 1)
            nc.scalar.activation(mask[:], mask_f[:], ACT.Copy).then_inc(casts, 1)
            act.wait_ge(setup, SETUP)

            def from_misc(count, dst, source=psm):
                act.wait_ge(misc_full, count + 1)
                nc.scalar.activation(dst, source, ACT.Copy).then_inc(misc_free, 1)

            def keys_from_misc(count, G):
                if G is not None:
                    act.wait_ge(k_placed, G * (QUAD * 16))
                act.wait_ge(misc_full, count + 1)
                nc.scalar.activation(kT_all[:], psm_b, ACT.Copy).then_inc(misc_free, 1)

            def evacuate(use, count, t, G):
                if use == "k":
                    keys_from_misc(count, G + 2)
                if use == "q1":
                    from_misc(count, q1T[t % 2][:], psm_b)
                if use == "q2":
                    from_misc(count, q2T[(t + 1) % 2][:], psm_b)
                if use in ("x0", "x1", "y0", "y1"):
                    half = slice(512 * int(use[1]), 512 * int(use[1]) + 512)
                    from_misc(count, (xT if use[0] == "x" else yT)[:, half], psm[:])

            def stack_queries(n):
                first, last = ((0, 3), (3, 5), (5, 6))[n]
                return nc.scalar.activation(q_rows[:, :, ROT * first:ROT * last].rearrange("p a (n r) -> p a n r", r=ROT),
                                            parts[0][:, :, n].unsqueeze(2).broadcast_to([P, JH, last - first, ROT]), ACT.Copy)

            def stack_keys(n):
                first, last = ((0, 3), (3, 5), (5, 6))[n]
                return nc.scalar.activation(k_rows[:, :, ROT * first:ROT * last].rearrange("p a (n r) -> p a n r", r=ROT),
                                            parts[1][:, :, 0:last - first], ACT.Copy)

            def place_values(batch):
                nc.scalar.activation(v1[:].rearrange("p (j h) r -> p j h r", h=HEADS)[:, :, :, 0:HS],
                                     qkv[:, :, 2 * D:3 * D].rearrange("p j (h r) -> p j h r", r=HS), ACT.Copy).then_inc(v_placed, 1)

            def copy_output(G, c):
                act.wait_ge(pv_done, G * STEPS + (STEPS if c else 4))
                nc.scalar.activation(oT[:, c], pso[:], ACT.Copy).then_inc(o_copied, 1)

            def exponential(G, n, pair):
                c, i = EXP_STEPS[n]
                size = 512 - max(0, i - 4 * c) * P
                act.wait_ge(s2_done, G * (2 * STEPS) + (2 * n + pair) + 1)
                nc.scalar.activation(prob[(2 * n + pair) % 4][:, :, 0:size], ps2[pair][:, :, 0:size], ACT.Exp, scale=SCORE_SCALE).then_inc(exp_done, 1)

            def slot(S):
                for n in range(STEPS):
                    exponential(S.G, n, 0)
                    if (n - 1, "end") in S.uses:
                        evacuate(S.uses[n - 1, "end"], S.count(S.uses[n - 1, "end"]), S.t, S.G)
                    exponential(S.G, n, 1)
                    if n == 0 and not S.first:
                        copy_output(S.G - 1, 1)
                    if n == 0 and S.t == 0:
                        act.wait_ge(misc_free, 1 + S.start)
                        place_values(S.b)
                    if n == 4:
                        copy_output(S.G, 0)
                    if (n, "mid") in S.uses:
                        evacuate(S.uses[n, "mid"], S.count(S.uses[n, "mid"]), S.t, S.G)
                    if S.t == 2 and S.more2 and n == 2:
                        act.wait_ge(q_copied, S.G + 2)
                        act.wait_ge(q_split, S.b + 2)
                        stack_queries(0)
                        stack_queries(1)
                    if S.t == 2 and S.more2 and n == 3:
                        stack_queries(2).then_inc(q_stacked, 1)
                        act.wait_ge(k_split, S.b + 2)
                        stack_keys(0)
                    if S.t == 2 and S.more2 and n == 4:
                        stack_keys(1)
                        stack_keys(2).then_inc(k_stacked, 1)

            for use in ("x0", "x1"):
                evacuate(use, first_count(use), 0, 0)
            act.wait_ge(zeroed, 1)
            act.wait_ge(q_split, 1)
            stack_queries(0)
            stack_queries(1)
            stack_queries(2).then_inc(q_stacked, 1)
            act.wait_ge(k_split, 1)
            stack_keys(0)
            stack_keys(1)
            stack_keys(2).then_inc(k_stacked, 1)
            keys_from_misc(first_count("k"), None)
            from_misc(first_count("q1"), q1T[0][:], psm_b)
            keys_from_misc(first_count("k next"), 1)
            from_misc(first_count("q1 next"), q1T[1][:], psm_b)
            from_misc(first_count("q2"), q2T[0][:], psm_b)
            slot(first_slot)
            with act.Fori(0, BATCH - 1) as b:
                for S in batch_slots(b):
                    slot(S)
            for S in last_slots:
                slot(S)
            copy_output(QUADS * BATCH - 1, 1)
            for use in ("y0", "y1"):
                evacuate(use, tail_count(use), 0, 0)

        @block.tensor
        def _(pe):
            def to_misc(count, rows):
                pe.wait_ge(misc_free, 1 + count)
                for j in range(TILES):
                    last = nc.tensor.transpose(psm_b[:, j * P:(j + 1) * P], rows(j), identb[:])
                last.then_inc(misc_full, 1)

            def quad_rows(rows, t):
                return lambda j: rows[:].rearrange("p (j h) r -> p j (h r)", h=HEADS)[:, j, P * t:P * (t + 1)]

            def quad_rows_with_maxima(t):
                return lambda j: qm_rows[t % 2][:, j].rearrange("p h r -> p (h r)")

            def produce(use, count, t, G):
                if use == "k":
                    to_misc(count, quad_rows(k_rows, (t + 2) % QUADS))
                elif use == "q1":
                    to_misc(count, quad_rows(q_rows, (t + 2) % QUADS))
                elif use == "q2":
                    pe.wait_ge(max_stacked, G + 2)
                    to_misc(count, quad_rows_with_maxima(t + 1))
                elif use[0] == "o" and use[1:] in "01":
                    c = int(use[1])
                    pe.wait_ge(o_copied, 1 + (G * 2 + 1 if c == 0 else G * 2))
                    pe.wait_ge(misc_free, 1 + count)
                    for j in range(4):
                        last = nc.tensor.transpose(psm[:, j * P:(j + 1) * P], oT[:, c, j * P:(j + 1) * P], ident[:])
                    last.then_inc(misc_full, 1)
                else:
                    pe.wait_ge(misc_free, 1 + count)
                    n = int(use[-1])
                    for j in range(4):
                        out = psm[:, j * P:(j + 1) * P]
                        if use[0] in "xy":
                            last = nc.tensor.transpose(out, (xn if use[0] == "x" else y)[:, 4 * n + j], ident[:])
                        elif use[0] == "o":
                            last = nc.tensor.matmul(out, yT[:, (4 * n + j) * P:(4 * n + j + 1) * P], wo[:], start=True, stop=True)
                        elif use[0] == "v":
                            last = nc.tensor.matmul(out, xT[:, (4 * n + j) * P:(4 * n + j + 1) * P], wqkv[:, 2 * D:3 * D], start=True, stop=True)
                        elif j < 2:
                            last = nc.tensor.matmul(psm[:, j * 2 * D:(j + 1) * 2 * D], xT[:, (2 * n + j) * P:(2 * n + j + 1) * P], wqkv[:, 0:2 * D],
                                                    start=True, stop=True)
                    last.then_inc(misc_full, 1)

            def max_step(G, t, n, heads=range(QUAD)):
                j, c = MAX_STEPS[n]
                size = min(512, P * (j + 1) - 512 * c)
                for h in heads:
                    u = G * (STEPS * QUAD) + (n * QUAD + h)
                    out = ps1[(n * QUAD + h) % 2]
                    diagonal = P * (j + 1) == 512 * c + size
                    pe.wait_ge(max_done, u + 1)
                    last = nc.tensor.matmul(out[:, 0:size], q1T[t % 2][:, j * P:(j + 1) * P], kT[t][h][:, 512 * c:512 * c + size],
                                            start=True, stop=not diagonal)
                    if diagonal:
                        last = nc.tensor.matmul(out[:, size - P:size], identb[:], mask[:, 0], start=False, stop=True)
                    last.then_inc(s1_done, 1)

            def exp_step(G, t, n, pair):
                c, i = EXP_STEPS[n]
                first = max(512 * c, P * i)
                size = 512 * (c + 1) - first
                pe.wait_ge(exp_done, G * (2 * STEPS) + (2 * n + pair) + 1)
                for h in range(2):
                    last = nc.tensor.matmul(ps2[pair][:, h, 0:size], kT[t][2 * pair + h][:, i * P:(i + 1) * P], q2T[t % 2][:, first:first + size],
                                            start=True, stop=(i < 4 * c))
                    if i >= 4 * c:
                        last = nc.tensor.matmul(ps2[pair][:, h, 0:P], identb[:], mask[:, 1], start=False, stop=True)
                last.then_inc(s2_done, 1)

            def value_step(G, t, n):
                c, i = EXP_STEPS[n]
                first = max(0, P * i - 512 * c)
                pe.wait_ge(exp_done, G * (2 * STEPS) + 2 * (n + 1) + BUFFERS)
                if i == 0:
                    pe.wait_ge(o_copied, 1 + G * 2 + c)
                for h in range(QUAD):
                    last = nc.tensor.matmul(pso[32 * h:32 * h + 32, first:512], v1[:, i * HEADS + QUAD * t + h, :],
                                            prob[(2 * n + h // 2) % 4][:, h % 2, 0:512 - first], start=(i == 0), stop=(i == 4 * c + 3))
                last.then_inc(pv_done, 1)

            def serve(S, use):
                if use == "x0":
                    pe.wait_ge(xn_done, S.b + 2)
                if use == "k" and S.t == 2:
                    pe.wait_ge(k_stacked, S.b + 2)
                    pe.wait_ge(q_stacked, S.b + 2)
                produce(use, S.count(use), S.t, S.G)

            def slot(S):
                pe.wait_ge(misc_free, 1 + S.start)
                for n in range(STEPS):
                    quad = S.maxima_of(n)
                    if quad and n == STEPS - LEAD:
                        pe.wait_ge(misc_free, 1 + S.count("q1") + 1)
                        pe.wait_ge(k_placed, (S.G + 3) * (QUAD * 16))
                    if quad:
                        max_step(*quad, [0])
                    exp_step(S.G, S.t, n, 0)
                    if quad:
                        max_step(*quad, [1])
                    exp_step(S.G, S.t, n, 1)
                    if quad:
                        max_step(*quad, [2])
                    if (n, "mid") in S.uses:
                        serve(S, S.uses[n, "mid"])
                    if n >= 1:
                        if n == 1 and S.t == 0:
                            pe.wait_ge(v_placed, S.b + 1)
                        value_step(S.G, S.t, n - 1)
                    elif not S.first:
                        value_step(S.G - 1, (S.t - 1) % QUADS, STEPS - 1)
                    if quad:
                        max_step(*quad, [3])
                    if (n, "end") in S.uses:
                        serve(S, S.uses[n, "end"])

            pe.wait_ge(weights_in, 7 * 16)
            pe.wait_ge(casts, 2)
            pe.wait_ge(setup, SETUP)
            pe.wait_ge(xn_done, 1)
            for use in FIRST_USES[0:first_count("k")]:
                produce(use, first_count(use), 0, 0)
            pe.wait_ge(q_stacked, 1)
            pe.wait_ge(k_stacked, 1)
            to_misc(first_count("k"), quad_rows(k_rows, 0))
            to_misc(first_count("q1"), quad_rows(q_rows, 0))
            pe.wait_ge(misc_free, 1 + first_count("q1") + 1)
            pe.wait_ge(k_placed, QUAD * 16)
            for n in range(STEPS):
                max_step(0, 0, n)
                if n == 5:
                    to_misc(first_count("k next"), quad_rows(k_rows, 1))
                if n == 6:
                    to_misc(first_count("q1 next"), quad_rows(q_rows, 1))
            pe.wait_ge(misc_free, 1 + first_count("q1 next") + 1)
            pe.wait_ge(k_placed, 2 * QUAD * 16)
            for n in range(LEAD):
                max_step(1, 1, n)
            pe.wait_ge(max_stacked, 1)
            to_misc(first_count("q2"), quad_rows_with_maxima(0))
            slot(first_slot)
            with pe.Fori(0, BATCH - 1) as b:
                for S in batch_slots(b):
                    slot(S)
            for S in last_slots:
                slot(S)
            value_step(QUADS * BATCH - 1, QUADS - 1, STEPS - 1)
            for use in TAIL_USES:
                produce(use, tail_count(use), 0, QUADS * BATCH)

        @block.vector
        def _(dve):
            def maxima(G, t, n, heads=range(QUAD)):
                j, c = MAX_STEPS[n]
                size = min(512, P * (j + 1) - 512 * c)
                for h in heads:
                    dve.wait_ge(s1_done, G * (STEPS * QUAD) + (n * QUAD + h + 1))
                    nc.vector.reduce_max(mx[:, c, j, h:h + 1], ps1[(n * QUAD + h) % 2][:, 0:size], AX.X).then_inc(max_done, 1)

            def negate_maxima(G, first=False):
                dve.drain()
                nc.vector.tensor_tensor(mx[:, 0, 4:8], mx[:, 0, 4:8], mx[:, 1, 4:8], ALU.max)
                if not first:
                    wait(dve, max_stacked, G)
                dve.drain()
                nc.vector.tensor_scalar(nm[:], mx[:, 0], -1.0, None, ALU.mult).then_inc(quad_max, 1)
                dve.drain()

            def statistics(batch):
                dve.wait_ge(x_loaded, batch * 16 + 16)
                for j in range(TILES):
                    nc.vector.bn_stats(stats[:, j], xb[:, j])
                dve.drain()
                for j in range(TILES):
                    last = nc.vector.bn_aggr(mv[:, j], stats[:, j])
                last.then_inc(stats_done, 1)

            def normalize(batch):
                dve.wait_ge(rstd_done, batch + 1)
                for j in range(TILES):
                    last = nc.vector.tensor_scalar(xn[:, j], xb[:, j], mv[:, j, 0:1], rstd[:, j:j + 1], ALU.subtract, ALU.mult)
                last.then_inc(xn_done, 1)

            def consume(use, count, t, batch):
                n = int(use[-1]) if use[-1] in "0123" else 0
                if use in ("o0", "o1"):
                    heads = psm[:].rearrange("p (j h r) -> p j h r", h=QUAD, r=32)
                    quad = (t - n) % QUADS
                    dve.wait_ge(misc_full, count + 1)
                    nc.vector.reciprocal(rden[:], heads[:, :, :, HS])
                    dve.drain()
                    nc.vector.tensor_tensor(y[:, 4 * n:4 * n + 4, 32 * quad:32 * quad + 32].rearrange("p j (h r) -> p j h r", r=HS), heads[:, :, :, 0:HS],
                                            rden[:].unsqueeze(3).broadcast_to([P, 4, QUAD, HS]), ALU.mult).then_inc(misc_free, 1)
                elif use[0:2] == "qk":
                    dve.wait_ge(misc_full, count + 1)
                    nc.vector.tensor_tensor(qkv[:, 2 * n:2 * n + 2, 0:2 * D], psm[:].rearrange("p (j d) -> p j d", j=2),
                                            bias[:, 0:2 * D].unsqueeze(1).broadcast_to([P, 2, 2 * D]), ALU.add).then_inc(misc_free, 1)
                elif use[0] == "v":
                    dve.wait_ge(misc_full, count + 1)
                    nc.vector.tensor_tensor(qkv[:, 4 * n:4 * n + 4, 2 * D:3 * D], psm[:].rearrange("p (j d) -> p j d", j=4),
                                            bias[:, 2 * D:3 * D].unsqueeze(1).broadcast_to([P, 4, D]), ALU.add).then_inc(misc_free, 1)
                elif use[0:3] == "out":
                    if n == 0:
                        dve.wait_ge(res_biased, batch + 1)
                    dve.wait_ge(misc_full, count + 1)
                    nc.vector.tensor_tensor(res[:, 4 * n:4 * n + 4], res[:, 4 * n:4 * n + 4], psm[:].rearrange("p (j d) -> p j d", j=4), ALU.add).then_inc(misc_free, 1)
                    dve.drain()
                    nc.vector.engine_nop().then_inc(out_done, 1)

            def slot(S):
                for n in range(STEPS):
                    quad = S.maxima_of(n)
                    if quad:
                        maxima(*quad, [0])
                    if (n - 1, "end") in S.uses:
                        use = S.uses[n - 1, "end"]
                        consume(use, S.count(use), S.t, S.b - 1)
                    if quad:
                        maxima(*quad, [1, 2])
                    if (n, "mid") in S.uses:
                        consume(S.uses[n, "mid"], S.count(S.uses[n, "mid"]), S.t, S.b - 1)
                    if quad:
                        maxima(*quad, [3])
                    if n == STEPS - LEAD - 1 and S.more1:
                        negate_maxima(S.G + 1)
                    if S.prep and n == 1:
                        statistics(S.b + 1)
                    if S.prep and n == 3:
                        normalize(S.b + 1)
                    if S.prep and n == 10:
                        dve.drain()
                        rotate(nc.vector, 0)
                    if S.prep and n == 11:
                        split(nc.vector, 0, 0)
                    if S.t == 2 and S.more2 and n < 2:
                        last = split(nc.vector, 0, n + 1)
                        if n == 1:
                            last.then_inc(q_split, 1)

            nc.vector.engine_nop().then_inc(exp_done, BUFFERS)
            nc.vector.engine_nop().then_inc(max_done, BUFFERS)
            statistics(0)
            nc.vector.memset(k_rows[:], 0.0)
            normalize(0)
            for zeros in [q_rows] + qm_rows:
                nc.vector.memset(zeros[:], 0.0)
            dve.drain()
            nc.vector.memset(k_rows[:, :, 24:27], 1.0)
            dve.wait_ge(weights_in, 7 * 16)
            for n, use in enumerate(FIRST_USES[0:first_count("v0")]):
                consume(use, first_count(use), 0, 0)
                for h in range(QUAD):
                    if n >= 2:
                        nc.vector.memset(kT[n - 2][h][:], 0.0)
            dve.drain()
            nc.vector.engine_nop().then_inc(zeroed, 1)
            rotate(nc.vector, 0)
            for n in range(3):
                last = split(nc.vector, 0, n)
            last.then_inc(q_split, 1)
            for use in ("v0", "v1"):
                consume(use, first_count(use), 0, 0)
            for n in range(STEPS):
                maxima(0, 0, n)
            negate_maxima(0, first=True)
            for n in range(LEAD):
                maxima(1, 1, n)
            slot(first_slot)
            with dve.Fori(0, BATCH - 1) as b:
                for S in batch_slots(b):
                    slot(S)
            for S in last_slots:
                slot(S)
            for use in TAIL_USES:
                consume(use, tail_count(use), 0, BATCH - 1)


def block(nc, x, out, fast_qkv, fast_norm, fast_lr_bias, fast_start, att_qkv, att_bias, att_out, att_out_bias,
          router, gate_proj, up_proj, down_proj, ident, block_ones, tri, rev, mask, cs):
    consts = {"ident": ident, "block_ones": block_ones, "tri": tri, "rev": rev, "mask": mask, "cs": cs}
    scratch = lambda n, shape: nc.dram_tensor(n, shape, F32, kind="Internal").ap()
    tok = scratch("tok", [CHUNKS, P, 2 * BATCH, 3 * D])
    turned = scratch("turned", [CHUNKS, P, BATCH, 3, CHUNK])
    x1, x2, x3 = (scratch(f"x{n}", [BATCH, SEQ, D]) for n in (1, 2, 3))
    groups = lambda t: t.rearrange("b (g n) d -> (b g) n d", n=GROUP)
    with ExitStack() as ctx:
        weights = expert_weights(nc, ctx, gate_proj, up_proj, down_proj)
        fast_weight_inputs(nc, x, tok, turned, fast_qkv, fast_lr_bias, fast_norm, consts)
        fast_weight_stage(nc, x, x1, tok, turned, fast_start, consts, weights)
        expert_stage(nc, "moe1", groups(x1), groups(x2), router, weights, consts)
        causal_attention_stage(nc, x2, x3, att_qkv, att_bias, att_out, att_out_bias, consts)
        expert_stage(nc, "moe2", groups(x3), groups(out), router, weights, consts)


def layouts(i):
    import numpy as np

    a = {k: np.asarray(v) for k, v in i.items()}
    c = lambda t: np.ascontiguousarray(t, dtype=t.dtype)

    def rope_halves(t):
        t = t.reshape(HEADS, HS, -1)
        return np.concatenate([t[:, ::2].reshape(HEADS * ROT, -1), t[:, 1::2].reshape(HEADS * ROT, -1)])

    def as_y(t):
        t = t.transpose(1, 0, 2).reshape(1, FW_HID, 1, FW_HEADS * FW_D)
        return np.tile(t, (2, 1, BATCH // 2, 1)).reshape(P, -1)

    def as_x(t):
        return np.tile(t.reshape(P, 1, FW_HID), (1, BATCH, 1)).reshape(P, -1)

    return {
        "x": c(a["L0_attn_a_hidden_states"]),
        "fast_qkv": c(np.concatenate([a["L0_attn_a_qkv_w"], a["L0_attn_a_lr_proj_w"]]).T),
        "fast_norm": c(np.concatenate([a["L0_attn_a_q_norm_w"], a["L0_attn_a_k_norm_w"]])[None]),
        "fast_lr_bias": c(a["L0_attn_a_lr_proj_b"][None]),
        "fast_start": c(np.stack([as_y(a["L0_attn_a_w0"]), as_y(a["L0_attn_a_w2"]), as_x(a["L0_attn_a_w1"])], 1)),
        "att_qkv": c(np.concatenate([rope_halves(a["L0_attn_b_Wq"]), rope_halves(a["L0_attn_b_Wk"]), a["L0_attn_b_Wv"]]).T),
        "att_bias": c(np.concatenate([rope_halves(a["L0_attn_b_bq"])[:, 0], rope_halves(a["L0_attn_b_bk"])[:, 0], a["L0_attn_b_bv"]])[None]),
        "att_out": c(a["L0_attn_b_Wo"].T),
        "att_out_bias": c(a["L0_attn_b_bo"][None]),
        "router": c(a["L0_ffn_gate_w"].T),
        "gate_proj": c(a["L0_ffn_gate_proj_w"].transpose(2, 0, 1)),
        "up_proj": c(a["L0_ffn_up_proj_w"].transpose(2, 0, 1)),
        "down_proj": c(a["L0_ffn_down_proj_w"].reshape(EXPERTS, D, 2, P).transpose(3, 0, 2, 1)),
    }


def constants():
    import numpy as np

    f = np.float32
    row, col = np.arange(P)[:, None], np.arange(P)[None]
    block_ones = row // FW_D == col // FW_D
    time, pair = np.arange(1, SEQ + 1, dtype=f)[:, None], np.arange(ROT, dtype=f)
    angle = (time * (f(1.0 / 10000.0) ** (f(2.0) * pair / f(HS))).astype(f)).astype(f)
    cs = np.stack([np.cos(angle), np.sin(angle)], 1).astype(f).reshape(TILES, P, 2, ROT).transpose(1, 0, 2, 3)
    return {
        "ident": np.eye(P, dtype=f),
        "block_ones": block_ones.astype(f),
        "tri": (row <= col).astype(f),
        "rev": np.tile(np.arange(EXPERTS, 0, -1, dtype=f), (P, GROUP // P, 1)),
        "mask": (np.stack([col > row, row > col], 1) * f(MASKED)).astype(f),
        "cs": np.ascontiguousarray(cs),
    }


def kernel(**inputs):
    import concourse.bacc as bacc
    from concourse.bass_utils import run_bass_kernel_spmd as run

    nc = bacc.Bacc("TRN2", target_bir_lowering=False, num_devices=1)
    arrays = {**layouts(inputs), **constants()}
    aps = {n: nc.dram_tensor(f"in_{n}", t.shape, mybir.dt.from_np(t.dtype), kind="ExternalInput").ap() for n, t in arrays.items()}
    out = nc.dram_tensor("out", (BATCH, SEQ, D), F32, kind="ExternalOutput").ap()
    block(nc, out=out, **aps)
    r = run(nc, [{f"in_{n}": t for n, t in arrays.items()}], core_ids=[0])
    return r.results[0]["out"]
```
